# Optimizing a Trainium2 kernel written in Bass

```python
import numpy as np
import jax
import jax.numpy as jnp

def _softmax(x, axis=-1):
    return jax.nn.softmax(x, axis=axis)

def _gelu(x):
    return jax.nn.gelu(x, approximate=True)

def _silu(x):
    return jax.nn.silu(x)

def _sigmoid(x):
    return jax.nn.sigmoid(x)

def _layernorm(x, axis=-1, eps=1e-05):
    m = jnp.mean(x, axis=axis, keepdims=True)
    v = jnp.var(x, axis=axis, keepdims=True)
    return (x - m) / jnp.sqrt(v + eps)

def _scatter_add(tgt, idx, src, axis=0):
    return tgt.at[idx].add(src)

def _segment_sum(src, seg, n):
    return jax.ops.segment_sum(src, seg, n)
kernel_name = 'mk_decoder_preln_d4_seqx_r8_1f1dfe'

def setup_inputs(seed: int=0):
    np.random.seed(seed)
    _w = jnp.asarray

    def _rec_inputs():
        import jax
        import jax.numpy as jnp
        _rk = jax.random.key(seed)
        x = 7.22e-05 + 1 * jax.random.normal(jax.random.fold_in(_rk, 1), (4, 256, 128), jnp.float32)
        _lenS = 256 - jax.random.randint(jax.random.fold_in(_rk, 7), (4,), 0, max(1, 256 // 4) + 1, jnp.int32)
        _lenS2 = 256 - jax.random.randint(jax.random.fold_in(_rk, 8), (4,), 0, max(1, 256 // 4) + 1, jnp.int32)
        _ctx_1024P = jax.random.normal(jax.random.fold_in(_rk, 11), (4, 16, 128), jnp.float32)
        _ctx_1024c = jax.random.dirichlet(jax.random.fold_in(_rk, 511), 0.3 * jnp.ones((16,), jnp.float32), (4, 256))
        _ctx_1024t = jnp.einsum('bsk,bkd->bsd', _ctx_1024c, _ctx_1024P)
        _ctx_1024t = _ctx_1024t * jax.lax.rsqrt(jnp.mean(jnp.square(_ctx_1024t)) + 1e-12) * 0.953939
        ctx_1024 = 4.13588e-05 + 0.999923 * (_ctx_1024t + 0.3 * jax.random.normal(jax.random.fold_in(_rk, 611), (4, 256, 128), jnp.float32))
        _validS = jnp.arange(256)[None, :] < _lenS[:, None]
        _validS2 = jnp.arange(256)[None, :] < _lenS2[:, None]
        _causal = jnp.tril(jnp.ones((256, 256), dtype=bool))
        mask_BxS2_bf1 = jnp.ones((4, 256), dtype=bool)
        return (x, ctx_1024, mask_BxS2_bf1)
    x, ctx_1024, mask_BxS2_bf1 = _rec_inputs()

    def _L0_attn_setup():
        import jax, jax.numpy as jnp
        import numpy as np
        B, T, C = (4, 256, 128)
        N_HEADS = 16
        HEAD_DIM = C // N_HEADS

        def rotary_embedding(seq_len, dim, dtype=jnp.float32):
            pos = jnp.arange(seq_len, dtype=dtype)[:, None]
            i = jnp.arange(0, dim, 2, dtype=dtype)[None, :]
            theta = pos / jnp.power(10000.0, i / dim)
            return (jnp.cos(theta), jnp.sin(theta))

        def apply_rotary(x, cos, sin):
            d = x.shape[-1]
            x1, x2 = (x[..., :d // 2], x[..., d // 2:])
            rotated = jnp.concatenate([-x2, x1], axis=-1)
            cos = jnp.concatenate([cos, cos], axis=-1)[None, :, None, :]
            sin = jnp.concatenate([sin, sin], axis=-1)[None, :, None, :]
            return x * cos + rotated * sin
        key = jax.random.key(seed)
        k1, k2, k3 = jax.random.split(key, 3)
        x = jax.random.normal(k1, (B, T, C), dtype=jnp.float32)
        w_qkv = jax.random.normal(k2, (C, 3 * C), dtype=jnp.float32) / np.sqrt(C)
        w_out = jax.random.normal(k3, (C, C), dtype=jnp.float32) / np.sqrt(C)
        return {'x': x, 'w_qkv': w_qkv, 'w_out': w_out}
    _L0_attn_all = _L0_attn_setup()
    _L0_attn_in = {k: v for k, v in _L0_attn_all.items() if k in ('w_qkv', 'w_out')}
    del _L0_attn_all

    def _L0_xattn_setup():
        import jax, jax.numpy as jnp
        import numpy as np
        D = 128
        key = jax.random.key(seed)
        ks = jax.random.split(key, 11)
        B, Sq, Skv = (4, 256, 256)
        s = 0.02
        return {'query': jax.random.normal(ks[0], (B, Sq, D), jnp.float32), 'key': jax.random.normal(ks[1], (B, Skv, D), jnp.float32), 'value': jax.random.normal(ks[2], (B, Skv, D), jnp.float32), 'Wq': jax.random.normal(ks[3], (D, D), jnp.float32) * s, 'bq': jnp.zeros((D,), jnp.float32), 'Wk': jax.random.normal(ks[4], (D, D), jnp.float32) * s, 'bk': jnp.zeros((D,), jnp.float32), 'Wv': jax.random.normal(ks[5], (D, D), jnp.float32) * s, 'bv': jnp.zeros((D,), jnp.float32), 'Wo': jax.random.normal(ks[6], (D, D), jnp.float32) * s, 'bo': jnp.zeros((D,), jnp.float32)}
    _L0_xattn_all = _L0_xattn_setup()
    _L0_xattn_in = {k: v for k, v in _L0_xattn_all.items() if k in ('Wq', 'bq', 'Wk', 'bk', 'Wv', 'bv', 'Wo', 'bo')}
    del _L0_xattn_all

    def _L0_ffn_setup():
        import jax, jax.numpy as jnp
        import numpy as np
        DIM = 128
        DEPTH = 6
        HEADS = 16
        DIM_HEAD = 64
        WINDOW = 32
        INNER = HEADS * DIM_HEAD
        DIM_INNER = int(DIM * 4 * 2 / 3)
        QK_SCALE = 8.0

        def shift_tokens(t):
            a, s = jnp.split(t, 2, -1)
            s = jnp.pad(s, ((0, 0), (1, 0), (0, 0)))[:, :-1]
            return jnp.concatenate([a, s], -1)

        def l2norm(t):
            return t / jnp.maximum(jnp.linalg.norm(t, axis=-1, keepdims=True), 1e-12)

        def rotate_half(x):
            x1, x2 = jnp.split(x, 2, -1)
            return jnp.concatenate([-x2, x1], -1)

        def rotary_tables(n):
            half = jnp.arange(0, DIM_HEAD, 2, dtype=jnp.float32)
            inv_freq = 1.0 / 10000.0 ** (half / DIM_HEAD)
            t = jnp.arange(n, dtype=jnp.float32)
            freqs = t[:, None] * inv_freq[None, :]
            freqs = jnp.concatenate([freqs, freqs], -1)
            base_scale = (half + 0.4 * DIM_HEAD) / (1.4 * DIM_HEAD)
            power = (t - n // 2) / (WINDOW // 2)
            scale = base_scale[None, :] ** power[:, None]
            scale = jnp.concatenate([scale, scale], -1)
            return (freqs, scale)

        def local_attention(q, k, v):
            b, h, n, d = q.shape
            w = WINDOW
            nw = n // w
            bq = q.reshape(b, h, nw, w, d)
            bk = k.reshape(b, h, nw, w, d)
            bv = v.reshape(b, h, nw, w, d)

            def look(t):
                p = jnp.pad(t, ((0, 0), (0, 0), (1, 0), (0, 0), (0, 0)))
                return jnp.concatenate([p[:, :, :nw], p[:, :, 1:]], axis=3)
            bk2, bv2 = (look(bk), look(bv))
            seq = jnp.arange(n).reshape(nw, w)
            seq_p = jnp.pad(seq, ((1, 0), (0, 0)), constant_values=-1)
            jt = jnp.concatenate([seq_p[:nw], seq_p[1:]], axis=1)
            it = seq[:, :, None]
            jb = jt[:, None, :]
            mask = (it < jb) | (it > jb + w) | (jb == -1)
            sim = jnp.einsum('bhwie,bhwje->bhwij', bq, bk2) * QK_SCALE
            sim = jnp.where(mask, -jnp.finfo(sim.dtype).max, sim)
            attn = jax.nn.softmax(sim, -1)
            out = jnp.einsum('bhwij,bhwje->bhwie', attn, bv2)
            return out.reshape(b, h, n, d)

        def attn_layer(x, Wqkv, qs, ksc, Wo):
            b, n, _ = x.shape
            qkv = x @ Wqkv
            q, k, v = jnp.split(qkv, 3, -1)
            sh = lambda t: t.reshape(b, n, HEADS, DIM_HEAD).transpose(0, 2, 1, 3)
            q, k, v = (sh(q), sh(k), sh(v))
            q = l2norm(q) * qs
            k = l2norm(k) * ksc
            freqs, scale = rotary_tables(n)
            cos, sin = (jnp.cos(freqs), jnp.sin(freqs))
            q = q * cos * scale + rotate_half(q) * sin * scale
            inv = 1.0 / scale
            k = k * cos * inv + rotate_half(k) * sin * inv
            out = local_attention(q, k, v)
            out = out.transpose(0, 2, 1, 3).reshape(b, n, INNER)
            return out @ Wo

        def ffn_layer(x, g, bln, W1, b1, W2, b2):
            mu = x.mean(-1, keepdims=True)
            var = ((x - mu) ** 2).mean(-1, keepdims=True)
            xn = (x - mu) / jnp.sqrt(var + 1e-05) * g + bln
            hg = xn @ W1 + b1
            a, gate = jnp.split(hg, 2, -1)
            return a * jax.nn.gelu(gate, approximate=False) @ W2 + b2
        key = jax.random.key(seed)
        ks = jax.random.split(key, 8)
        B, N = (2, 256)
        init = lambda k, shape: jax.random.normal(k, shape, jnp.float32) * 0.02
        return {'x': jax.random.normal(ks[0], (B, N, DIM), jnp.float32), 'Wqkv': init(ks[1], (DEPTH, DIM, 3 * INNER)), 'q_scale': jnp.ones((DEPTH, DIM_HEAD), jnp.float32), 'k_scale': jnp.ones((DEPTH, DIM_HEAD), jnp.float32), 'Wo': init(ks[2], (DEPTH, INNER, DIM)), 'ln_g': jnp.ones((DEPTH, DIM), jnp.float32), 'ln_b': jnp.zeros((DEPTH, DIM), jnp.float32), 'W1': init(ks[3], (DEPTH, DIM, 2 * DIM_INNER)), 'b1': jnp.zeros((DEPTH, 2 * DIM_INNER), jnp.float32), 'W2': init(ks[4], (DEPTH, DIM_INNER, DIM)), 'b2': jnp.zeros((DEPTH, DIM), jnp.float32)}
    _L0_ffn_all = _L0_ffn_setup()
    _L0_ffn_in = {k: v for k, v in _L0_ffn_all.items() if k in ('Wqkv', 'q_scale', 'k_scale', 'Wo', 'ln_g', 'ln_b', 'W1', 'b1', 'W2', 'b2')}
    del _L0_ffn_all

    def _L1_attn_setup():
        import jax, jax.numpy as jnp
        import numpy as np
        HEAD_DIM = 64
        N_HEADS = 16
        BASE = 10000.0
        MAX_T = 512

        def _rope_tables():
            inv = 1.0 / BASE ** (np.arange(0, HEAD_DIM, 2, dtype=np.float32) / HEAD_DIM)
            t = np.arange(MAX_T, dtype=np.float32)
            ang = np.outer(t, inv)
            return (jnp.asarray(np.cos(ang)), jnp.asarray(np.sin(ang)))
        _COS, _SIN = _rope_tables()

        def apply_rope(x):
            head0, rest = (x[:, :, :1], x[:, :, 1:])
            B, H, N1, D = rest.shape
            xr = rest.reshape(B, H, N1, D // 2, 2)
            xe, xo = (xr[..., 0], xr[..., 1])
            c = _COS[:N1][None, None, :, :]
            s = _SIN[:N1][None, None, :, :]
            re = xe * c - xo * s
            im = xe * s + xo * c
            rot = jnp.stack([re, im], axis=-1).reshape(B, H, N1, D)
            return jnp.concatenate([head0, rot], axis=2)
        key = jax.random.key(seed)
        ks = jax.random.split(key, 5)
        B, N, DIM = (2, 256, 128)
        HD = N_HEADS * HEAD_DIM
        x = jax.random.normal(ks[0], (B, N, DIM), dtype=jnp.float32)
        wq = jax.random.normal(ks[1], (HD, DIM), dtype=jnp.float32) * 0.02
        wk = jax.random.normal(ks[2], (HD, DIM), dtype=jnp.float32) * 0.02
        wv = jax.random.normal(ks[3], (HD, DIM), dtype=jnp.float32) * 0.02
        wo = jax.random.normal(ks[4], (DIM, HD), dtype=jnp.float32) * 0.02
        return {'x': x, 'wq': wq, 'wk': wk, 'wv': wv, 'wo': wo}
    _L1_attn_all = _L1_attn_setup()
    _L1_attn_in = {k: v for k, v in _L1_attn_all.items() if k in ('wq', 'wk', 'wv', 'wo')}
    del _L1_attn_all

    def _L1_xattn_setup():
        import jax, jax.numpy as jnp
        import numpy as np
        B, N, M = (2, 256, 256)
        QUERY_DIM = 128
        CONTEXT_DIM = 128
        HEADS = 16
        DIM_HEAD = 64
        INNER = HEADS * DIM_HEAD
        SCALE = DIM_HEAD ** (-0.5)
        key = jax.random.key(seed)
        ks = jax.random.split(key, 7)
        x = jax.random.normal(ks[0], (B, N, QUERY_DIM), dtype=jnp.float32)
        context = jax.random.normal(ks[1], (B, M, CONTEXT_DIM), dtype=jnp.float32)
        mask = jnp.ones((B, M), dtype=bool)
        s = 0.02
        Wq = jax.random.normal(ks[2], (QUERY_DIM, INNER), dtype=jnp.float32) * s
        Wk = jax.random.normal(ks[3], (CONTEXT_DIM, INNER), dtype=jnp.float32) * s
        Wv = jax.random.normal(ks[4], (CONTEXT_DIM, INNER), dtype=jnp.float32) * s
        Wo = jax.random.normal(ks[5], (INNER, QUERY_DIM), dtype=jnp.float32) * s
        bo = jnp.zeros((QUERY_DIM,), dtype=jnp.float32)
        return {'x': x, 'context': context, 'mask': mask, 'Wq': Wq, 'Wk': Wk, 'Wv': Wv, 'Wo': Wo, 'bo': bo}
    _L1_xattn_all = _L1_xattn_setup()
    _L1_xattn_in = {k: v for k, v in _L1_xattn_all.items() if k in ('Wq', 'Wk', 'Wv', 'Wo', 'bo')}
    del _L1_xattn_all

    def _L1_ffn_setup():
        import jax, jax.numpy as jnp
        import numpy as np
        D_MODEL = 128
        EXPANSION = 4
        D_HIDDEN = D_MODEL * EXPANSION
        NUM_STAGES = int(np.log2(D_HIDDEN))

        def butterfly(y, weights, dim):
            lead = y.shape[:-1]
            for stage in range(weights.shape[0]):
                s = 2 ** stage
                nb = dim // (2 * s)
                yr = y.reshape(*lead, nb, 2, s)
                a = yr[..., 0, :]
                b = yr[..., 1, :]
                w = weights[stage].reshape(nb, s, 2, 2)
                na = w[..., 0, 0] * a + w[..., 0, 1] * b
                nb2 = w[..., 1, 0] * a + w[..., 1, 1] * b
                y = jnp.stack([na, nb2], axis=-2).reshape(*lead, dim)
            return y
        key = jax.random.key(seed)
        ks = jax.random.split(key, 6)
        B, S = (4, 256)
        x = jax.random.normal(ks[0], (B, S, D_MODEL), jnp.float32)
        W_exp = jax.random.normal(ks[1], (D_MODEL, D_HIDDEN), jnp.float32) * 0.02
        b_exp = jnp.zeros((D_HIDDEN,), jnp.float32)
        up_weights = jax.random.normal(ks[2], (NUM_STAGES, D_HIDDEN // 2, 2, 2), jnp.float32) * 0.02
        up_bias = jnp.zeros((D_HIDDEN,), jnp.float32)
        down_weights = jax.random.normal(ks[3], (NUM_STAGES, D_HIDDEN // 2, 2, 2), jnp.float32) * 0.02
        W_con = jax.random.normal(ks[4], (D_HIDDEN, D_MODEL), jnp.float32) * 0.02
        b_con = jnp.zeros((D_MODEL,), jnp.float32)
        down_bias = jnp.zeros((D_MODEL,), jnp.float32)
        return dict(x=x, W_exp=W_exp, b_exp=b_exp, up_weights=up_weights, up_bias=up_bias, down_weights=down_weights, W_con=W_con, b_con=b_con, down_bias=down_bias)
    _L1_ffn_all = _L1_ffn_setup()
    _L1_ffn_in = {k: v for k, v in _L1_ffn_all.items() if k in ('W_exp', 'b_exp', 'up_weights', 'up_bias', 'down_weights', 'W_con', 'b_con', 'down_bias')}
    del _L1_ffn_all

    def _L2_attn_setup():
        import jax, jax.numpy as jnp
        import numpy as np
        H, D = (8, 128)
        HID = 128
        K = 4
        EPS_QK = 1e-06
        EPS_NORM = 1e-05

        def short_conv(x, w):
            k = w.shape[-1]
            xp = jnp.pad(x, ((0, 0), (k - 1, 0), (0, 0)))
            xc = jnp.transpose(xp, (0, 2, 1))
            y = jax.lax.conv_general_dilated(xc, w, window_strides=(1,), padding='VALID', feature_group_count=w.shape[0])
            return jax.nn.silu(jnp.transpose(y, (0, 2, 1)))

        def _rmsn(t, eps):
            return t * jax.lax.rsqrt(jnp.mean(t * t, axis=-1, keepdims=True) + eps)
        key = jax.random.key(seed)
        ks = jax.random.split(key, 16)
        s = 0.02
        inp = {'x': jax.random.normal(ks[0], (2, 128, HID), dtype=jnp.float32), 'Wq': jax.random.normal(ks[1], (H * D, HID), dtype=jnp.float32) * s, 'Wk': jax.random.normal(ks[2], (H * D, HID), dtype=jnp.float32) * s, 'Wv': jax.random.normal(ks[3], (H * D, HID), dtype=jnp.float32) * s, 'wq_conv': jax.random.normal(ks[4], (H * D, 1, K), dtype=jnp.float32) * 0.3, 'wk_conv': jax.random.normal(ks[5], (H * D, 1, K), dtype=jnp.float32) * 0.3, 'wv_conv': jax.random.normal(ks[6], (H * D, 1, K), dtype=jnp.float32) * 0.3, 'Wfa': jax.random.normal(ks[7], (D, HID), dtype=jnp.float32) * s, 'Wfb': jax.random.normal(ks[8], (H * D, D), dtype=jnp.float32) * s, 'Wb': jax.random.normal(ks[9], (H, HID), dtype=jnp.float32) * s, 'Wga': jax.random.normal(ks[10], (D, HID), dtype=jnp.float32) * s, 'Wgb': jax.random.normal(ks[11], (H * D, D), dtype=jnp.float32) * s, 'A_log': jnp.log(jax.random.uniform(ks[12], (H,), minval=1.0, maxval=16.0, dtype=jnp.float32)), 'dt_bias': jnp.zeros((H, D), dtype=jnp.float32), 'o_norm_w': jnp.ones((D,), dtype=jnp.float32), 'Wo': jax.random.normal(ks[13], (HID, H * D), dtype=jnp.float32) * s}
        return inp
    _L2_attn_all = _L2_attn_setup()
    _L2_attn_in = {k: v for k, v in _L2_attn_all.items() if k in ('Wq', 'Wk', 'Wv', 'wq_conv', 'wk_conv', 'wv_conv', 'Wfa', 'Wfb', 'Wb', 'Wga', 'Wgb', 'A_log', 'dt_bias', 'o_norm_w', 'Wo')}
    del _L2_attn_all

    def _L2_xattn_setup():
        import jax, jax.numpy as jnp
        import numpy as np
        BETA = 128
        NUM_HEADS = 16
        NORM = (BETA // NUM_HEADS) ** (-0.5)
        key = jax.random.key(seed)
        ks = jax.random.split(key, 6)
        B, N = (4, 256)
        D_in_q = D_in_k = D_in_v = 128
        D_out_k = D_out_v = 128
        q = jax.random.normal(ks[0], (B, N, D_in_q), dtype=jnp.float32)
        k = jax.random.normal(ks[1], (B, N, D_in_k), dtype=jnp.float32)
        v = jax.random.normal(ks[2], (B, N, D_in_v), dtype=jnp.float32)
        Wq = jax.random.normal(ks[3], (D_out_k, D_in_q), dtype=jnp.float32) * D_in_q ** (-0.5)
        Wk = jax.random.normal(ks[4], (D_out_k, D_in_k), dtype=jnp.float32) * D_in_k ** (-0.5)
        Wv = jax.random.normal(ks[5], (D_out_v, D_in_v), dtype=jnp.float32) * D_in_v ** (-0.5)
        return {'q': q, 'k': k, 'v': v, 'Wq': Wq, 'Wk': Wk, 'Wv': Wv}
    _L2_xattn_all = _L2_xattn_setup()
    _L2_xattn_in = {k: v for k, v in _L2_xattn_all.items() if k in ('Wq', 'Wk', 'Wv')}
    del _L2_xattn_all

    def _L2_ffn_setup():
        import jax, jax.numpy as jnp
        import numpy as np
        EPS = 1e-05

        def _ln_stats(x):
            mu = jnp.mean(x, axis=-1, keepdims=True)
            var = jnp.mean((x - mu) ** 2, axis=-1, keepdims=True)
            return (x - mu) * jax.lax.rsqrt(var + EPS)
        B, S, H, I, E = (2, 256, 128, 512, 8)
        key = jax.random.key(seed)
        ks = jax.random.split(key, 8)
        inp = {'hidden_states': jax.random.normal(ks[0], (B, S, H), dtype=jnp.float32), 'router_ln_w': jnp.ones((H,), jnp.float32), 'router_ln_b': jnp.zeros((H,), jnp.float32), 'router_w': jax.random.normal(ks[1], (H, E), dtype=jnp.float32) * 0.02, 'router_b': jnp.zeros((E,), jnp.float32), 'exp_ln_w': jnp.ones((E, H), jnp.float32), 'exp_ln_b': jnp.zeros((E, H), jnp.float32), 'w1': jax.random.normal(ks[2], (E, H, I), dtype=jnp.float32) * 0.02, 'b1': jnp.zeros((E, I), jnp.float32), 'w2': jax.random.normal(ks[3], (E, I, H), dtype=jnp.float32) * 0.02, 'b2': jnp.zeros((E, H), jnp.float32), 'out_ln_w': jnp.ones((H,), jnp.float32), 'out_ln_b': jnp.zeros((H,), jnp.float32)}
        return inp
    _L2_ffn_all = _L2_ffn_setup()
    _L2_ffn_in = {k: v for k, v in _L2_ffn_all.items() if k in ('router_ln_w', 'router_ln_b', 'router_w', 'router_b', 'exp_ln_w', 'exp_ln_b', 'w1', 'b1', 'w2', 'b2', 'out_ln_w', 'out_ln_b')}
    del _L2_ffn_all

    def _L3_attn_setup():
        import jax, jax.numpy as jnp
        import numpy as np
        from jax import lax
        DIM, D_STATE, D_CONV, NUM_HEADS, EXPAND = (128, 128, 4, 1, 2)
        D_INNER = EXPAND * DIM
        BATCH, SEQ = (4, 512)

        def _silu(v):
            return v * jax.nn.sigmoid(v)
        key = jax.random.key(seed)
        ks = jax.random.split(key, 7)
        s = 0.02
        return {'x': jax.random.normal(ks[0], (BATCH, SEQ, DIM), jnp.float32), 'in_proj_w': jax.random.normal(ks[1], (2 * D_INNER, DIM), jnp.float32) * s, 'conv_w': jax.random.normal(ks[2], (D_INNER, 1, D_CONV), jnp.float32) * s, 'conv_b': jnp.zeros((D_INNER,), jnp.float32), 'x_proj_w': jax.random.normal(ks[3], (2 * D_STATE + NUM_HEADS, D_INNER), jnp.float32) * s, 'dt_proj_w': jax.random.normal(ks[4], (D_INNER, NUM_HEADS), jnp.float32) * s, 'dt_proj_b': jnp.zeros((D_INNER,), jnp.float32), 'A_log': jnp.tile(jnp.log(jnp.arange(1, D_STATE + 1, dtype=jnp.float32)), (NUM_HEADS, 1)), 'norm_w': jnp.ones((D_INNER,), jnp.float32), 'out_proj_w': jax.random.normal(ks[5], (DIM, D_INNER), jnp.float32) * s}
    _L3_attn_all = _L3_attn_setup()
    _L3_attn_in = {k: v for k, v in _L3_attn_all.items() if k in ('in_proj_w', 'conv_w', 'conv_b', 'x_proj_w', 'dt_proj_w', 'dt_proj_b', 'A_log', 'norm_w', 'out_proj_w')}
    del _L3_attn_all

    def _L3_xattn_setup():
        import jax, jax.numpy as jnp
        import numpy as np
        B, S, E = (8, 256, 128)
        EPS = 0.001

        def _layer_norm(x, gamma, beta):
            mu = jnp.mean(x, axis=-1, keepdims=True)
            var = jnp.mean(jnp.square(x - mu), axis=-1, keepdims=True)
            return gamma * (x - mu) * jax.lax.rsqrt(var + EPS) + beta

        def _attention(q_in, k_in, v_in, WQ, WK, WV, causal):
            Q = jnp.einsum('bse,ed->bsd', q_in, WQ)
            K = jnp.einsum('bse,ed->bsd', k_in, WK)
            V = jnp.einsum('bse,ed->bsd', v_in, WV)
            d = K.shape[-1]
            scores = jnp.einsum('bqd,bkd->bqk', Q, K) / jnp.sqrt(jnp.float32(d))
            if causal:
                qlen, klen = (scores.shape[-2], scores.shape[-1])
                mask = jnp.triu(jnp.ones((qlen, klen), bool), k=1)
                scores = jnp.where(mask[None], -jnp.inf, scores)
            p = jax.nn.softmax(scores, axis=-1)
            return jnp.einsum('bqk,bkd->bqd', p, V)
        key = jax.random.key(seed)
        ks = jax.random.split(key, 10)
        sc = 1.0 / np.sqrt(E)
        return {'inputs': jax.random.normal(ks[0], (B, S, E), jnp.float32), 'context': jax.random.normal(ks[1], (B, S, E), jnp.float32), 'Wq': jax.random.normal(ks[2], (E, E), jnp.float32) * sc, 'Wk': jax.random.normal(ks[3], (E, E), jnp.float32) * sc, 'Wv': jax.random.normal(ks[4], (E, E), jnp.float32) * sc, 'Wcq': jax.random.normal(ks[5], (E, E), jnp.float32) * sc, 'Wck': jax.random.normal(ks[6], (E, E), jnp.float32) * sc, 'Wcv': jax.random.normal(ks[7], (E, E), jnp.float32) * sc, 'gamma': jnp.ones((E,), jnp.float32), 'beta': jnp.zeros((E,), jnp.float32), 'W1': jax.random.normal(ks[8], (E, E), jnp.float32) * sc, 'b1': jnp.zeros((E,), jnp.float32)}
    _L3_xattn_all = _L3_xattn_setup()
    _L3_xattn_in = {k: v for k, v in _L3_xattn_all.items() if k in ('Wq', 'Wk', 'Wv', 'Wcq', 'Wck', 'Wcv', 'gamma', 'beta', 'W1', 'b1')}
    del _L3_xattn_all

    def _L3_ffn_setup():
        import jax, jax.numpy as jnp
        import numpy as np
        E = 8
        K = 2
        CF = 1.25
        key = jax.random.key(seed)
        kx, kr, kg, ku, kd = jax.random.split(key, 5)
        D, F = (128, 512)
        x = jax.random.normal(kx, (4, 256, D), dtype=jnp.float32)
        router_w = 0.02 * jax.random.normal(kr, (E, D), dtype=jnp.float32)
        wg = jax.random.normal(kg, (E, D, F), dtype=jnp.float32) / np.sqrt(D)
        wu = jax.random.normal(ku, (E, D, F), dtype=jnp.float32) / np.sqrt(D)
        wd = jax.random.normal(kd, (E, F, D), dtype=jnp.float32) / np.sqrt(F)
        return {'x': x, 'router_w': router_w, 'wg': wg, 'wu': wu, 'wd': wd}
    _L3_ffn_all = _L3_ffn_setup()
    _L3_ffn_in = {k: v for k, v in _L3_ffn_all.items() if k in ('router_w', 'wg', 'wu', 'wd')}
    del _L3_ffn_all
    return {'x': x, 'ctx_1024': ctx_1024, 'mask_BxS2_bf1': mask_BxS2_bf1, 'L0_attn_w_qkv': _L0_attn_in['w_qkv'], 'L0_attn_w_out': _L0_attn_in['w_out'], 'L0_xattn_Wq': _L0_xattn_in['Wq'], 'L0_xattn_bq': _L0_xattn_in['bq'], 'L0_xattn_Wk': _L0_xattn_in['Wk'], 'L0_xattn_bk': _L0_xattn_in['bk'], 'L0_xattn_Wv': _L0_xattn_in['Wv'], 'L0_xattn_bv': _L0_xattn_in['bv'], 'L0_xattn_Wo': _L0_xattn_in['Wo'], 'L0_xattn_bo': _L0_xattn_in['bo'], 'L0_ffn_Wqkv': _L0_ffn_in['Wqkv'], 'L0_ffn_q_scale': _L0_ffn_in['q_scale'], 'L0_ffn_k_scale': _L0_ffn_in['k_scale'], 'L0_ffn_Wo': _L0_ffn_in['Wo'], 'L0_ffn_ln_g': _L0_ffn_in['ln_g'], 'L0_ffn_ln_b': _L0_ffn_in['ln_b'], 'L0_ffn_W1': _L0_ffn_in['W1'], 'L0_ffn_b1': _L0_ffn_in['b1'], 'L0_ffn_W2': _L0_ffn_in['W2'], 'L0_ffn_b2': _L0_ffn_in['b2'], 'L1_attn_wq': _L1_attn_in['wq'], 'L1_attn_wk': _L1_attn_in['wk'], 'L1_attn_wv': _L1_attn_in['wv'], 'L1_attn_wo': _L1_attn_in['wo'], 'L1_xattn_Wq': _L1_xattn_in['Wq'], 'L1_xattn_Wk': _L1_xattn_in['Wk'], 'L1_xattn_Wv': _L1_xattn_in['Wv'], 'L1_xattn_Wo': _L1_xattn_in['Wo'], 'L1_xattn_bo': _L1_xattn_in['bo'], 'L1_ffn_W_exp': _L1_ffn_in['W_exp'], 'L1_ffn_b_exp': _L1_ffn_in['b_exp'], 'L1_ffn_up_weights': _L1_ffn_in['up_weights'], 'L1_ffn_up_bias': _L1_ffn_in['up_bias'], 'L1_ffn_down_weights': _L1_ffn_in['down_weights'], 'L1_ffn_W_con': _L1_ffn_in['W_con'], 'L1_ffn_b_con': _L1_ffn_in['b_con'], 'L1_ffn_down_bias': _L1_ffn_in['down_bias'], 'L2_attn_Wq': _L2_attn_in['Wq'], 'L2_attn_Wk': _L2_attn_in['Wk'], 'L2_attn_Wv': _L2_attn_in['Wv'], 'L2_attn_wq_conv': _L2_attn_in['wq_conv'], 'L2_attn_wk_conv': _L2_attn_in['wk_conv'], 'L2_attn_wv_conv': _L2_attn_in['wv_conv'], 'L2_attn_Wfa': _L2_attn_in['Wfa'], 'L2_attn_Wfb': _L2_attn_in['Wfb'], 'L2_attn_Wb': _L2_attn_in['Wb'], 'L2_attn_Wga': _L2_attn_in['Wga'], 'L2_attn_Wgb': _L2_attn_in['Wgb'], 'L2_attn_A_log': _L2_attn_in['A_log'], 'L2_attn_dt_bias': _L2_attn_in['dt_bias'], 'L2_attn_o_norm_w': _L2_attn_in['o_norm_w'], 'L2_attn_Wo': _L2_attn_in['Wo'], 'L2_xattn_Wq': _L2_xattn_in['Wq'], 'L2_xattn_Wk': _L2_xattn_in['Wk'], 'L2_xattn_Wv': _L2_xattn_in['Wv'], 'L2_ffn_router_ln_w': _L2_ffn_in['router_ln_w'], 'L2_ffn_router_ln_b': _L2_ffn_in['router_ln_b'], 'L2_ffn_router_w': _L2_ffn_in['router_w'], 'L2_ffn_router_b': _L2_ffn_in['router_b'], 'L2_ffn_exp_ln_w': _L2_ffn_in['exp_ln_w'], 'L2_ffn_exp_ln_b': _L2_ffn_in['exp_ln_b'], 'L2_ffn_w1': _L2_ffn_in['w1'], 'L2_ffn_b1': _L2_ffn_in['b1'], 'L2_ffn_w2': _L2_ffn_in['w2'], 'L2_ffn_b2': _L2_ffn_in['b2'], 'L2_ffn_out_ln_w': _L2_ffn_in['out_ln_w'], 'L2_ffn_out_ln_b': _L2_ffn_in['out_ln_b'], 'L3_attn_in_proj_w': _L3_attn_in['in_proj_w'], 'L3_attn_conv_w': _L3_attn_in['conv_w'], 'L3_attn_conv_b': _L3_attn_in['conv_b'], 'L3_attn_x_proj_w': _L3_attn_in['x_proj_w'], 'L3_attn_dt_proj_w': _L3_attn_in['dt_proj_w'], 'L3_attn_dt_proj_b': _L3_attn_in['dt_proj_b'], 'L3_attn_A_log': _L3_attn_in['A_log'], 'L3_attn_norm_w': _L3_attn_in['norm_w'], 'L3_attn_out_proj_w': _L3_attn_in['out_proj_w'], 'L3_xattn_Wq': _L3_xattn_in['Wq'], 'L3_xattn_Wk': _L3_xattn_in['Wk'], 'L3_xattn_Wv': _L3_xattn_in['Wv'], 'L3_xattn_Wcq': _L3_xattn_in['Wcq'], 'L3_xattn_Wck': _L3_xattn_in['Wck'], 'L3_xattn_Wcv': _L3_xattn_in['Wcv'], 'L3_xattn_gamma': _L3_xattn_in['gamma'], 'L3_xattn_beta': _L3_xattn_in['beta'], 'L3_xattn_W1': _L3_xattn_in['W1'], 'L3_xattn_b1': _L3_xattn_in['b1'], 'L3_ffn_router_w': _L3_ffn_in['router_w'], 'L3_ffn_wg': _L3_ffn_in['wg'], 'L3_ffn_wu': _L3_ffn_in['wu'], 'L3_ffn_wd': _L3_ffn_in['wd']}

def reference(x, ctx_1024, mask_BxS2_bf1, L0_attn_w_qkv, L0_attn_w_out, L0_xattn_Wq, L0_xattn_bq, L0_xattn_Wk, L0_xattn_bk, L0_xattn_Wv, L0_xattn_bv, L0_xattn_Wo, L0_xattn_bo, L0_ffn_Wqkv, L0_ffn_q_scale, L0_ffn_k_scale, L0_ffn_Wo, L0_ffn_ln_g, L0_ffn_ln_b, L0_ffn_W1, L0_ffn_b1, L0_ffn_W2, L0_ffn_b2, L1_attn_wq, L1_attn_wk, L1_attn_wv, L1_attn_wo, L1_xattn_Wq, L1_xattn_Wk, L1_xattn_Wv, L1_xattn_Wo, L1_xattn_bo, L1_ffn_W_exp, L1_ffn_b_exp, L1_ffn_up_weights, L1_ffn_up_bias, L1_ffn_down_weights, L1_ffn_W_con, L1_ffn_b_con, L1_ffn_down_bias, L2_attn_Wq, L2_attn_Wk, L2_attn_Wv, L2_attn_wq_conv, L2_attn_wk_conv, L2_attn_wv_conv, L2_attn_Wfa, L2_attn_Wfb, L2_attn_Wb, L2_attn_Wga, L2_attn_Wgb, L2_attn_A_log, L2_attn_dt_bias, L2_attn_o_norm_w, L2_attn_Wo, L2_xattn_Wq, L2_xattn_Wk, L2_xattn_Wv, L2_ffn_router_ln_w, L2_ffn_router_ln_b, L2_ffn_router_w, L2_ffn_router_b, L2_ffn_exp_ln_w, L2_ffn_exp_ln_b, L2_ffn_w1, L2_ffn_b1, L2_ffn_w2, L2_ffn_b2, L2_ffn_out_ln_w, L2_ffn_out_ln_b, L3_attn_in_proj_w, L3_attn_conv_w, L3_attn_conv_b, L3_attn_x_proj_w, L3_attn_dt_proj_w, L3_attn_dt_proj_b, L3_attn_A_log, L3_attn_norm_w, L3_attn_out_proj_w, L3_xattn_Wq, L3_xattn_Wk, L3_xattn_Wv, L3_xattn_Wcq, L3_xattn_Wck, L3_xattn_Wcv, L3_xattn_gamma, L3_xattn_beta, L3_xattn_W1, L3_xattn_b1, L3_ffn_router_w, L3_ffn_wg, L3_ffn_wu, L3_ffn_wd):
    import jax
    import jax.numpy as jnp

    def _L0_attn_ref(x, w_qkv, w_out):
        import jax, jax.numpy as jnp
        import numpy as np
        B, T, C = (4, 256, 128)
        N_HEADS = 16
        HEAD_DIM = C // N_HEADS

        def rotary_embedding(seq_len, dim, dtype=jnp.float32):
            pos = jnp.arange(seq_len, dtype=dtype)[:, None]
            i = jnp.arange(0, dim, 2, dtype=dtype)[None, :]
            theta = pos / jnp.power(10000.0, i / dim)
            return (jnp.cos(theta), jnp.sin(theta))

        def apply_rotary(x, cos, sin):
            d = x.shape[-1]
            x1, x2 = (x[..., :d // 2], x[..., d // 2:])
            rotated = jnp.concatenate([-x2, x1], axis=-1)
            cos = jnp.concatenate([cos, cos], axis=-1)[None, :, None, :]
            sin = jnp.concatenate([sin, sin], axis=-1)[None, :, None, :]
            return x * cos + rotated * sin
        b, t, c = x.shape
        qkv = jnp.einsum('btc,cd->btd', x, w_qkv)
        q, k, v = jnp.split(qkv, 3, axis=-1)
        q = q.reshape(b, t, N_HEADS, HEAD_DIM)
        k = k.reshape(b, t, N_HEADS, HEAD_DIM)
        v = v.reshape(b, t, N_HEADS, HEAD_DIM)
        cos, sin = rotary_embedding(t, HEAD_DIM, dtype=x.dtype)
        q = apply_rotary(q, cos, sin)
        k = apply_rotary(k, cos, sin)
        scale = jnp.sqrt(jnp.asarray(HEAD_DIM, dtype=x.dtype))
        attn = jnp.einsum('bqhd,bkhd->bhqk', q, k) / scale
        mask = jnp.tril(jnp.ones((t, t), dtype=jnp.bool_))
        attn = jnp.where(mask[None, None, :, :], attn, jnp.asarray(-1000000000.0, dtype=x.dtype))
        attn = jax.nn.softmax(attn, axis=-1)
        out = jnp.einsum('bhqk,bkhd->bqhd', attn, v).reshape(b, t, c)
        return jnp.einsum('btc,cd->btd', out, w_out)

    def _L0_xattn_ref(query, key, value, Wq, bq, Wk, bk, Wv, bv, Wo, bo):
        import jax, jax.numpy as jnp
        import numpy as np
        D = 128
        Q = jnp.einsum('bsd,de->bse', query, Wq) + bq
        K = jnp.einsum('bsd,de->bse', key, Wk) + bk
        V = jnp.einsum('bsd,de->bse', value, Wv) + bv
        scale = 1.0 / jnp.sqrt(jnp.asarray(D, Q.dtype))
        scores = jnp.einsum('bqd,bkd->bqk', Q, K) * scale
        attn = jax.nn.softmax(scores, axis=-1)
        out = jnp.einsum('bqk,bkd->bqd', attn, V)
        return jnp.einsum('bsd,de->bse', out, Wo) + bo

    def _L0_ffn_ref(x, Wqkv, q_scale, k_scale, Wo, ln_g, ln_b, W1, b1, W2, b2):
        import jax, jax.numpy as jnp
        import numpy as np
        DIM = 128
        DEPTH = 6
        HEADS = 16
        DIM_HEAD = 64
        WINDOW = 32
        INNER = HEADS * DIM_HEAD
        DIM_INNER = int(DIM * 4 * 2 / 3)
        QK_SCALE = 8.0

        def shift_tokens(t):
            a, s = jnp.split(t, 2, -1)
            s = jnp.pad(s, ((0, 0), (1, 0), (0, 0)))[:, :-1]
            return jnp.concatenate([a, s], -1)

        def l2norm(t):
            return t / jnp.maximum(jnp.linalg.norm(t, axis=-1, keepdims=True), 1e-12)

        def rotate_half(x):
            x1, x2 = jnp.split(x, 2, -1)
            return jnp.concatenate([-x2, x1], -1)

        def rotary_tables(n):
            half = jnp.arange(0, DIM_HEAD, 2, dtype=jnp.float32)
            inv_freq = 1.0 / 10000.0 ** (half / DIM_HEAD)
            t = jnp.arange(n, dtype=jnp.float32)
            freqs = t[:, None] * inv_freq[None, :]
            freqs = jnp.concatenate([freqs, freqs], -1)
            base_scale = (half + 0.4 * DIM_HEAD) / (1.4 * DIM_HEAD)
            power = (t - n // 2) / (WINDOW // 2)
            scale = base_scale[None, :] ** power[:, None]
            scale = jnp.concatenate([scale, scale], -1)
            return (freqs, scale)

        def local_attention(q, k, v):
            b, h, n, d = q.shape
            w = WINDOW
            nw = n // w
            bq = q.reshape(b, h, nw, w, d)
            bk = k.reshape(b, h, nw, w, d)
            bv = v.reshape(b, h, nw, w, d)

            def look(t):
                p = jnp.pad(t, ((0, 0), (0, 0), (1, 0), (0, 0), (0, 0)))
                return jnp.concatenate([p[:, :, :nw], p[:, :, 1:]], axis=3)
            bk2, bv2 = (look(bk), look(bv))
            seq = jnp.arange(n).reshape(nw, w)
            seq_p = jnp.pad(seq, ((1, 0), (0, 0)), constant_values=-1)
            jt = jnp.concatenate([seq_p[:nw], seq_p[1:]], axis=1)
            it = seq[:, :, None]
            jb = jt[:, None, :]
            mask = (it < jb) | (it > jb + w) | (jb == -1)
            sim = jnp.einsum('bhwie,bhwje->bhwij', bq, bk2) * QK_SCALE
            sim = jnp.where(mask, -jnp.finfo(sim.dtype).max, sim)
            attn = jax.nn.softmax(sim, -1)
            out = jnp.einsum('bhwij,bhwje->bhwie', attn, bv2)
            return out.reshape(b, h, n, d)

        def attn_layer(x, Wqkv, qs, ksc, Wo):
            b, n, _ = x.shape
            qkv = x @ Wqkv
            q, k, v = jnp.split(qkv, 3, -1)
            sh = lambda t: t.reshape(b, n, HEADS, DIM_HEAD).transpose(0, 2, 1, 3)
            q, k, v = (sh(q), sh(k), sh(v))
            q = l2norm(q) * qs
            k = l2norm(k) * ksc
            freqs, scale = rotary_tables(n)
            cos, sin = (jnp.cos(freqs), jnp.sin(freqs))
            q = q * cos * scale + rotate_half(q) * sin * scale
            inv = 1.0 / scale
            k = k * cos * inv + rotate_half(k) * sin * inv
            out = local_attention(q, k, v)
            out = out.transpose(0, 2, 1, 3).reshape(b, n, INNER)
            return out @ Wo

        def ffn_layer(x, g, bln, W1, b1, W2, b2):
            mu = x.mean(-1, keepdims=True)
            var = ((x - mu) ** 2).mean(-1, keepdims=True)
            xn = (x - mu) / jnp.sqrt(var + 1e-05) * g + bln
            hg = xn @ W1 + b1
            a, gate = jnp.split(hg, 2, -1)
            return a * jax.nn.gelu(gate, approximate=False) @ W2 + b2
        for i in range(DEPTH):
            x = attn_layer(shift_tokens(x), Wqkv[i], q_scale[i], k_scale[i], Wo[i]) + x
            x = ffn_layer(shift_tokens(x), ln_g[i], ln_b[i], W1[i], b1[i], W2[i], b2[i]) + x
        return x

    def _L1_attn_ref(x, wq, wk, wv, wo):
        import jax, jax.numpy as jnp
        import numpy as np
        HEAD_DIM = 64
        N_HEADS = 16
        BASE = 10000.0
        MAX_T = 512

        def _rope_tables():
            inv = 1.0 / BASE ** (np.arange(0, HEAD_DIM, 2, dtype=np.float32) / HEAD_DIM)
            t = np.arange(MAX_T, dtype=np.float32)
            ang = np.outer(t, inv)
            return (jnp.asarray(np.cos(ang)), jnp.asarray(np.sin(ang)))
        _COS, _SIN = _rope_tables()

        def apply_rope(x):
            head0, rest = (x[:, :, :1], x[:, :, 1:])
            B, H, N1, D = rest.shape
            xr = rest.reshape(B, H, N1, D // 2, 2)
            xe, xo = (xr[..., 0], xr[..., 1])
            c = _COS[:N1][None, None, :, :]
            s = _SIN[:N1][None, None, :, :]
            re = xe * c - xo * s
            im = xe * s + xo * c
            rot = jnp.stack([re, im], axis=-1).reshape(B, H, N1, D)
            return jnp.concatenate([head0, rot], axis=2)
        B, N, DIM = x.shape
        scale = HEAD_DIM ** 0.5
        q = x @ wq.T
        k = x @ wk.T
        v = x @ wv.T
        q = q.reshape(B, N_HEADS, N, HEAD_DIM)
        k = k.reshape(B, N_HEADS, N, HEAD_DIM)
        v = v.reshape(B, N_HEADS, N, HEAD_DIM)
        q = apply_rope(q)
        k = apply_rope(k)
        scores = jnp.einsum('bhnd,bhmd->bhnm', q, k) / scale
        w = jax.nn.softmax(scores, axis=-1)
        out = jnp.einsum('bhnm,bhmd->bhnd', w, v)
        out = out.reshape(B, N, N_HEADS * HEAD_DIM)
        return out @ wo.T

    def _L1_xattn_ref(x, context, mask, Wq, Wk, Wv, Wo, bo):
        import jax, jax.numpy as jnp
        import numpy as np
        B, N, M = (2, 256, 256)
        QUERY_DIM = 128
        CONTEXT_DIM = 128
        HEADS = 16
        DIM_HEAD = 64
        INNER = HEADS * DIM_HEAD
        SCALE = DIM_HEAD ** (-0.5)
        b, n, _ = x.shape
        m = context.shape[1]
        q = (x @ Wq).reshape(b, n, HEADS, DIM_HEAD)
        k = (context @ Wk).reshape(b, m, HEADS, DIM_HEAD)
        v = (context @ Wv).reshape(b, m, HEADS, DIM_HEAD)
        dots = jnp.einsum('bnhd,bmhd->bhnm', q, k) * SCALE
        neg = -jnp.finfo(dots.dtype).max
        dots = jnp.where(mask[:, None, None, :], dots, neg)
        attn = jax.nn.softmax(dots, axis=-1)
        out = jnp.einsum('bhnm,bmhd->bnhd', attn, v).reshape(b, n, INNER)
        return out @ Wo + bo

    def _L1_ffn_ref(x, W_exp, b_exp, up_weights, up_bias, down_weights, W_con, b_con, down_bias):
        import jax, jax.numpy as jnp
        import numpy as np
        D_MODEL = 128
        EXPANSION = 4
        D_HIDDEN = D_MODEL * EXPANSION
        NUM_STAGES = int(np.log2(D_HIDDEN))

        def butterfly(y, weights, dim):
            lead = y.shape[:-1]
            for stage in range(weights.shape[0]):
                s = 2 ** stage
                nb = dim // (2 * s)
                yr = y.reshape(*lead, nb, 2, s)
                a = yr[..., 0, :]
                b = yr[..., 1, :]
                w = weights[stage].reshape(nb, s, 2, 2)
                na = w[..., 0, 0] * a + w[..., 0, 1] * b
                nb2 = w[..., 1, 0] * a + w[..., 1, 1] * b
                y = jnp.stack([na, nb2], axis=-2).reshape(*lead, dim)
            return y
        h = jnp.einsum('bsd,dh->bsh', x, W_exp) + b_exp
        h = butterfly(h, up_weights, D_HIDDEN)
        h = jax.nn.gelu(h + up_bias, approximate=False)
        h = butterfly(h, down_weights, D_HIDDEN)
        y = jnp.einsum('bsh,hd->bsd', h, W_con) + b_con
        return y + down_bias

    def _L2_attn_ref(x, Wq, Wk, Wv, wq_conv, wk_conv, wv_conv, Wfa, Wfb, Wb, Wga, Wgb, A_log, dt_bias, o_norm_w, Wo):
        import jax, jax.numpy as jnp
        import numpy as np
        H, D = (8, 128)
        HID = 128
        K = 4
        EPS_QK = 1e-06
        EPS_NORM = 1e-05

        def short_conv(x, w):
            k = w.shape[-1]
            xp = jnp.pad(x, ((0, 0), (k - 1, 0), (0, 0)))
            xc = jnp.transpose(xp, (0, 2, 1))
            y = jax.lax.conv_general_dilated(xc, w, window_strides=(1,), padding='VALID', feature_group_count=w.shape[0])
            return jax.nn.silu(jnp.transpose(y, (0, 2, 1)))

        def _rmsn(t, eps):
            return t * jax.lax.rsqrt(jnp.mean(t * t, axis=-1, keepdims=True) + eps)
        B, T, _ = x.shape
        scale = float(D) ** (-0.5)
        q = short_conv(x @ Wq.T, wq_conv).reshape(B, T, H, D)
        k = short_conv(x @ Wk.T, wk_conv).reshape(B, T, H, D)
        v = short_conv(x @ Wv.T, wv_conv).reshape(B, T, H, D)
        q = scale ** 2 * _rmsn(q, EPS_QK)
        k = scale * _rmsn(k, EPS_QK)
        a_logits = (x @ Wfa.T @ Wfb.T).reshape(B, T, H, D)
        g = -jnp.exp(A_log)[None, None, :, None] * jax.nn.softplus(a_logits + dt_bias)
        beta = jax.nn.sigmoid(x @ Wb.T)

        def step(S, inputs):
            q_t, k_t, v_t, g_t, b_t = inputs
            S = S * jnp.exp(g_t)[..., None]
            kv = jnp.einsum('bhd,bhdv->bhv', k_t, S)
            delta = b_t[..., None] * (v_t - kv)
            S = S + k_t[..., None] * delta[:, :, None, :]
            o = jnp.einsum('bhd,bhdv->bhv', q_t, S)
            return (S, o)
        tb = lambda t: jnp.moveaxis(t, 1, 0)
        S0 = jnp.zeros((B, H, D, D), dtype=x.dtype)
        _, o_t = jax.lax.scan(step, S0, (tb(q), tb(k), tb(v), tb(g), tb(beta)))
        out = jnp.moveaxis(o_t, 0, 1)
        gate = (x @ Wga.T @ Wgb.T).reshape(B, T, H, D)
        out = _rmsn(out, EPS_NORM) * o_norm_w * jax.nn.sigmoid(gate)
        return out.reshape(B, T, H * D) @ Wo.T

    def _L2_xattn_ref(q, k, v, Wq, Wk, Wv):
        import jax, jax.numpy as jnp
        import numpy as np
        BETA = 128
        NUM_HEADS = 16
        NORM = (BETA // NUM_HEADS) ** (-0.5)
        qp = jax.nn.relu(jnp.einsum('bnd,od->bno', q, Wq))
        kp = jax.nn.relu(jnp.einsum('bnd,od->bno', k, Wk))
        vp = jax.nn.relu(jnp.einsum('bnd,od->bno', v, Wv))
        B, N, D = qp.shape
        dh = D // NUM_HEADS
        qh = qp.reshape(B, N, NUM_HEADS, dh)
        kh = kp.reshape(B, N, NUM_HEADS, dh)
        vh = vp.reshape(B, N, NUM_HEADS, vp.shape[-1] // NUM_HEADS)
        E = NORM * jnp.einsum('bqhd,bkhd->bhqk', qh, kh)
        A = jax.nn.softmax(E, axis=-1)
        out = jnp.einsum('bhqk,bkhd->bqhd', A, vh)
        return out.reshape(B, N, -1)

    def _L2_ffn_ref(hidden_states, router_ln_w, router_ln_b, router_w, router_b, exp_ln_w, exp_ln_b, w1, b1, w2, b2, out_ln_w, out_ln_b):
        import jax, jax.numpy as jnp
        import numpy as np
        EPS = 1e-05

        def _ln_stats(x):
            mu = jnp.mean(x, axis=-1, keepdims=True)
            var = jnp.mean((x - mu) ** 2, axis=-1, keepdims=True)
            return (x - mu) * jax.lax.rsqrt(var + EPS)
        K = 2
        x = hidden_states
        xhat = _ln_stats(x)
        router_logits = (xhat * router_ln_w + router_ln_b) @ router_w + router_b
        routing_weights, selected = jax.lax.top_k(router_logits, K)
        routing_weights = jax.nn.softmax(routing_weights, axis=-1)
        xn = xhat[None] * exp_ln_w[:, None, None, :] + exp_ln_b[:, None, None, :]
        h = jnp.einsum('ebsh,ehi->ebsi', xn, w1) + b1[:, None, None, :]
        h = jax.nn.gelu(h, approximate=False)
        eo = jnp.einsum('ebsi,eih->ebsh', h, w2) + b2[:, None, None, :]
        eo = jnp.moveaxis(eo, 0, 2)
        gathered = jnp.take_along_axis(eo, selected[..., None], axis=2)
        combined = jnp.sum(routing_weights[..., None] * gathered, axis=2)
        return _ln_stats(combined) * out_ln_w + out_ln_b

    def _L3_attn_ref(x, in_proj_w, conv_w, conv_b, x_proj_w, dt_proj_w, dt_proj_b, A_log, norm_w, out_proj_w):
        import jax, jax.numpy as jnp
        import numpy as np
        from jax import lax
        DIM, D_STATE, D_CONV, NUM_HEADS, EXPAND = (128, 128, 4, 1, 2)
        D_INNER = EXPAND * DIM
        BATCH, SEQ = (4, 512)

        def _silu(v):
            return v * jax.nn.sigmoid(v)
        batch, seq, dim = x.shape
        d_inner = conv_w.shape[0]
        d_conv = conv_w.shape[2]
        num_heads, d_state = A_log.shape
        xz = jnp.einsum('btd,ed->bte', x, in_proj_w)
        x_inner, z = jnp.split(xz, 2, axis=-1)
        x_nch = jnp.transpose(x_inner, (0, 2, 1))
        x_conv = lax.conv_general_dilated(x_nch, conv_w, window_strides=(1,), padding=[(d_conv - 1, 0)], dimension_numbers=('NCH', 'OIH', 'NCH'), feature_group_count=d_inner)
        x_conv = jnp.transpose(x_conv, (0, 2, 1)) + conv_b
        x_conv = _silu(x_conv)
        x_dbl = jnp.einsum('btd,ed->bte', x_conv, x_proj_w)
        dt = x_dbl[..., :num_heads]
        Bm = x_dbl[..., num_heads:num_heads + d_state]
        Cm = x_dbl[..., num_heads + d_state:]
        dt = jax.nn.softplus(jnp.einsum('bth,dh->btd', dt, dt_proj_w) + dt_proj_b)
        A = -jnp.exp(A_log)
        A_mean = jnp.mean(A, axis=0)

        def step(h, inp):
            u_t, dt_t, B_t, C_t = inp
            dA = jnp.exp(dt_t[:, :, None] * A_mean)
            dB = dt_t[:, :, None] * B_t[:, None, :]
            h = dA * h + dB * u_t[:, :, None]
            y_t = jnp.einsum('bds,bs->bd', h, C_t)
            return (h, y_t)
        xs = (jnp.transpose(x_conv, (1, 0, 2)), jnp.transpose(dt, (1, 0, 2)), jnp.transpose(Bm, (1, 0, 2)), jnp.transpose(Cm, (1, 0, 2)))
        h0 = jnp.zeros((batch, d_inner, d_state), x.dtype)
        _, ys = lax.scan(step, h0, xs)
        y = jnp.transpose(ys, (1, 0, 2))
        eps = jnp.finfo(y.dtype).eps
        y = y * lax.rsqrt(jnp.mean(jnp.square(y), axis=-1, keepdims=True) + eps) * norm_w
        y = y * _silu(z)
        return jnp.einsum('btd,od->bto', y, out_proj_w)

    def _L3_xattn_ref(inputs, context, Wq, Wk, Wv, Wcq, Wck, Wcv, gamma, beta, W1, b1):
        import jax, jax.numpy as jnp
        import numpy as np
        B, S, E = (8, 256, 128)
        EPS = 0.001

        def _layer_norm(x, gamma, beta):
            mu = jnp.mean(x, axis=-1, keepdims=True)
            var = jnp.mean(jnp.square(x - mu), axis=-1, keepdims=True)
            return gamma * (x - mu) * jax.lax.rsqrt(var + EPS) + beta

        def _attention(q_in, k_in, v_in, WQ, WK, WV, causal):
            Q = jnp.einsum('bse,ed->bsd', q_in, WQ)
            K = jnp.einsum('bse,ed->bsd', k_in, WK)
            V = jnp.einsum('bse,ed->bsd', v_in, WV)
            d = K.shape[-1]
            scores = jnp.einsum('bqd,bkd->bqk', Q, K) / jnp.sqrt(jnp.float32(d))
            if causal:
                qlen, klen = (scores.shape[-2], scores.shape[-1])
                mask = jnp.triu(jnp.ones((qlen, klen), bool), k=1)
                scores = jnp.where(mask[None], -jnp.inf, scores)
            p = jax.nn.softmax(scores, axis=-1)
            return jnp.einsum('bqk,bkd->bqd', p, V)
        a = _attention(inputs, inputs, inputs, Wq, Wk, Wv, causal=True) + inputs
        h = _layer_norm(a, gamma, beta)
        c = _attention(h, context, context, Wcq, Wck, Wcv, causal=False) + h
        h = _layer_norm(c, gamma, beta)
        f = jax.nn.relu(jnp.einsum('bse,ed->bsd', h, W1) + b1)
        out = _layer_norm(f + h, gamma, beta)
        return jax.nn.relu(out)

    def _L3_ffn_ref(x, router_w, wg, wu, wd):
        import jax, jax.numpy as jnp
        import numpy as np
        E = 8
        K = 2
        CF = 1.25
        B, L, D = x.shape
        xf = x.reshape(-1, D)
        N = xf.shape[0]
        capacity = max(1, int(CF * N / E))
        logits = xf @ router_w.T
        probs = jax.nn.softmax(logits, axis=-1)
        topw, topi = jax.lax.top_k(probs, K)
        topw = topw / (topw.sum(-1, keepdims=True) + 1e-06)
        fe = topi.reshape(-1)
        fw = topw.reshape(-1)
        ft = jnp.repeat(jnp.arange(N), K)
        order = jnp.lexsort((-fw, fe))
        se, sw, st = (fe[order], fw[order], ft[order])
        counts = jax.ops.segment_sum(jnp.ones_like(se), se, num_segments=E)
        starts = jnp.cumsum(counts) - counts
        rank = jnp.arange(N * K) - starts[se]
        keep = rank < capacity
        pos = jnp.where(keep, rank, capacity)
        disp = jnp.zeros((E, capacity + 1, D), x.dtype).at[se, pos].set(xf[st])
        disp = disp[:, :capacity]
        g = jnp.einsum('ecd,edf->ecf', disp, wg)
        u = jnp.einsum('ecd,edf->ecf', disp, wu)
        eo = jnp.einsum('ecf,efd->ecd', jax.nn.silu(g) * u, wd)
        gathered = eo[se, jnp.minimum(pos, capacity - 1)]
        contrib = gathered * (sw * keep.astype(x.dtype))[:, None]
        out = jnp.zeros_like(xf).at[st].add(contrib)
        return out.reshape(B, L, D)
    x = x + _L0_attn_ref(_layernorm(x, axis=-1), L0_attn_w_qkv, L0_attn_w_out)
    x = x + _L0_xattn_ref(_layernorm(x, axis=-1), ctx_1024, ctx_1024, L0_xattn_Wq, L0_xattn_bq, L0_xattn_Wk, L0_xattn_bk, L0_xattn_Wv, L0_xattn_bv, L0_xattn_Wo, L0_xattn_bo)
    x = x + _L0_ffn_ref(_layernorm(x, axis=-1), L0_ffn_Wqkv, L0_ffn_q_scale, L0_ffn_k_scale, L0_ffn_Wo, L0_ffn_ln_g, L0_ffn_ln_b, L0_ffn_W1, L0_ffn_b1, L0_ffn_W2, L0_ffn_b2)
    x = x + _L1_attn_ref(_layernorm(x, axis=-1), L1_attn_wq, L1_attn_wk, L1_attn_wv, L1_attn_wo)
    x = x + _L1_xattn_ref(_layernorm(x, axis=-1), ctx_1024, mask_BxS2_bf1, L1_xattn_Wq, L1_xattn_Wk, L1_xattn_Wv, L1_xattn_Wo, L1_xattn_bo)
    x = x + _L1_ffn_ref(_layernorm(x, axis=-1), L1_ffn_W_exp, L1_ffn_b_exp, L1_ffn_up_weights, L1_ffn_up_bias, L1_ffn_down_weights, L1_ffn_W_con, L1_ffn_b_con, L1_ffn_down_bias)
    x = x + _L2_attn_ref(_layernorm(x, axis=-1), L2_attn_Wq, L2_attn_Wk, L2_attn_Wv, L2_attn_wq_conv, L2_attn_wk_conv, L2_attn_wv_conv, L2_attn_Wfa, L2_attn_Wfb, L2_attn_Wb, L2_attn_Wga, L2_attn_Wgb, L2_attn_A_log, L2_attn_dt_bias, L2_attn_o_norm_w, L2_attn_Wo)
    x = x + _L2_xattn_ref(_layernorm(x, axis=-1), ctx_1024, ctx_1024, L2_xattn_Wq, L2_xattn_Wk, L2_xattn_Wv)
    x = x + _L2_ffn_ref(_layernorm(x, axis=-1), L2_ffn_router_ln_w, L2_ffn_router_ln_b, L2_ffn_router_w, L2_ffn_router_b, L2_ffn_exp_ln_w, L2_ffn_exp_ln_b, L2_ffn_w1, L2_ffn_b1, L2_ffn_w2, L2_ffn_b2, L2_ffn_out_ln_w, L2_ffn_out_ln_b)
    x = x + _L3_attn_ref(_layernorm(x, axis=-1), L3_attn_in_proj_w, L3_attn_conv_w, L3_attn_conv_b, L3_attn_x_proj_w, L3_attn_dt_proj_w, L3_attn_dt_proj_b, L3_attn_A_log, L3_attn_norm_w, L3_attn_out_proj_w)
    x = x + _L3_xattn_ref(_layernorm(x, axis=-1), ctx_1024, L3_xattn_Wq, L3_xattn_Wk, L3_xattn_Wv, L3_xattn_Wcq, L3_xattn_Wck, L3_xattn_Wcv, L3_xattn_gamma, L3_xattn_beta, L3_xattn_W1, L3_xattn_b1)
    x = x + _L3_ffn_ref(_layernorm(x, axis=-1), L3_ffn_router_w, L3_ffn_wg, L3_ffn_wu, L3_ffn_wd)
    return x

_drawn_inputs = setup_inputs


def setup_inputs(seed=0):
    import zlib

    import numpy as np

    out = dict(_drawn_inputs(seed))
    spreads = {'L0_xattn_bq': (0.0, 0.8),
     'L0_xattn_bk': (0.0, 2.0),
     'L0_xattn_bv': (0.0, 0.1),
     'L0_xattn_bo': (0.0, 0.1),
     'L0_ffn_q_scale': (1.0, 0.2),
     'L0_ffn_k_scale': (1.0, 0.2),
     'L0_ffn_ln_g': (1.0, 0.6),
     'L0_ffn_ln_b': (0.0, 0.283),
     'L0_ffn_b1': (0.0, 0.1),
     'L0_ffn_b2': (0.0, 0.1),
     'L1_xattn_bo': (0.0, 0.1),
     'L1_ffn_b_exp': (0.0, 0.1),
     'L1_ffn_up_bias': (0.0, 0.1),
     'L1_ffn_b_con': (0.0, 0.1),
     'L1_ffn_down_bias': (0.0, 0.1),
     'L2_attn_dt_bias': (0.0, 0.8),
     'L2_attn_o_norm_w': (1.0, 0.6),
     'L2_ffn_router_ln_w': (1.0, 0.2),
     'L2_ffn_router_ln_b': (0.0, 0.1),
     'L2_ffn_router_b': (0.0, 0.1),
     'L2_ffn_exp_ln_w': (1.0, 0.2),
     'L2_ffn_exp_ln_b': (0.0, 0.29),
     'L2_ffn_b1': (0.0, 0.1),
     'L2_ffn_b2': (0.0, 0.1),
     'L2_ffn_out_ln_w': (1.0, 0.2),
     'L2_ffn_out_ln_b': (0.0, 0.1),
     'L3_attn_conv_b': (0.0, 0.8),
     'L3_attn_dt_proj_b': (0.0, 0.8),
     'L3_attn_norm_w': (1.0, 0.6),
     'L3_xattn_gamma': (1.0, 0.2),
     'L3_xattn_beta': (0.0, 0.1),
     'L3_xattn_b1': (0.0, 0.406)}
    factors = {'L0_xattn_Wq': 8.0,
     'L0_xattn_Wk': 8.0,
     'L1_attn_wq': 8.0,
     'L1_attn_wk': 8.0,
     'L1_xattn_Wq': 3.912,
     'L1_xattn_Wk': 4.808,
     'L2_attn_Wfa': 8.0,
     'L2_attn_Wfb': 64.0,
     'L2_attn_Wb': 3.301,
     'L2_attn_Wga': 6.357,
     'L2_attn_Wgb': 4.387,
     'L2_attn_A_log': 8.0,
     'L3_attn_in_proj_w': 8.0,
     'L3_attn_conv_w': 8.0,
     'L3_attn_x_proj_w': 8.0,
     'L3_attn_dt_proj_w': 8.0,
     'L3_attn_A_log': 8.0,
     'L3_attn_out_proj_w': 8.0}
    for name, (base, spread) in spreads.items():
        noise = np.random.default_rng([zlib.crc32(name.encode()), seed]).standard_normal(out[name].shape)
        drawn = base * np.exp(spread * noise) if base else spread * noise
        out[name] = jnp.asarray(drawn.astype(out[name].dtype))
    for name, factor in factors.items():
        out[name] = (out[name] * factor).astype(out[name].dtype)
    return out
```

```python
from contextlib import ExitStack, contextmanager

import numpy as np

import concourse.bass as bass
from concourse import mybir

P = 128
B, T, D = 4, 256, 128
TILES = B * T // P
HALVES = T // P
TOK = B * T
F32 = mybir.dt.float32
BF16 = mybir.dt.bfloat16
U8 = mybir.dt.uint8
U32 = mybir.dt.uint32
ALU = mybir.AluOpType
ACT = mybir.ActivationFunctionType
AX_X = mybir.AxisListType.X
BIG = 1e24
BANK = 512


def after(eng, sem, n):
    if n > 0:
        eng.wait_ge(sem, n)


class Chain:

    def __init__(self, eng, sem):
        self.eng, self.sem, self.n = eng, sem, 0

    def link(self, ins):
        self.n += 1
        ins.then_inc(self.sem, 1)
        self.eng.wait_ge(self.sem, self.n)


class Core:

    POOL = 44

    def __init__(self, nc, ctx, dram):
        self.nc, self.ctx, self.dram = nc, ctx, dram
        self.pools = [[nc.alloc_semaphore(f"pool{p}_{i}") for i in range(self.POOL)] for p in range(2)]
        self.turn = 0
        self.uid = 0
        self.x = self.sbuf(ctx, "x", [P, TILES, D])
        self.xT = self.sbuf(ctx, "xT", [P, TOK])
        self.ctxT = self.sbuf(ctx, "ctxT", [P, TOK])
        self.ident = self.sbuf(ctx, "ident", [P, P])
        self.identb = self.sbuf(ctx, "identb", [P, P], BF16)
        self.causal = self.sbuf(ctx, "causal", [P, HALVES, T], BF16)
        self.band = self.sbuf(ctx, "band", [P, HALVES, T], BF16)
        self.scratch = nc.dram_tensor("scratch", (4, TOK, 1024), F32, kind="Internal").ap()
        self.ps = [ctx.enter_context(nc.psum_tensor(f"bank{i}", [P, BANK], F32)) for i in range(8)]

    def sbuf(self, ctx, name, shape, dt=F32):
        self.uid += 1
        return ctx.enter_context(self.nc.sbuf_tensor(f"{name}_{self.uid}", shape, dt))

    @contextmanager
    def stage(self, *names):
        mine, other = self.pools[self.turn], self.pools[1 - self.turn]
        self.turn = 1 - self.turn
        assert len(names) <= self.POOL
        with self.nc.Block() as block:
            @block.gpsimd
            def _(pool):
                pool.sem_clear(range(other[0].num, other[-1].num + 1))
            yield (block, *mine[:len(names)])

    @contextmanager
    def loop(self, n):
        turn = self.turn
        with self.nc.Fori(0, n) as i:
            yield i
        assert self.turn == turn


def load(sync, sem, loads):
    for dst, src in loads:
        sync.dma_start(dst, src).then_inc(sem, 16)
    after(sync, sem, 16 * len(loads))


def constants(k):
    with k.stage("loaded", "zeroed", "made") as (block, loaded, zeroed, made):
        @block.sync
        def _(sync):
            load(sync, loaded, [
                (k.x[:, :, :], k.dram["x"].rearrange("(t p) d -> p t d", p=P)),
                (k.ctxT[:, :], k.dram["ctxT"]),
            ])

        @block.gpsimd
        def _(pool):
            for m in (k.ident, k.identb):
                pool.memset(m[:, :], 0.0).then_inc(zeroed, 1)
            for m in (k.causal, k.band):
                pool.memset(m[:, :, :], 0.0).then_inc(zeroed, 1)
            pool.wait_ge(zeroed, 4)
            for m in (k.ident, k.identb):
                pool.affine_select(out=m[:, :], in_=m[:, :], compare_op=ALU.not_equal, fill=1.0, base=0,
                                   pattern=[[-1, P]], channel_multiplier=1).then_inc(made, 1)
            for m in (k.causal, k.band):
                pool.affine_select(out=m[:, :, :], in_=m[:, :, :], compare_op=ALU.is_ge, fill=-BIG, base=0,
                                   pattern=[[P, HALVES], [-1, T]], channel_multiplier=1).then_inc(made, 1)
            pool.wait_ge(made, 4)
            pool.affine_select(out=k.band[:, :, :], in_=k.band[:, :, :], compare_op=ALU.is_ge, fill=-BIG,
                               base=32, pattern=[[-P, HALVES], [1, T]], channel_multiplier=-1).then_inc(made, 1)
            pool.wait_ge(made, 5)


def layer_norm(k, src, dst, dstT, eps=1e-5, loads=(), gamma=None, beta=None):
    with ExitStack() as ctx:
        stats = k.sbuf(ctx, "stats", [P, TILES, 6])
        mv = k.sbuf(ctx, "mean_var", [P, TILES, 2])
        std = k.sbuf(ctx, "std", [P, TILES])
        rstd = k.sbuf(ctx, "rstd", [P, TILES])
        with k.stage("loaded", "own", "var", "rooted", "normed", "turned", "copied") as (
                block, loaded, own, var, rooted, normed, turned, copied):
            @block.sync
            def _(sync):
                load(sync, loaded, loads)

            @block.vector
            def _(dve):
                for t in range(TILES):
                    dve.bn_stats(stats[:, t, :], src[:, t, :]).then_inc(own, 1)
                for t in range(TILES):
                    dve.wait_ge(own, t + 1)
                    dve.bn_aggr(mv[:, t, :], stats[:, t, :]).then_inc(own, 1)
                dve.wait_ge(own, 2 * TILES)
                dve.tensor_scalar(std[:, :], mv[:, :, 1], eps, None, ALU.add).then_inc(var, 1)
                dve.wait_ge(rooted, 1)
                dve.reciprocal(rstd[:, :], std[:, :]).then_inc(own, 1)
                dve.wait_ge(own, 2 * TILES + 1)
                if gamma is not None:
                    after(dve, loaded, 16 * len(loads))
                done = 2 * TILES + 1
                for t in range(TILES):
                    ins = dve.tensor_scalar(dst[:, t, :], src[:, t, :], mv[:, t, 0:1], rstd[:, t:t + 1],
                                            ALU.subtract, ALU.mult)
                    if gamma is None:
                        ins.then_inc(normed, 1)
                        continue
                    ins.then_inc(own, 1)
                    dve.wait_ge(own, done + 1)
                    dve.tensor_tensor(dst[:, t, :], dst[:, t, :], gamma, ALU.mult).then_inc(own, 1)
                    dve.wait_ge(own, done + 2)
                    dve.tensor_tensor(dst[:, t, :], dst[:, t, :], beta, ALU.add).then_inc(normed, 1)
                    done += 2

            @block.tensor
            def _(pe):
                for t in range(TILES if dstT is not None else 0):
                    pe.wait_ge(normed, t + 1)
                    pe.transpose(k.ps[t // 4][:, t % 4 * P:(t % 4 + 1) * P], dst[:, t, :],
                                 k.ident[:, :]).then_inc(turned, 1)

            @block.scalar
            def _(act):
                act.wait_ge(var, 1)
                act.activation(std[:, :], std[:, :], ACT.Sqrt).then_inc(rooted, 1)
                for half in range(2 if dstT is not None else 0):
                    act.wait_ge(turned, 4 * half + 4)
                    act.activation(dstT[:, half * 512:(half + 1) * 512], k.ps[half][:, :],
                                   ACT.Copy).then_inc(copied, 1)


def project(k, jobs, loads=()):
    RING = 4
    work = []
    for srcT, w, dst, bias, relu in jobs:
        cols = w.shape[-1]
        for t in range(TILES):
            for c in range(0, cols, BANK):
                work.append((srcT, w, dst, bias, relu, t, c, min(BANK, cols - c)))
    by_act = [w[3] is None and n % 2 == 1 for n, w in enumerate(work)]
    acts = [sum(by_act[:n]) for n in range(len(work) + 1)]
    with k.stage("loaded", "product", "dve_copied", "act_copied") as (block, loaded, product, dve_copied,
                                                                       act_copied):
        @block.sync
        def _(sync):
            load(sync, loaded, loads)

        @block.tensor
        def _(pe):
            for n, (srcT, w, _, _, _, t, c, m) in enumerate(work):
                if n >= RING:
                    after(pe, act_copied if by_act[n - RING] else dve_copied,
                          acts[n - RING + 1] if by_act[n - RING] else n - RING + 1 - acts[n - RING + 1])
                pe.matmul(k.ps[n % RING][:, :m], srcT[:, t * P:(t + 1) * P], w[:, c:c + m],
                          start=True, stop=True).then_inc(product, 1)

        @block.scalar
        def _(act):
            for n, (_, _, dst, _, relu, t, c, m) in enumerate(work):
                if by_act[n]:
                    act.wait_ge(product, n + 1)
                    act.activation(dst[:, t, c:c + m], k.ps[n % RING][:, :m],
                                   ACT.Relu if relu else ACT.Copy).then_inc(act_copied, 1)

        @block.vector
        def _(dve):
            after(dve, loaded, 16 * len(loads))
            for n, (_, _, dst, bias, relu, t, c, m) in enumerate(work):
                if by_act[n]:
                    continue
                dve.wait_ge(product, n + 1)
                if bias is not None:
                    ins = dve.tensor_tensor(dst[:, t, c:c + m], k.ps[n % RING][:, :m], bias[:, c:c + m], ALU.add)
                elif relu:
                    ins = dve.tensor_scalar(dst[:, t, c:c + m], k.ps[n % RING][:, :m], 0.0, None, ALU.max)
                else:
                    ins = dve.tensor_copy(dst[:, t, c:c + m], k.ps[n % RING][:, :m])
                ins.then_inc(dve_copied, 1)


def out_project(k, o, w, y, bias=None, loads=()):
    chunks = o.shape[2] // P
    groups = -(-chunks // 4)
    with ExitStack() as ctx:
        oT = k.sbuf(ctx, "oT", [P, 2, chunks * P])
        with k.stage("loaded", "turned", "copied", "product", "added", "biased") as (
                block, loaded, turned, copied, product, added, biased):
            @block.sync
            def _(sync):
                load(sync, loaded, loads)

            @block.tensor
            def _(pe):
                for t in range(TILES + 1):
                    if t < TILES:
                        for g in range(groups):
                            after(pe, copied, groups * (t - 2) + g + 1)
                            for c in range(4 * g, min(4 * g + 4, chunks)):
                                ins = pe.transpose(k.ps[t % 2 * 2 + g][:, c % 4 * P:(c % 4 + 1) * P],
                                                   o[:, t, c * P:(c + 1) * P], k.ident[:, :])
                            ins.then_inc(turned, 1)
                    if t >= 1:
                        u = t - 1
                        pe.wait_ge(copied, groups * (u + 1))
                        after(pe, added, u - 1)
                        for c in range(chunks):
                            ins = pe.matmul(k.ps[4 + u % 2][:, :D], oT[:, u % 2, c * P:(c + 1) * P], w[:, c, :],
                                            start=(c == 0), stop=(c == chunks - 1))
                        ins.then_inc(product, 1)

            @block.scalar
            def _(act):
                for t in range(TILES):
                    after(act, product, t - 1)
                    for g in range(groups):
                        act.wait_ge(turned, groups * t + g + 1)
                        m = min(4, chunks - 4 * g) * P
                        act.activation(oT[:, t % 2, g * 512:g * 512 + m], k.ps[t % 2 * 2 + g][:, :m],
                                       ACT.Copy).then_inc(copied, 1)

            @block.vector
            def _(dve):
                for t in range(TILES):
                    if bias is not None:
                        dve.tensor_tensor(y[:, t, :], y[:, t, :], bias, ALU.add).then_inc(biased, 1)
                        dve.wait_ge(biased, t + 1)
                    dve.wait_ge(product, t + 1)
                    dve.tensor_tensor(y[:, t, :], y[:, t, :], k.ps[4 + t % 2][:, :D],
                                      ALU.add).then_inc(added, 1)


def attention(k, q, kk, v, o, heads, d, scale, mask=None, causal=False, key_row=None, q_factor=None, k_factor=None):
    wide = 32 if d < 32 else d
    pack = min(heads, P // wide)
    packs = heads // pack
    group = min(heads, 4 if d == 64 else 16)
    keys = [P, T] if causal else [T, T]
    with ExitStack() as ctx:
        qs = k.sbuf(ctx, "q_packed", [P, 2, HALVES, P])
        ks = k.sbuf(ctx, "k_packed", [P, 2, HALVES, P])
        qkT = k.sbuf(ctx, "qkT", [P, 2, 4 * P])
        prob = k.sbuf(ctx, "prob", [P, 3, HALVES, T])
        probT = k.sbuf(ctx, "probT", [P, 2, HALVES, T])
        peak = k.sbuf(ctx, "peak", [P, heads, HALVES])
        sums = k.sbuf(ctx, "sums", [P, heads, HALVES])
        rsum = k.sbuf(ctx, "rsum", [P, heads, HALVES])

        if wide != d:
            with k.stage("zeroed") as (block, zeroed):
                @block.gpsimd
                def _(pool):
                    pool.memset(qs[:, :, :, :], 0.0).then_inc(zeroed, 1)
                    pool.memset(ks[:, :, :, :], 0.0).then_inc(zeroed, 1)
                    pool.wait_ge(zeroed, 2)

        def block_of(b):
            with k.stage("packed", "turned", "unpacked", "scored", "peaked", "scaled", "weighed", "p_turned",
                         "p_copied", "mixed", "inverted", "normed") as (
                    block, packed, turned, unpacked, scored, peaked, scaled, weighed, p_turned, p_copied, mixed,
                    inverted, normed):
                tiles = bass.ds(HALVES * b, HALVES)

                @block.gpsimd
                def _(pool):
                    for n in range(packs):
                        after(pool, turned, n - 1)
                        hs = slice(n * pack, (n + 1) * pack)
                        cols = slice(n * pack * d, (n + 1) * pack * d)
                        for dst, src, factor in ((qs, q, None), (ks, kk, k_factor)):
                            out = dst[:, n % 2, :, :].rearrange("p t (s w) -> p t s w", w=wide)[:, :, 0:pack, 0:d]
                            src = src[:, tiles, cols].rearrange("p t (h d) -> p t h d", d=d)
                            if factor is None:
                                pool.tensor_copy(out, src).then_inc(packed, 1)
                            else:
                                pool.tensor_tensor(out, src, factor[:, tiles, hs].unsqueeze(3).to_broadcast(
                                    [P, HALVES, pack, d]), ALU.mult).then_inc(packed, 1)

                @block.tensor
                def _(pe):
                    def turn(n):
                        pe.wait_ge(packed, 2 * (n + 1))
                        after(pe, unpacked, n)
                        for i, src in enumerate((qs, ks)):
                            for t in range(HALVES):
                                ins = pe.transpose(k.ps[0][:, (2 * i + t) * P:(2 * i + t + 1) * P],
                                                   src[:, n % 2, t, :], k.ident[:, :])
                        ins.then_inc(turned, 1)

                    def score(i):
                        n = i // pack
                        pe.wait_ge(unpacked, n + 1)
                        after(pe, weighed, 2 * (i - 2))
                        lo = i % pack * wide
                        bank = k.ps[1 + i % 3]
                        for t in range(HALVES):
                            out = bank[:, t * T:t * T + keys[t]]
                            ins = pe.matmul(out, qkT[lo:lo + d, n % 2, t * P:(t + 1) * P],
                                            qkT[lo:lo + d, n % 2, 2 * P:2 * P + keys[t]],
                                            start=True, stop=(mask is None and key_row is None))
                            if mask is not None:
                                ins = pe.matmul(out, k.identb[:, :], mask[:, t, 0:keys[t]], start=False, stop=True)
                            if key_row is not None:
                                ins = pe.matmul(out, key_row[0][:, :], key_row[1][:, bass.ds(b * T, T)],
                                                start=False, stop=True)
                        ins.then_inc(scored, 1)

                    def turn_prob(i):
                        pe.wait_ge(weighed, 2 * (i + 1))
                        after(pe, p_copied, i - 1)
                        for t in range(HALVES):
                            for u in range(keys[t] // P):
                                ins = pe.transpose(k.ps[4 + i % 2][:, u * T + t * P:u * T + (t + 1) * P],
                                                   prob[:, i % 3, t, u * P:(u + 1) * P], k.ident[:, :])
                        ins.then_inc(p_turned, 1)

                    def mix(i):
                        pe.wait_ge(p_copied, i + 1)
                        g = i // group
                        if i % group == 0:
                            after(pe, normed, HALVES * (g - 1))
                        for t in range(HALVES):
                            at = (t * group + i % group) * d
                            for u in range(keys[t] // P):
                                ins = pe.matmul(k.ps[6 + g % 2][:, at:at + d],
                                                probT[:, i % 2, u, t * P:(t + 1) * P],
                                                v[:, bass.ds(HALVES * b + u, 1), i * d:(i + 1) * d]
                                                .rearrange("p a d -> p (a d)"),
                                                start=(u == 0), stop=(u == keys[t] // P - 1))
                        ins.then_inc(mixed, 1)

                    turn(0)
                    for i in range(heads + 3):
                        if i < heads:
                            if i % pack == 0 and i // pack + 1 < packs:
                                turn(i // pack + 1)
                            score(i)
                        if 2 <= i < heads + 2:
                            turn_prob(i - 2)
                        if i >= 3:
                            mix(i - 3)

                @block.scalar
                def _(act):
                    def unpack(n):
                        act.wait_ge(turned, n + 1)
                        after(act, scored, (n - 1) * pack)
                        act.activation(qkT[:, n % 2, :], k.ps[0][:, :], ACT.Copy).then_inc(unpacked, 1)

                    unpack(0)
                    for i in range(heads):
                        if i % pack == 0 and i // pack + 1 < packs:
                            unpack(i // pack + 1)
                        act.wait_ge(scaled, i + 1)
                        after(act, p_turned, i - 2)
                        for t in range(HALVES):
                            by = scale if q_factor is None else q_factor[:, bass.ds(HALVES * b + t, 1), i]
                            act.activation(prob[:, i % 3, t, 0:keys[t]], k.ps[1 + i % 3][:, t * T:t * T + keys[t]],
                                           ACT.Exp, bias=peak[:, i, t:t + 1], scale=by,
                                           accum_out=sums[:, i, t:t + 1]).then_inc(weighed, 1)

                @block.vector
                def _(dve):
                    def copy_prob(i):
                        dve.wait_ge(p_turned, i + 1)
                        after(dve, mixed, i - 1)
                        bank = k.ps[4 + i % 2]
                        if causal:
                            dve.tensor_copy(probT[:, i % 2, 0, :], bank[:, 0:T])
                            dve.tensor_copy(probT[:, i % 2, 1, P:T], bank[:, T + P:2 * T]).then_inc(p_copied, 1)
                        else:
                            dve.tensor_copy(probT[:, i % 2, :, :], bank[:, :].rearrange("p (u t) -> p u t", u=2)
                                            ).then_inc(p_copied, 1)

                    def normalise(g):
                        dve.wait_ge(mixed, (g + 1) * group)
                        dve.wait_ge(weighed, 2 * (g + 1) * group)
                        hs = slice(g * group, (g + 1) * group)
                        dve.reciprocal(rsum[:, hs, :], sums[:, hs, :]).then_inc(inverted, 1)
                        dve.wait_ge(inverted, g + 1)
                        for t in range(HALVES):
                            out = o[:, bass.ds(HALVES * b + t, 1), g * group * d:(g + 1) * group * d]
                            dve.tensor_tensor(
                                out.rearrange("p a (h d) -> p (a h) d", d=d),
                                k.ps[6 + g % 2][:, t * group * d:(t + 1) * group * d].rearrange(
                                    "p (h d) -> p h d", d=d),
                                rsum[:, hs, t:t + 1].to_broadcast([P, group, d]), ALU.mult).then_inc(normed, 1)

                    for i in range(heads + 3):
                        if i < heads:
                            dve.wait_ge(scored, i + 1)
                            bank = k.ps[1 + i % 3]
                            if causal:
                                for t in range(HALVES):
                                    dve.tensor_reduce(peak[:, i, t:t + 1], bank[:, t * T:t * T + keys[t]], AX_X,
                                                      ALU.max, negate=True).then_inc(peaked, 1)
                            else:
                                dve.tensor_reduce(peak[:, i, :], bank[:, :].rearrange("p (t k) -> p t k", k=T),
                                                  AX_X, ALU.max, negate=True).then_inc(peaked, 2)
                            dve.wait_ge(peaked, 2 * (i + 1))
                            if q_factor is None:
                                dve.tensor_scalar(peak[:, i, :], peak[:, i, :], scale, None,
                                                  ALU.mult).then_inc(scaled, 1)
                            else:
                                dve.tensor_tensor(peak[:, i, :], peak[:, i, :], q_factor[:, tiles, i],
                                                  ALU.mult).then_inc(scaled, 1)
                        if 2 <= i < heads + 2:
                            copy_prob(i - 2)
                        if i >= 3 and (i - 2) % group == 0:
                            normalise((i - 2) // group - 1)

        with k.loop(B // 2) as b2:
            block_of(2 * b2)
            block_of(2 * b2 + 1)


def rope(k, jobs, tmp, swaps, norm=None):
    work = [(b, job) for b in range(B) for job in range(len(jobs))]
    with k.stage("dve_own", "pool_own") as (block, dve_own, pool_own):
        def steps(eng, sem, mine, tmps):
            done = 0
            for b, j in mine:
                qk, cos, sin = jobs[j]
                heads, d = qk.shape[2], qk.shape[3]
                at = slice(HALVES * b, HALVES * (b + 1))
                a, c = (m[:, 0:HALVES * heads * d].rearrange("p (t h d) -> p t h d", t=HALVES, h=heads) for m in tmps)
                eng.tensor_tensor(a, qk[:, at], cos.unsqueeze(2).to_broadcast([P, HALVES, heads, d]),
                                  ALU.mult).then_inc(sem, 1)
                for to, fro in swaps:
                    n = d // 2
                    eng.tensor_tensor(c[:, :, :, to], qk[:, at, :, fro],
                                      sin[:, :, to].unsqueeze(2).to_broadcast([P, HALVES, heads, n]),
                                      ALU.mult).then_inc(sem, 1)
                eng.wait_ge(sem, done + 3)
                if norm is None:
                    eng.tensor_tensor(qk[:, at], a, c, ALU.add).then_inc(sem, 1)
                    done += 4
                else:
                    eng.tensor_tensor(a, a, c, ALU.add).then_inc(sem, 1)
                    eng.wait_ge(sem, done + 4)
                    eng.tensor_tensor(qk[:, at], a, norm[j][:, at, :].unsqueeze(3).to_broadcast(
                        [P, HALVES, heads, d]), ALU.mult).then_inc(sem, 1)
                    done += 5
                eng.wait_ge(sem, done)

        n = len(work) * 5 // 8

        @block.vector
        def _(dve):
            steps(dve, dve_own, work[:n], tmp[0:2])

        @block.gpsimd
        def _(pool):
            steps(pool, pool_own, work[n:], tmp[2:4])


def layer0_attention(k):
    H, d = 16, 8
    dr = k.dram
    with ExitStack() as ctx:
        w = k.sbuf(ctx, "w_qkv", [P, 3 * D])
        wo = k.sbuf(ctx, "w_out", [P, 1, D])
        cos = k.sbuf(ctx, "cos", [P, HALVES, d])
        sin = k.sbuf(ctx, "sin", [P, HALVES, d])
        qkv = k.sbuf(ctx, "qkv", [P, TILES, 3 * D])
        o = k.sbuf(ctx, "o", [P, TILES, D])
        tmp = [k.sbuf(ctx, "rope_tmp", [P, HALVES * 2 * D]) for _ in range(4)]
        xn = k.sbuf(ctx, "xn", [P, TILES, D])
        layer_norm(k, k.x, xn, k.xT, loads=[
            (w[:, :], dr["L0_attn_w_qkv"]), (wo[:, 0, :], dr["L0_attn_w_out"]),
            (cos[:, :, :], dr["rope8"][0]), (sin[:, :, :], dr["rope8"][1])])
        project(k, [(k.xT, w, qkv, None, False)])
        qk = qkv[:, :, 0:2 * D].rearrange("p t (h d) -> p t h d", d=d)
        lo, hi = slice(0, d // 2), slice(d // 2, d)
        rope(k, [(qk, cos[:, :, :], sin[:, :, :])], tmp, [(lo, hi), (hi, lo)])
        attention(k, qkv, qkv[:, :, D:2 * D], qkv[:, :, 2 * D:3 * D], o, H, d, d ** -0.5, mask=k.causal,
                  causal=True)
        out_project(k, o, wo, k.x)


def layer0_cross(k):
    dr = k.dram
    with ExitStack() as ctx:
        w = {n: k.sbuf(ctx, n, [P, D]) for n in ("Wq", "Wk", "Wv")}
        bias = {n: k.sbuf(ctx, n, [P, D]) for n in ("bq", "bk", "bv", "bo")}
        wo = k.sbuf(ctx, "wo", [P, 1, D])
        xn, q, kk, v, o = (k.sbuf(ctx, n, [P, TILES, D]) for n in ("xn", "q", "k", "v", "o"))
        layer_norm(k, k.x, xn, k.xT, loads=[(w[n][:, :], dr["L0_xattn_" + n]) for n in w]
                   + [(bias[n][:, :], dr["L0_xattn_" + n].partition_broadcast(P)) for n in bias]
                   + [(wo[:, 0, :], dr["L0_xattn_Wo"])])
        project(k, [(k.xT, w["Wq"], q, bias["bq"], False), (k.ctxT, w["Wk"], kk, bias["bk"], False),
                    (k.ctxT, w["Wv"], v, bias["bv"], False)])
        attention(k, q, kk, v, o, 1, D, D ** -0.5)
        out_project(k, o, wo, k.x, bias["bo"][:, :])


def turn_shifted(k, y, yT, loads):
    with k.stage("loaded", "turned", "copied") as (block, loaded, turned, copied):
        @block.sync
        def _(sync):
            load(sync, loaded, loads)

        @block.tensor
        def _(pe):
            for t in range(TILES):
                pe.transpose(k.ps[t // 4][:, t % 4 * P:(t % 4 + 1) * P], y[:, t, :],
                             k.ident[:, :]).then_inc(turned, 1)

        @block.scalar
        def _(act):
            for n in range(2):
                act.wait_ge(turned, 4 * n + 4)
                act.activation(yT[0:64, n * BANK:(n + 1) * BANK], k.ps[n][0:64, :], ACT.Copy).then_inc(copied, 1)
                act.activation(yT[64:P, n * BANK:(n + 1) * BANK].rearrange("p (b t) -> p b t", t=T)[:, :, 1:T],
                               k.ps[n][64:P, :].rearrange("p (b t) -> p b t", t=T)[:, :, 0:T - 1],
                               ACT.Copy).then_inc(copied, 1)
                act.activation(yT[64:P, n * BANK:(n + 1) * BANK].rearrange("p (b t) -> p b t", t=T)[:, :, 0],
                               k.ident[64:P, 0:2], ACT.Copy).then_inc(copied, 1)


def shift_tokens(k, y, ys, loads):
    with k.stage("loaded", "copied") as (block, loaded, copied):
        @block.sync
        def _(sync):
            load(sync, loaded, [
                (ys[1:P, :, 64:D], y[0:P - 1, :, 64:D]),
                (ys[0:1, 1:TILES:2, 64:D], y[P - 1:P, 0:TILES:2, 64:D])] + loads)

        @block.gpsimd
        def _(pool):
            pool.memset(ys[0:1, 0:TILES:2, 64:D], 0.0).then_inc(copied, 1)

        @block.vector
        def _(dve):
            dve.tensor_copy(ys[:, :, 0:64], y[:, :, 0:64]).then_inc(copied, 1)


def project_rotated(k, w, qkv, d, sq, tmp, norms, stab, tabs, swaps, scale):
    RING = 8
    chunks = w.shape[-1] // BANK
    heads = w.shape[-1] // 3 // d
    with k.stage("product", "copied", "squared", "summed", "rooted", "own", "scaled", "dve_own", "pool_own",
                 "dve_rotated", "pool_rotated") as (
            block, product, copied, squared, summed, rooted, own, scaled, dve_own, pool_own, dve_rotated,
            pool_rotated):
        qk = qkv[:, :, 0:2 * heads * d].rearrange("p t (h d) -> p t h d", d=d)
        CUT = 22
        tmp = tmp.rearrange("p (h d) -> p h d", d=d)
        tmp = [tmp[:, 0:CUT], tmp[:, CUT:2 * CUT], tmp[:, 2 * CUT:CUT + 2 * heads],
               tmp[:, CUT + 2 * heads:4 * heads]]

        @block.tensor
        def _(pe):
            for n in range(TILES * chunks):
                t, c = n // chunks, n % chunks
                after(pe, copied, n - RING + 1)
                pe.matmul(k.ps[n % RING][:, :], k.xT[:, t * P:(t + 1) * P], w[:, c * BANK:(c + 1) * BANK],
                          start=True, stop=True).then_inc(product, 1)

        @block.scalar
        def _(act):
            for t in range(TILES):
                for c in range(chunks):
                    act.wait_ge(product, t * chunks + c + 1)
                    act.activation(qkv[:, t, c * BANK:(c + 1) * BANK], k.ps[(t * chunks + c) % RING][:, :],
                                   ACT.Copy).then_inc(copied, 1)
                after(act, summed, t - 1)
                act.wait_ge(copied, (t + 1) * chunks)
                act.activation(sq[:, t % 2, :, :], qk[:, t, :, :], ACT.Square).then_inc(squared, 1)
            act.wait_ge(summed, TILES)
            act.activation(norms[:, :, :], norms[:, :, :], ACT.Sqrt).then_inc(rooted, 1)

        def rotate(eng, sem, rotated, done, t, lo, hi, a, c):
            parts = [(m, max(lo, m * heads), min(hi, (m + 1) * heads)) for m in range(2)]
            parts = [p for p in parts if p[1] < p[2]]
            for m, x, y in parts:
                n = y - x
                eng.tensor_tensor(a[:, x - lo:y - lo, :], qk[:, t, x:y, :],
                                  stab[:, 2 * m, t % 2:t % 2 + 1, :].to_broadcast([P, n, d]), ALU.mult).then_inc(sem, 1)
                for to, fro in swaps:
                    eng.tensor_tensor(c[:, x - lo:y - lo, to], qk[:, t, x:y, fro],
                                      stab[:, 2 * m + 1, t % 2:t % 2 + 1, to].to_broadcast([P, n, d // 2]),
                                      ALU.mult).then_inc(sem, 1)
                done += 3
            eng.wait_ge(sem, done)
            eng.tensor_tensor(qk[:, t, lo:hi, :], a[:, 0:hi - lo, :], c[:, 0:hi - lo, :], ALU.add).then_inc(rotated, 1)
            return done

        @block.gpsimd
        def _(pool):
            for dst, src, by in tabs:
                pool.tensor_tensor(dst, src, by.unsqueeze(1).to_broadcast(list(src.shape)),
                                   ALU.mult).then_inc(scaled, 1)
            pool.wait_ge(scaled, len(tabs))
            done = 0
            for t in range(TILES):
                pool.wait_ge(squared, t + 1)
                after(pool, pool_rotated, t)
                done = rotate(pool, pool_own, pool_rotated, done, t, CUT, 2 * heads, *tmp[2:4])

        @block.vector
        def _(dve):
            dve.wait_ge(scaled, len(tabs))
            done = 0
            for t in range(TILES):
                dve.wait_ge(squared, t + 1)
                dve.tensor_reduce(norms[:, t, :], sq[:, t % 2, :, :], AX_X, ALU.add).then_inc(summed, 1)
                after(dve, dve_rotated, t)
                done = rotate(dve, dve_own, dve_rotated, done, t, 0, CUT, *tmp[0:2])
            dve.wait_ge(rooted, 1)
            dve.tensor_scalar(norms[:, :, :], norms[:, :, :], 1e-12, None, ALU.max).then_inc(own, 1)
            dve.wait_ge(own, 1)
            dve.reciprocal(norms[:, :, :], norms[:, :, :]).then_inc(own, 1)
            dve.wait_ge(own, 2)
            dve.tensor_scalar(norms[:, :, 0:heads], norms[:, :, 0:heads], scale, None, ALU.mult).then_inc(own, 1)


def glu_ffn(k, y, w1, b1, w2, b2, inner):
    chunks = [(c, min(P, inner - c)) for c in range(0, inner, P)]
    steps = [(c, n) for c in range(len(chunks)) for n in range(2)]
    with ExitStack() as ctx:
        hT = k.sbuf(ctx, "hT", [P, len(chunks), TOK])
        gate = k.sbuf(ctx, "gate", [P, 2, BANK])
        with k.stage("gated", "gelued", "upped", "hidden", "product", "biased", "added") as (
                block, gated, gelued, upped, hidden, product, biased, added):
            @block.tensor
            def _(pe):
                for s, (c, n) in enumerate(steps):
                    at, m = chunks[c]
                    cols = slice(n * BANK, (n + 1) * BANK)
                    after(pe, gelued, s - 1)
                    pe.matmul(k.ps[s % 2][:m, :], w1[:, inner + at:inner + at + m], k.xT[:, cols],
                              start=True, stop=True).then_inc(gated, 1)
                    after(pe, hidden, s - 1)
                    pe.matmul(k.ps[2 + s % 2][:m, :], w1[:, at:at + m], k.xT[:, cols],
                              start=True, stop=True).then_inc(upped, 1)
                pe.wait_ge(hidden, len(steps))
                for t in range(TILES):
                    after(pe, added, t - 1)
                    for c, (at, m) in enumerate(chunks):
                        ins = pe.matmul(k.ps[4 + t % 2][:, :D], hT[:m, c, t * P:(t + 1) * P], w2[:m, c, :],
                                        start=(c == 0), stop=(c == len(chunks) - 1))
                    ins.then_inc(product, 1)

            @block.scalar
            def _(act):
                for s, (c, n) in enumerate(steps):
                    m = chunks[c][1]
                    act.wait_ge(gated, s + 1)
                    after(act, hidden, s - 1)
                    act.activation(gate[:m, s % 2, :], k.ps[s % 2][:m, :], ACT.Gelu,
                                   bias=b1[:m, 1, c:c + 1]).then_inc(gelued, 1)

            @block.vector
            def _(dve):
                for s, (c, n) in enumerate(steps):
                    m = chunks[c][1]
                    dve.wait_ge(gelued, s + 1)
                    dve.wait_ge(upped, s + 1)
                    dve.scalar_tensor_tensor(hT[:m, c, n * BANK:(n + 1) * BANK], k.ps[2 + s % 2][:m, :],
                                             b1[:m, 0, c:c + 1], gate[:m, s % 2, :], ALU.add,
                                             ALU.mult).then_inc(hidden, 1)
                for t in range(TILES):
                    dve.tensor_tensor(y[:, t, :], y[:, t, :], b2[:, :], ALU.add).then_inc(biased, 1)
                    dve.wait_ge(biased, t + 1)
                    dve.wait_ge(product, t + 1)
                    dve.tensor_tensor(y[:, t, :], y[:, t, :], k.ps[4 + t % 2][:, :D], ALU.add).then_inc(added, 1)


def add_to_x(k, y):
    with k.stage("added") as (block, added):
        @block.vector
        def _(dve):
            dve.tensor_tensor(k.x[:, :, :], k.x[:, :, :], y[:, :, :], ALU.add).then_inc(added, 1)


def layer0_local(k):
    DEPTH, H, d, INNER = 6, 16, 64, 341
    dr = k.dram
    with ExitStack() as ctx:
        wqkv = k.sbuf(ctx, "wqkv", [P, 3 * H * d])
        wo = k.sbuf(ctx, "wo", [P, H * d // P, D])
        w1 = k.sbuf(ctx, "w1", [P, 2 * INNER])
        w2 = k.sbuf(ctx, "w2", [P, 3, D])
        b1 = k.sbuf(ctx, "b1", [P, 2, 3])
        b2 = k.sbuf(ctx, "b2", [P, D])
        g, beta = (k.sbuf(ctx, n, [P, D]) for n in ("ln_g", "ln_b"))
        tab = k.sbuf(ctx, "rotary", [P, 4, HALVES, d])
        stab = k.sbuf(ctx, "rotary_scaled", [P, 4, HALVES, d])
        scales = k.sbuf(ctx, "qk_scales", [P, 2, d])
        rnorm = k.sbuf(ctx, "rnorm", [P, TILES, 2 * H])
        y = k.sbuf(ctx, "y", [P, TILES, D])
        layer_norm(k, k.x, y, None, loads=[(tab[:, :, :, :], dr["rope64"].rearrange("m p t d -> p m t d"))])
        lo, hi = slice(0, d // 2), slice(d // 2, d)
        with k.loop(DEPTH) as i:
            def of(name):
                a = dr["L0_ffn_" + name][bass.ds(i, 1)]
                return a.rearrange("i a b -> (i a) b") if len(a.shape) == 3 else a.rearrange("i a -> (i a)")

            with ExitStack() as inner:
                qkv = k.sbuf(inner, "qkv", [P, TILES, 3 * H * d])
                o = k.sbuf(inner, "o", [P, TILES, H * d])
                qk = qkv[:, :, 0:2 * H * d].rearrange("p t (h d) -> p t h d", d=d)
                turn_shifted(k, y, k.xT, [
                    (wqkv[:, :], of("Wqkv")), (wo[:, :, :], of("Wo").rearrange("(c p) n -> p c n", p=P)),
                    (scales[:, 0, :], of("q_scale").partition_broadcast(P)),
                    (scales[:, 1, :], of("k_scale").partition_broadcast(P))])
                tabs = []
                for n in range(2):
                    tabs += [(stab[:, 2 * n, :, :], tab[:, 2 * n, :, :], scales[:, n, :]),
                             (stab[:, 2 * n + 1, :, lo], tab[:, 2 * n + 1, :, lo], scales[:, n, hi]),
                             (stab[:, 2 * n + 1, :, hi], tab[:, 2 * n + 1, :, hi], scales[:, n, lo])]
                flat = o[:, :, :].rearrange("p t n -> p (t n)")
                sq = flat[:, 0:2 * 2 * H * d].rearrange("p (a h d) -> p a h d", a=2, d=d)
                project_rotated(k, wqkv, qkv, d, sq, flat[:, 4 * H * d:], rnorm, stab, tabs, [(lo, hi), (hi, lo)], 8.0)
                HD = H * d
                attention(k, qkv, qkv[:, :, HD:2 * HD], qkv[:, :, 2 * HD:3 * HD], o, H, d, 8.0, mask=k.band,
                          causal=True, q_factor=rnorm[:, :, 0:H], k_factor=rnorm[:, :, H:2 * H])
                out_project(k, o, wo, y)
            with ExitStack() as inner:
                ys = k.sbuf(inner, "y_shifted", [P, TILES, D])
                w2_i, b1_i = of("W2"), of("b1")
                full = INNER // P
                shift_tokens(k, y, ys, [
                    (w1[:, :], of("W1")),
                    (w2[:, 0:full, :], w2_i[0:full * P, :].rearrange("(c p) n -> p c n", p=P)),
                    (w2[0:INNER - full * P, full, :], w2_i[full * P:INNER, :]),
                    (b2[:, :], of("b2").partition_broadcast(P)), (g[:, :], of("ln_g").partition_broadcast(P)),
                    (beta[:, :], of("ln_b").partition_broadcast(P))]
                    + [(b1[0:m, n, c:c + 1], b1_i[n * INNER + c * P:n * INNER + c * P + m].rearrange("(p a) -> p a", a=1))
                       for n in range(2) for c, m in ((0, P), (1, P), (2, INNER - 2 * P))])
                layer_norm(k, ys, ys, k.xT, gamma=g[:, :], beta=beta[:, :])
                glu_ffn(k, y, w1, b1, w2, b2, INNER)
        add_to_x(k, y)


def bounce(k, moves):
    with k.stage("written", "read") as (block, written, read):
        @block.sync
        def _(sync):
            for dram, src, _ in moves:
                sync.dma_start(dram, src).then_inc(written, 16)
            sync.wait_ge(written, 16 * len(moves))
            n = 0
            for _, _, reads in moves:
                for dst, src in reads:
                    sync.dma_start(dst, src).then_inc(read, 16)
                    n += 16
            sync.wait_ge(read, n)


def layer1_attention(k):
    H, d = 16, 64
    HD = H * d
    dr = k.dram
    with ExitStack() as ctx:
        w = k.sbuf(ctx, "wqkv", [P, 3 * HD])
        wo = k.sbuf(ctx, "wo", [P, HD // P, D])
        rot = k.sbuf(ctx, "rotary", [P, 2, HALVES, d])
        qkv = k.sbuf(ctx, "qkv", [P, TILES, 3 * HD])
        o = k.sbuf(ctx, "o", [P, TILES, HD])
        xn = o[:, 0, :].rearrange("p (t d) -> p t d", d=D)
        layer_norm(k, k.x, xn, k.xT, loads=[(w[:, n * HD:(n + 1) * HD], dr["L1_attn_" + name])
                                            for n, name in enumerate(("wq", "wk", "wv"))]
                   + [(wo[:, :, :], dr["L1_attn_wo"].rearrange("(c p) n -> p c n", p=P)),
                      (rot[:, :, :, :], dr["ropeP"].rearrange("m p t d -> p m t d"))])
        project(k, [(k.xT, w, qkv, None, False)])

        def as_tokens(m):
            return m.rearrange("(t p) c -> p t c", p=P)

        def as_heads(m):
            return m.rearrange("(b n) c -> b (n c)", b=B).rearrange("b (h t p d) -> b t p h d", h=H, t=HALVES, p=P)

        def parts(sb, m):
            return [(sb[:, HALVES * b + t, :].rearrange("p (h d) -> p h d", d=d), as_heads(m)[b, t])
                    for b in range(B) for t in range(HALVES)]

        scratch = [k.scratch[n] for n in range(3)]
        bounce(k, [(as_tokens(scratch[n]), qkv[:, :, n * HD:(n + 1) * HD],
                    parts(qkv[:, :, n * HD:(n + 1) * HD], scratch[n])) for n in range(3)])
        flat = o[:, :, :].rearrange("p t n -> p (t n)")
        even, odd = slice(0, d, 2), slice(1, d, 2)
        rope(k, [(qkv[:, :, n * HD:(n + 1) * HD].rearrange("p t (h d) -> p t h d", d=d), rot[:, 0, :, :],
                  rot[:, 1, :, :]) for n in range(2)],
             [flat[:, n * 2048:(n + 1) * 2048] for n in range(4)], [(even, odd), (odd, even)])
        attention(k, qkv, qkv[:, :, HD:2 * HD], qkv[:, :, 2 * HD:3 * HD], o, H, d, d ** -0.5)
        with k.stage("written", "read") as (block, written, read):
            @block.sync
            def _(sync):
                m = k.scratch[3]
                for src, dst in parts(o, m):
                    sync.dma_start(dst, src).then_inc(written, 16)
                sync.wait_ge(written, 16 * TILES)
                sync.dma_start(o[:, :, :], as_tokens(m)).then_inc(read, 16)
                sync.wait_ge(read, 16)
        out_project(k, o, wo, k.x)


def layer1_cross(k):
    H, d = 16, 64
    HD = H * d
    dr = k.dram
    with ExitStack() as ctx:
        w = {n: k.sbuf(ctx, n, [P, HD]) for n in ("Wq", "Wk", "Wv")}
        wo = k.sbuf(ctx, "wo", [P, HD // P, D])
        bo = k.sbuf(ctx, "bo", [P, D])
        valid = k.sbuf(ctx, "valid", [1, TOK], U8)
        row = k.sbuf(ctx, "mask_row", [1, TOK], BF16)
        ones = k.sbuf(ctx, "ones", [1, P], BF16)
        qkv = k.sbuf(ctx, "qkv", [P, TILES, 3 * HD])
        o = k.sbuf(ctx, "o", [P, TILES, HD])
        xn = o[:, 0, :].rearrange("p (t d) -> p t d", d=D)
        layer_norm(k, k.x, xn, k.xT, loads=[(w[n][:, :], dr["L1_xattn_" + n]) for n in w] + [
            (wo[:, :, :], dr["L1_xattn_Wo"].rearrange("(c p) n -> p c n", p=P)),
            (bo[:, :], dr["L1_xattn_bo"].partition_broadcast(P)), (valid[:, :], dr["mask_BxS2_bf1"])])
        q, kk, v = (qkv[:, :, n * HD:(n + 1) * HD] for n in range(3))
        project(k, [(k.xT, w["Wq"], q, None, False), (k.ctxT, w["Wk"], kk, None, False),
                    (k.ctxT, w["Wv"], v, None, False)])
        with k.stage("made") as (block, made):
            @block.vector
            def _(dve):
                dve.memset(ones[:, :], 1.0).then_inc(made, 1)
                dve.tensor_scalar(row[:, :], valid[:, :], 1.0, 3.38e38, ALU.subtract, ALU.mult).then_inc(made, 1)
                dve.wait_ge(made, 2)
        attention(k, q, kk, v, o, H, d, d ** -0.5, key_row=(ones, row))
        out_project(k, o, wo, k.x, bo[:, :])


def butterfly_step(eng, sem, done, y, w, tmp, stage, turned):
    s = 2 ** stage
    groups, hidden = y.shape[1], y.shape[2]
    nb = hidden // (2 * s)
    yr = y.rearrange("p g (n a s) -> p g n a s", a=2, s=s)
    a, b = yr[:, :, :, 0, :], yr[:, :, :, 1, :]
    t = [m.rearrange("p g (n s) -> p g n s", s=s) for m in tmp]

    def by(i, j):
        m = w[:, :, j, i] if turned else w[:, :, i, j]
        return m.rearrange("p (n s) -> p n s", s=s).unsqueeze(1).to_broadcast([P, groups, nb, s])

    eng.tensor_tensor(t[0], a, by(0, 0), ALU.mult).then_inc(sem, 1)
    eng.tensor_tensor(t[1], b, by(0, 1), ALU.mult).then_inc(sem, 1)
    eng.tensor_tensor(t[2], a, by(1, 0), ALU.mult).then_inc(sem, 1)
    eng.tensor_tensor(t[3], b, by(1, 1), ALU.mult).then_inc(sem, 1)
    eng.wait_ge(sem, done + 4)
    eng.tensor_tensor(a, t[0], t[1], ALU.add).then_inc(sem, 1)
    eng.tensor_tensor(b, t[2], t[3], ALU.add).then_inc(sem, 1)
    eng.wait_ge(sem, done + 6)
    return done + 6


def layer1_ffn(k):
    HID, STAGES = 512, 9
    C = HID // P
    dr = k.dram
    with ExitStack() as ctx:
        up = k.sbuf(ctx, "up", [P, 2, HID])
        down = k.sbuf(ctx, "down", [P, 1, HID])
        wu = k.sbuf(ctx, "up_weights", [P, STAGES, HID // 2, 2, 2])
        wd = k.sbuf(ctx, "down_weights", [P, STAGES, HID // 2, 2, 2])
        tmp = [k.sbuf(ctx, "tmp_up", [P, 2, HID // 2]) for _ in range(4)]
        tmp2 = [k.sbuf(ctx, "tmp_down", [P, 1, HID // 2]) for _ in range(4)]
        up_bias = k.sbuf(ctx, "up_bias", [P, C])
        bias = k.sbuf(ctx, "bias", [P, C])
        bc, bd = (k.sbuf(ctx, n, [P, D]) for n in ("b_con", "down_bias"))
        contract = k.sbuf(ctx, "contract", [P, C, D])
        hT = k.sbuf(ctx, "hT", [P, C, TOK])
        xn = k.sbuf(ctx, "xn", [P, TILES, D])
        layer_norm(k, k.x, xn, k.xT, loads=[
            (up[:, 0, :], dr["L1_ffn_W_exp"]), (up[:, 1, :], dr["L1_ffn_b_exp"].partition_broadcast(P)),
            (down[:, 0, :], dr["L1_ffn_W_con"]),
            (wu[:, :, :, :, :].rearrange("p s n i j -> p (s n i j)"), dr["L1_ffn_up_weights"].partition_broadcast(P)),
            (wd[:, :, :, :, :].rearrange("p s n i j -> p (s n i j)"), dr["L1_ffn_down_weights"].partition_broadcast(P)),
            (up_bias[:, :], dr["L1_ffn_up_bias"]),
            (bc[:, :], dr["L1_ffn_b_con"].partition_broadcast(P)),
            (bd[:, :], dr["L1_ffn_down_bias"].partition_broadcast(P))])
        with k.stage("up_own", "down_own", "turned", "down_turned", "biased", "contracted") as (
                block, up_own, down_own, turned, down_turned, biased, contracted):
            @block.vector
            def _(dve):
                done = 0
                for s in range(STAGES):
                    done = butterfly_step(dve, up_own, done, up[:, :, :], wu[:, s], [m[:, :, :] for m in tmp], s, False)
                dve.wait_ge(turned, 1)
                dve.tensor_tensor(bias[:, :], k.ps[0][:, 0:HID:P], up_bias[:, :], ALU.add).then_inc(biased, 1)
                dve.wait_ge(down_turned, 1)
                dve.tensor_copy(contract[:, :, :], k.ps[1][:, :].rearrange("p (c d) -> p c d", d=D)
                                ).then_inc(contracted, 1)

            @block.gpsimd
            def _(pool):
                done = 0
                for s in reversed(range(STAGES)):
                    done = butterfly_step(pool, down_own, done, down[:, :, :], wd[:, s], [m[:, :, :] for m in tmp2], s,
                                          True)

            @block.tensor
            def _(pe):
                pe.wait_ge(up_own, 6 * STAGES)
                for c in range(C):
                    ins = pe.transpose(k.ps[0][:, c * P:(c + 1) * P], up[:, 1, c * P:(c + 1) * P], k.ident[:, :])
                ins.then_inc(turned, 1)
                pe.wait_ge(down_own, 6 * STAGES)
                for c in range(C):
                    ins = pe.transpose(k.ps[1][:, c * P:(c + 1) * P], down[:, 0, c * P:(c + 1) * P], k.ident[:, :])
                ins.then_inc(down_turned, 1)

        with k.stage("upped", "gelued", "product", "own", "added") as (block, upped, gelued, product, own, added):
            @block.tensor
            def _(pe):
                for s in range(2 * C):
                    c, n = s // 2, s % 2
                    after(pe, gelued, s - 3)
                    pe.matmul(k.ps[s % 4][:, :], up[:, 0, c * P:(c + 1) * P], k.xT[:, n * BANK:(n + 1) * BANK],
                              start=True, stop=True).then_inc(upped, 1)
                pe.wait_ge(gelued, 2 * C)
                for t in range(TILES):
                    after(pe, added, t - 1)
                    for c in range(C):
                        ins = pe.matmul(k.ps[4 + t % 2][:, :D], hT[:, c, t * P:(t + 1) * P], contract[:, c, :],
                                        start=(c == 0), stop=(c == C - 1))
                    ins.then_inc(product, 1)

            @block.scalar
            def _(act):
                for s in range(2 * C):
                    c, n = s // 2, s % 2
                    act.wait_ge(upped, s + 1)
                    act.activation(hT[:, c, n * BANK:(n + 1) * BANK], k.ps[s % 4][:, :], ACT.Gelu,
                                   bias=bias[:, c:c + 1]).then_inc(gelued, 1)

            @block.vector
            def _(dve):
                dve.tensor_tensor(bc[:, :], bc[:, :], bd[:, :], ALU.add).then_inc(own, 1)
                dve.wait_ge(own, 1)
                for t in range(TILES):
                    dve.tensor_tensor(k.x[:, t, :], k.x[:, t, :], bc[:, :], ALU.add).then_inc(own, 1)
                    dve.wait_ge(own, t + 2)
                    dve.wait_ge(product, t + 1)
                    dve.tensor_tensor(k.x[:, t, :], k.x[:, t, :], k.ps[4 + t % 2][:, :D], ALU.add).then_inc(added, 1)


def delta_setup(k, w, low, beta, neg_a, wb, loads_a_log):
    with k.stage("product", "betas", "copied") as (block, product, betas, copied):
        @block.tensor
        def _(pe):
            for m in range(2):
                for n in range(2):
                    pe.matmul(k.ps[2 * m + n][:, :], w[:, m, :], k.xT[:, n * BANK:(n + 1) * BANK],
                              start=True, stop=True).then_inc(product, 1)
            for t in range(TILES):
                ins = pe.matmul(k.ps[4][:, t * 8:(t + 1) * 8], k.xT[:, t * P:(t + 1) * P], wb[:, :],
                                start=True, stop=True)
            ins.then_inc(betas, 1)

        @block.vector
        def _(dve):
            for m in range(2):
                for n in range(2):
                    dve.wait_ge(product, 2 * m + n + 1)
                    dve.tensor_copy(low[:, m, n * BANK:(n + 1) * BANK], k.ps[2 * m + n][:, :]).then_inc(copied, 1)

        @block.scalar
        def _(act):
            act.activation(neg_a[:, 0, :], loads_a_log, ACT.Exp).then_inc(copied, 1)
            act.wait_ge(betas, 1)
            act.activation(beta[:, :, :], k.ps[4][:, 0:TILES * 8].rearrange("p (t h) -> p t h", h=8),
                           ACT.Sigmoid).then_inc(copied, 1)
            act.wait_ge(copied, 6)
            act.activation(neg_a[:, 1, :], neg_a[:, 0, :], ACT.Copy, scale=-1.0).then_inc(copied, 1)


def delta_qkv(k, w, conv, qkv, loads):
    with k.stage("loaded", "arrived", "product", "tapped", "added", "silu") as (
            block, loaded, arrived, product, tapped, added, silu):
        @block.sync
        def _(sync):
            load(sync, loaded, loads)
            sync.sem_inc(arrived, 1)

        @block.tensor
        def _(pe):
            pe.wait_ge(arrived, 1)
            for m in range(3):
                for n in range(2):
                    pe.matmul(k.ps[2 * m + n][:, :], w[:, m, :], k.xT[:, n * BANK:(n + 1) * BANK],
                              start=True, stop=True).then_inc(product, 1)

        @block.scalar
        def _(act):
            act.wait_ge(arrived, 1)
            for m in range(3):
                for n in range(2):
                    act.wait_ge(product, 2 * m + n + 1)
                    act.activation(qkv[:, m, n * BANK:(n + 1) * BANK], k.ps[2 * m + n][:, :], ACT.Copy,
                                   scale=conv[:, m, 3:4]).then_inc(tapped, 1)
            for m in range(3):
                act.wait_ge(added, 6 * (m + 1))
                act.activation(qkv[:, m, :], qkv[:, m, :], ACT.Silu).then_inc(silu, 1)

        @block.vector
        def _(dve):
            done = 0
            for m in range(3):
                for n in range(2):
                    dve.wait_ge(tapped, 2 * m + n + 1)
                    y = qkv[:, m, n * BANK:(n + 1) * BANK].rearrange("p (b t) -> p b t", t=T)
                    x = k.ps[2 * m + n][:, :].rearrange("p (b t) -> p b t", t=T)
                    for back in (1, 2, 3):
                        dve.scalar_tensor_tensor(y[:, :, back:T], x[:, :, 0:T - back], conv[:, m, 3 - back:4 - back],
                                                 y[:, :, back:T], ALU.mult, ALU.add).then_inc(added, 1)
                        done += 1
                        dve.wait_ge(added, done)


def log1p_small(dve, sem, done, e, series, small):
    dve.tensor_scalar(small, e, 1.0 / 64, None, ALU.is_lt).then_inc(sem, 1)
    dve.tensor_scalar(series, e, -0.25, None, ALU.mult).then_inc(sem, 1)
    for n, c in enumerate((1.0 / 3, -0.5, 1.0)):
        dve.wait_ge(sem, done + 2 + n)
        dve.scalar_tensor_tensor(series, series, c, e, ALU.add, ALU.mult).then_inc(sem, 1)
    dve.wait_ge(sem, done + 5)


def delta_gates(k, h, s):
    nq, nk = (s["factors"][:, 0:TILES], s["factors"][:, TILES:2 * TILES])
    with k.stage("squared", "z", "gate", "v_turned", "sums", "absed", "logs", "floored", "own", "rooted",
                 "own_pool", "sig", "act_own") as (
            block, squared, z, gate, v_turned, sums, absed, logs, floored, own, rooted, own_pool, sig, act_own):
        q, kk, v = (s["qkv"][:, m, :] for m in range(3))
        spare = s["kq"].rearrange("p a t m d -> p (a t m d)")
        log, series, small = (spare[:, n * TOK:(n + 1) * TOK] for n in range(3))

        @block.gpsimd
        def _(pool):
            pool.tensor_tensor(s["sq"][:, 0, :], q, q, ALU.mult).then_inc(squared, 1)
            pool.tensor_tensor(s["sq"][:, 1, :], kk, kk, ALU.mult).then_inc(squared, 1)
            pool.tensor_tensor(s["sq"][:, 2, :], q, kk, ALU.mult).then_inc(squared, 1)
            pool.memset(s["suffix"][:, :], 0.0).then_inc(own_pool, 1)

        @block.tensor
        def _(pe):
            for n in range(2):
                pe.matmul(k.ps[n][:, :], s["w"][:, 3, :], s["low"][:, 0, n * BANK:(n + 1) * BANK],
                          start=True, stop=True).then_inc(z, 1)
            for t in range(TILES):
                cols = slice(t % 4 * P, (t % 4 + 1) * P)
                pe.matmul(k.ps[2 + t // 4][:, cols], s["low"][:, 1, t * P:(t + 1) * P], s["w"][:, 4, :],
                          start=True, stop=True).then_inc(gate, 1)
            for t in range(TILES):
                cols = slice(t % 4 * P, (t % 4 + 1) * P)
                pe.transpose(k.ps[4 + t // 4][:, cols], v[:, t * P:(t + 1) * P], k.ident[:, :]).then_inc(v_turned, 1)
            for m in range(3):
                pe.wait_ge(squared, m + 1)
                for t in range(TILES):
                    ins = pe.matmul(k.ps[6][:, m * TILES + t:m * TILES + t + 1], s["sq"][:, m, t * P:(t + 1) * P],
                                    s["ones"][:, :], start=True, stop=True)
            ins.then_inc(sums, 1)

        @block.scalar
        def _(act):
            for n in range(2):
                cols = slice(n * BANK, (n + 1) * BANK)
                act.wait_ge(z, n + 1)
                act.activation(s["decay"][:, cols], k.ps[n][:, :], ACT.Abs, bias=s["dt"][:, 0:1]).then_inc(absed, 1)
            act.wait_ge(absed, 2)
            act.activation(s["decay"][:, :], s["decay"][:, :], ACT.Exp, scale=-1.0).then_inc(absed, 1)
            act.wait_ge(absed, 3)
            act.activation(log, s["decay"][:, :], ACT.Ln, bias=1.0).then_inc(logs, 1)
            act.wait_ge(own, 1)
            act.activation(s["factors"][:, :], s["factors"][:, :], ACT.Sqrt).then_inc(rooted, 1)
            for n in range(2):
                act.wait_ge(gate, 4 * n + 4)
                act.activation(s["gate"][:, 4 * n:4 * n + 4, :], k.ps[2 + n][:, :].rearrange(
                    "p (t d) -> p t d", d=P), ACT.Sigmoid).then_inc(sig, 1)

        @block.vector
        def _(dve):
            dve.wait_ge(sums, 1)
            dve.tensor_scalar(s["factors"][:, :], k.ps[6][:, 0:2 * TILES], 1.0 / P, 1e-6, ALU.mult,
                              ALU.add).then_inc(own, 1)
            for n in range(2):
                cols = slice(n * BANK, (n + 1) * BANK)
                dve.wait_ge(absed, n + 1)
                dve.tensor_scalar(s["prefix"][:, cols], k.ps[n][:, :], s["dt"][:, 0:1], 0.0, ALU.add,
                                  ALU.max).then_inc(floored, 1)
            dve.wait_ge(absed, 3)
            log1p_small(dve, floored, 2, s["decay"][:, :], series, small)
            dve.wait_ge(logs, 1)
            dve.copy_predicated(log, small.bitcast(U32), series).then_inc(floored, 1)
            dve.wait_ge(floored, 2 + 5 + 1)
            dve.tensor_tensor(s["prefix"][:, :], s["prefix"][:, :], log, ALU.add).then_inc(own, 1)
            dve.wait_ge(own, 2)
            dve.tensor_scalar(s["prefix"][:, :], s["prefix"][:, :], s["neg_a"][:, 1, bass.ds(h, 1)], None,
                              ALU.mult).then_inc(own, 1)
            dve.wait_ge(rooted, 1)
            dve.reciprocal(s["factors"][:, :], s["factors"][:, :]).then_inc(own, 1)
            dve.wait_ge(own, 4)
            beta = s["beta"][:, :, bass.ds(h, 1)].rearrange("p t a -> p (t a)")
            scale = float(P) ** -0.5
            dve.scalar_tensor_tensor(s["v_factor"][:, :], nk, scale, beta, ALU.mult, ALU.mult).then_inc(own, 1)
            dve.wait_ge(own, 5)
            dve.scalar_tensor_tensor(s["k_factor"][:, :], nk, scale, s["v_factor"][:, :], ALU.mult,
                                     ALU.mult).then_inc(own, 1)
            dve.tensor_scalar(s["q_factor"][:, :], nq, scale * scale, None, ALU.mult).then_inc(own, 1)
            dve.wait_ge(own, 7)
            dve.tensor_scalar(s["minus_k_factor"][:, :], s["k_factor"][:, :], -1.0, None, ALU.mult).then_inc(own, 1)
            dve.tensor_copy(s["qk_same"][:, :], k.ps[6][:, 2 * TILES:3 * TILES]).then_inc(own, 1)
            dve.wait_ge(own, 9)
            for t in range(TILES):
                dve.wait_ge(v_turned, t + 1)
                dve.tensor_scalar(s["vb"][:, t, :], k.ps[4 + t // 4][:, t % 4 * P:(t % 4 + 1) * P],
                                  s["v_factor"][:, t:t + 1], None, ALU.mult).then_inc(own, 1)
                dve.tensor_scalar(s["att"][:, t, :], k.ident[:, :], s["qk_same"][:, t:t + 1], None,
                                  ALU.mult).then_inc(own, 1)
                for a in range(2):
                    dve.tensor_copy(s["inv"][:, t, a, :], k.ident[:, :]).then_inc(own, 1)


def delta_levels(k, s):
    LEVELS = 7
    PAIRS = TILES // 2
    STEPS = LEVELS * PAIRS
    q, kk = s["qkv"][:, 0, :], s["qkv"][:, 1, :]

    def split(m, l):
        return m.rearrange("p (n a s) -> p n a s", a=2, s=2 ** l)

    with k.stage("summed", "own_pool", "decayed", "k_scaled", "q_scaled", "paired", "masked", "folded", "unfolded",
                 "corrected", "updated") as (block, summed, own_pool, decayed, k_scaled, q_scaled, paired, masked,
                                             folded, unfolded, corrected, updated):
        @block.gpsimd
        def _(pool):
            for l in range(LEVELS + 1):
                if l > 0:
                    pre, suf = split(s["prefix"], l - 1), split(s["suffix"], l - 1)
                    shape = [P, pre.shape[1], 2 ** (l - 1)]
                    end = 2 ** (l - 1) - 1
                    pool.wait_ge(decayed, 2 * l)
                    pool.tensor_tensor(suf[:, :, 0, :], suf[:, :, 0, :], pre[:, :, 1, end:end + 1].to_broadcast(shape),
                                       ALU.add).then_inc(own_pool, 1)
                    pool.wait_ge(own_pool, 2 * l - 1)
                    pool.tensor_tensor(pre[:, :, 1, :], pre[:, :, 1, :], pre[:, :, 0, end:end + 1].to_broadcast(shape),
                                       ALU.add).then_inc(own_pool, 1)
                    pool.wait_ge(own_pool, 2 * l)
                    pool.sem_inc(summed, 1)
                if l < LEVELS:
                    pool.wait_ge(decayed, 2 * (l + 1))
                    after(pool, paired, PAIRS * (l - 1))
                    pool.tensor_tensor(s["kq"][:, l % 2, :, 0, :], kk.rearrange("p (t d) -> p t d", d=P),
                                       s["scales"][:, l % 2, :].rearrange("p (t d) -> p t d", d=P),
                                       ALU.mult).then_inc(k_scaled, 1)

        @block.scalar
        def _(act):
            def exps(l):
                if l > 0:
                    act.wait_ge(summed, l)
                after(act, k_scaled, l - 1)
                after(act, q_scaled, l - 1)
                out = split(s["scales"][:, l % 2, :], l)
                act.activation(out[:, :, 0, :], split(s["suffix"], l)[:, :, 0, :], ACT.Exp).then_inc(decayed, 1)
                act.activation(out[:, :, 1, :], split(s["prefix"], l)[:, :, 1, :], ACT.Exp).then_inc(decayed, 1)

            exps(0)
            for n in range(STEPS):
                if n % PAIRS == 0 and n // PAIRS + 1 < LEVELS:
                    exps(n // PAIRS + 1)
                act.wait_ge(folded, n + 1)
                after(act, corrected, n - 1)
                act.activation(s["fold"][:, n % 2, :], k.ps[2 + n % 2][:, 0:2 * P], ACT.Copy).then_inc(unfolded, 1)

        @block.tensor
        def _(pe):
            def pair(n):
                l, p = n // PAIRS, n % PAIRS
                if p == 0:
                    pe.wait_ge(k_scaled, l + 1)
                    pe.wait_ge(q_scaled, l + 1)
                after(pe, masked, n - 1)
                for a in range(2):
                    ins = pe.matmul(k.ps[n % 2][:, a * 2 * P:(a + 1) * 2 * P], s["kq"][:, l % 2, 2 * p + a, 0, :],
                                    s["kq"][:, l % 2, 2 * p + a, :, :], start=True, stop=True)
                ins.then_inc(paired, 1)

            def fold(n):
                p = n % PAIRS
                pe.wait_ge(masked, n + 1)
                after(pe, updated, n - PAIRS + 1)
                after(pe, unfolded, n - 1)
                for a in range(2):
                    ins = pe.matmul(k.ps[2 + n % 2][:, a * P:(a + 1) * P], s["lower"][:, 2 * p + a, :],
                                    s["inv"][:, 2 * p + a, 1, :], start=True, stop=True)
                ins.then_inc(folded, 1)

            def correct(n):
                p = n % PAIRS
                pe.wait_ge(unfolded, n + 1)
                after(pe, updated, n - 1)
                for a in range(2):
                    y = s["fold"][:, n % 2, a * P:(a + 1) * P]
                    at = a * 2 * P
                    pe.matmul(k.ps[4 + n % 2][:, at:at + P], y, s["inv"][:, 2 * p + a, 0, :], start=True, stop=True)
                    ins = pe.matmul(k.ps[4 + n % 2][:, at + P:at + 2 * P], s["inv"][:, 2 * p + a, 0, :], y,
                                    start=True, stop=True)
                ins.then_inc(corrected, 1)

            for n in range(STEPS + 2):
                if n < STEPS:
                    pair(n)
                if 1 <= n < STEPS + 1:
                    fold(n - 1)
                if n >= 2:
                    correct(n - 2)

        @block.vector
        def _(dve):
            def scale_q(l):
                dve.wait_ge(decayed, 2 * (l + 1))
                after(dve, paired, PAIRS * (l - 1))
                dve.tensor_tensor(s["kq"][:, l % 2, :, 1, :], q.rearrange("p (t d) -> p t d", d=P),
                                  s["scales"][:, l % 2, :].rearrange("p (t d) -> p t d", d=P),
                                  ALU.mult).then_inc(q_scaled, 1)

            scale_q(0)
            for n in range(STEPS + 2):
                if n < STEPS:
                    l, p = n // PAIRS, n % PAIRS
                    dve.wait_ge(paired, n + 1)
                    after(dve, folded, n - PAIRS + 1)
                    for a in range(2):
                        t = 2 * p + a
                        dve.scalar_tensor_tensor(s["lower"][:, t, :], k.ps[n % 2][:, a * 2 * P:a * 2 * P + P],
                                                 s["k_factor"][:, t:t + 1], s["right_left"][:, l, :], ALU.mult,
                                                 ALU.mult)
                    dve.copy_predicated(s["att"][:, 2 * p:2 * p + 2, :],
                                        s["left_right"].bitcast(U32)[:, l, :].unsqueeze(1).to_broadcast([P, 2, P]),
                                        k.ps[n % 2][:, :].rearrange("p (a m i) -> p a m i", a=2, m=2)[:, :, 1, :]
                                        ).then_inc(masked, 1)
                if n >= 2:
                    m = n - 2
                    p = m % PAIRS
                    dve.wait_ge(corrected, m + 1)
                    inv = s["inv"][:, 2 * p:2 * p + 2, :, :].rearrange("p a m i -> p (a m i)")
                    dve.tensor_tensor(inv, inv, k.ps[4 + m % 2][:, :], ALU.subtract).then_inc(updated, 1)
                if n % PAIRS == 1 and n // PAIRS + 1 < LEVELS and n < STEPS:
                    scale_q(n // PAIRS + 1)


def delta_outputs(k, h, s):
    q, kk = (s["qkv"][:, m, :].rearrange("p (b c t) -> p b c t", c=HALVES, t=P) for m in range(2))
    pre, suf = (s[n].rearrange("p (b c t) -> p b c t", c=HALVES, t=P) for n in ("prefix", "suffix"))
    with k.stage("decayed", "scaled", "k_turned", "k_copied", "u0", "u0_copied", "o0", "state", "state_copied",
                 "read", "w1", "u1", "u1_copied", "o1", "own", "squared", "rooted", "gated") as (
            block, decayed, scaled, k_turned, k_copied, u0, u0_copied, o0, state, state_copied, read, w1, u1,
            u1_copied, o1, own, squared, rooted, gated):
        def bank(i, b):
            return k.ps[i][:, b * P:(b + 1) * P]

        @block.scalar
        def _(act):
            act.activation(s["ends"][:, 0, :, :], suf[:, :, 0, :], ACT.Exp).then_inc(decayed, 1)
            act.activation(s["ends"][:, 1, :, :], pre[:, :, 1, :], ACT.Exp).then_inc(decayed, 1)
            act.wait_ge(u0, 1)
            act.activation(s["u"][:, 0, :, :], k.ps[1][:, :].rearrange("p (b d) -> p b d", d=P),
                           ACT.Copy).then_inc(u0_copied, 1)
            act.wait_ge(state, 1)
            act.activation(s["state"][:, :, :], k.ps[3][:, :].rearrange("p (b d) -> p b d", d=P),
                           ACT.Copy).then_inc(state_copied, 1)
            act.wait_ge(u1, 1)
            act.activation(s["u"][:, 1, :, :], k.ps[5][:, :].rearrange("p (b d) -> p b d", d=P),
                           ACT.Copy).then_inc(u1_copied, 1)
            for b in range(B):
                for c in range(HALVES):
                    act.wait_ge(own, HALVES * b + c + 1)
                    act.activation(s["sq"][:, 0, 0:P], s["o_head"][:, HALVES * b + c, :], ACT.Square,
                                   accum_out=s["o_sums"][:, HALVES * b + c:HALVES * b + c + 1]).then_inc(squared, 1)
                    act.wait_ge(squared, HALVES * b + c + 1)
            act.wait_ge(own, TILES + 1)
            act.activation(s["o_sums"][:, :], s["o_sums"][:, :], ACT.Sqrt).then_inc(rooted, 1)

        @block.gpsimd
        def _(pool):
            pool.wait_ge(decayed, 2)
            pool.tensor_tensor(s["k_end"][:, :, :], kk[:, :, 0, :], s["ends"][:, 0, :, :], ALU.mult).then_inc(scaled, 1)
            pool.tensor_tensor(s["k_start"][:, :, :], kk[:, :, 1, :], s["ends"][:, 1, :, :], ALU.mult).then_inc(scaled, 1)
            pool.tensor_tensor(s["q_start"][:, :, :], q[:, :, 1, :], s["ends"][:, 1, :, :], ALU.mult).then_inc(scaled, 1)
            for t in range(TILES):
                pool.tensor_tensor(s["gate"][:, t, :], s["gate"][:, t, :], s["norm_w"][:, :], ALU.mult).then_inc(gated, 1)

        @block.tensor
        def _(pe):
            for b in range(B):
                ins = pe.matmul(bank(1, b), s["inv"][:, HALVES * b, 1, :], s["vb"][:, HALVES * b, :], start=True, stop=True)
            ins.then_inc(u0, 1)
            pe.wait_ge(scaled, 1)
            for b in range(B):
                ins = pe.transpose(bank(0, b), s["k_end"][:, b, :], k.ident[:, :])
            ins.then_inc(k_turned, 1)
            pe.wait_ge(u0_copied, 1)
            for b in range(B):
                ins = pe.matmul(bank(2, b), s["att"][:, HALVES * b, :], s["u"][:, 0, b, :], start=True, stop=True)
            ins.then_inc(o0, 1)
            pe.wait_ge(k_copied, 1)
            for b in range(B):
                ins = pe.matmul(bank(3, b), s["k_end_tokens"][:, b, :], s["u"][:, 0, b, :], start=True, stop=True)
            ins.then_inc(state, 1)
            pe.wait_ge(state_copied, 1)
            pe.wait_ge(scaled, 3)
            for b in range(B):
                ins = pe.matmul(bank(4, b), s["k_start"][:, b, :], s["state"][:, b, :], start=True, stop=True)
            ins.then_inc(read, 1)
            pe.wait_ge(w1, B)
            for b in range(B):
                ins = pe.matmul(bank(5, b), s["inv"][:, HALVES * b + 1, 1, :], s["vb"][:, HALVES * b + 1, :],
                                start=True, stop=True)
            ins.then_inc(u1, 1)
            pe.wait_ge(u1_copied, 1)
            for b in range(B):
                pe.matmul(bank(6, b), s["q_start"][:, b, :], s["state"][:, b, :], start=True, stop=False)
                ins = pe.matmul(bank(6, b), s["att"][:, HALVES * b + 1, :], s["u"][:, 1, b, :], start=False, stop=True)
            ins.then_inc(o1, 1)

        @block.vector
        def _(dve):
            dve.wait_ge(k_turned, 1)
            dve.tensor_copy(s["k_end_tokens"][:, :, :], k.ps[0][:, :].rearrange("p (b d) -> p b d", d=P)
                            ).then_inc(k_copied, 1)
            dve.wait_ge(read, 1)
            for b in range(B):
                t = HALVES * b + 1
                dve.scalar_tensor_tensor(s["vb"][:, t, :], bank(4, b), s["minus_k_factor"][:, t:t + 1], s["vb"][:, t, :],
                                         ALU.mult, ALU.add).then_inc(w1, 1)
            dve.wait_ge(o1, 1)
            for b in range(B):
                for c in range(HALVES):
                    t = HALVES * b + c
                    dve.tensor_scalar(s["o_head"][:, t, :], bank(2 if c == 0 else 6, b), s["q_factor"][:, t:t + 1], None,
                                      ALU.mult).then_inc(own, 1)
            dve.wait_ge(squared, TILES)
            dve.tensor_scalar(s["o_sums"][:, :], s["o_sums"][:, :], 1.0 / P, 1e-5, ALU.mult, ALU.add).then_inc(own, 1)
            dve.wait_ge(rooted, 1)
            dve.reciprocal(s["o_sums"][:, :], s["o_sums"][:, :]).then_inc(own, 1)
            dve.wait_ge(own, TILES + 2)
            dve.wait_ge(gated, TILES)
            for t in range(TILES):
                dve.scalar_tensor_tensor(s["o"][:, t, bass.ds(h * P, P)], s["o_head"][:, t, :], s["o_sums"][:, t:t + 1],
                                         s["gate"][:, t, :], ALU.mult, ALU.mult)


def layer2_delta(k):
    H = 8
    dr = k.dram
    with ExitStack() as ctx:
        s = {}

        def room(name, shape, dt=F32):
            t = k.sbuf(ctx, name, shape, dt)
            s[name] = t[tuple(slice(None) for _ in shape)]
            return s[name]

        bottleneck = room("bottleneck", [P, 2, P])
        wb = room("wb", [P, H])
        room("beta", [P, TILES, H])
        room("neg_a", [P, 2, H])
        room("a_log", [P, H])
        room("low", [P, 2, TOK])
        room("w", [P, 5, P])
        room("conv", [P, 3, 4])
        room("dt", [P, 1])
        room("norm_w", [P, P])
        room("ones", [P, 1])
        room("right_left", [P, 7, P])
        room("left_right", [P, 7, P])
        room("qkv", [P, 3, TOK])
        room("sq", [P, 3, TOK])
        for name in ("decay", "prefix", "suffix"):
            room(name, [P, TOK])
        for name in ("vb", "att", "gate", "lower", "o_head"):
            room(name, [P, TILES, P])
        room("inv", [P, TILES, 2, P])
        room("factors", [P, 2 * TILES])
        for name in ("v_factor", "k_factor", "q_factor", "minus_k_factor", "qk_same", "o_sums"):
            room(name, [P, TILES])
        room("kq", [P, 2, TILES, 2, P])
        room("scales", [P, 2, TOK])
        room("fold", [P, 2, 2 * P])
        room("ends", [P, 2, B, P])
        for name in ("k_end", "k_start", "q_start", "k_end_tokens", "state"):
            room(name, [P, B, P])
        room("u", [P, 2, B, P])
        room("o", [P, TILES, H * P])
        wo = room("wo", [P, H, D])
        layer_norm(k, k.x, s["o_head"], k.xT, loads=[
            (bottleneck[:, 0, :], dr["L2_attn_Wfa"]), (bottleneck[:, 1, :], dr["L2_attn_Wga"]), (wb, dr["L2_attn_Wb"]),
            (s["a_log"], dr["L2_attn_A_log"].partition_broadcast(P)),
            (s["norm_w"], dr["L2_attn_o_norm_w"].partition_broadcast(P)), (s["right_left"], dr["right_left"]),
            (s["left_right"], dr["left_right"]), (wo, dr["L2_attn_Wo"].rearrange("(c p) n -> p c n", p=P))])
        delta_setup(k, bottleneck, s["low"], s["beta"], s["neg_a"], wb, s["a_log"])
        with k.stage("made") as (block, made):
            @block.gpsimd
            def _(pool):
                pool.memset(s["ones"], 1.0).then_inc(made, 1)
        with k.loop(H) as h:
            delta_qkv(k, s["w"], s["conv"], s["qkv"], [
                (s["w"][:, n, :], dr["L2_attn_" + name][:, bass.ds(h * P, P)])
                for n, name in enumerate(("Wq", "Wk", "Wv", "Wfb", "Wgb"))] + [
                (s["conv"][:, n, :], dr[f"L2_attn_w{name}_conv"][bass.ds(h * P, P), :]) for n, name in enumerate("qkv")]
                + [(s["dt"], dr["L2_attn_dt_bias"][bass.ds(h * P, P), :])])
            delta_gates(k, h, s)
            delta_levels(k, s)
            delta_outputs(k, h, s)
        out_project(k, s["o"], wo, k.x)


def layer2_cross(k):
    H, d = 16, 8
    dr = k.dram
    with ExitStack() as ctx:
        w = {n: k.sbuf(ctx, n, [P, D]) for n in ("Wq", "Wk", "Wv")}
        xn, q, kk, v, o = (k.sbuf(ctx, n, [P, TILES, D]) for n in ("xn", "q", "k", "v", "o"))
        layer_norm(k, k.x, xn, k.xT, loads=[(w[n][:, :], dr["L2_xattn_" + n]) for n in w])
        project(k, [(k.xT, w["Wq"], q, None, True), (k.ctxT, w["Wk"], kk, None, True),
                    (k.ctxT, w["Wv"], v, None, True)])
        attention(k, q, kk, v, o, H, d, d ** -0.5)
        add_to_x(k, o)


def first_best(dve, own, values, best, hit, tmp, rising):
    shape = list(values.shape)
    own.link(dve.tensor_reduce(best, values, AX_X, ALU.max))
    own.link(dve.tensor_tensor(tmp, values, best.unsqueeze(2).to_broadcast(shape), ALU.is_equal))
    own.link(dve.tensor_tensor(tmp, tmp, rising.unsqueeze(1).to_broadcast(shape), ALU.mult))
    own.link(dve.tensor_reduce(hit[:, :, 0], tmp, AX_X, ALU.max))
    own.link(dve.tensor_copy(best_index := hit[:, :, 1], hit[:, :, 0]))
    own.link(dve.tensor_tensor(tmp, tmp, best_index.unsqueeze(2).to_broadcast(shape), ALU.is_equal))
    own.link(dve.tensor_copy(hit, tmp))


def experts(k, E, F, source, weights, gate, total, gated):
    C = F // P
    ups = 2 if gated else 1
    with ExitStack() as ctx:
        up = k.sbuf(ctx, "expert_up", [P, 2, ups, F])
        down = k.sbuf(ctx, "expert_down", [P, 2, C, D])
        cols = k.sbuf(ctx, "expert_columns", [P, 2, C + 2])
        scaled = k.sbuf(ctx, "expert_x", [P, TOK])
        hT = k.sbuf(ctx, "hT", [P, C, TOK])
        act_out = k.sbuf(ctx, "act_out", [P, 2, BANK])

        def loads(e, at):
            def of(name):
                a = weights[name][bass.ds(e, 1)]
                return a.rearrange("e a b -> (e a) b")
            if gated:
                ins = [(up[:, at, 0, :], of("wg")), (up[:, at, 1, :], of("wu"))]
                last = "wd"
            else:
                ins = [(up[:, at, 0, :], of("w1")), (cols[:, at, :], of("cols"))]
                last = "w2"
            return ins + [(down[:, at, :, :], of(last).rearrange("(c p) n -> p c n", p=P))]

        def one(e, at, following):
            steps = [(c, n) for c in range(C) for n in range(2)]
            with k.stage("loaded", "scaled", "gates", "acted", "ups", "hidden", "product", "added") as (
                    block, loaded, x_scaled, gates, acted, upped, hidden, product, added):
                x = source if gated else scaled

                @block.sync
                def _(sync):
                    load(sync, loaded, following)

                @block.tensor
                def _(pe):
                    if not gated:
                        pe.wait_ge(x_scaled, 1)
                    for s, (c, n) in enumerate(steps):
                        after(pe, acted, s - 1)
                        pe.matmul(k.ps[s % 2][:, :], up[:, at, 0, c * P:(c + 1) * P], x[:, n * BANK:(n + 1) * BANK],
                                  start=True, stop=True).then_inc(gates, 1)
                        if gated:
                            after(pe, hidden, s - 1)
                            pe.matmul(k.ps[2 + s % 2][:, :], up[:, at, 1, c * P:(c + 1) * P],
                                      x[:, n * BANK:(n + 1) * BANK], start=True, stop=True).then_inc(upped, 1)
                    pe.wait_ge(hidden if gated else acted, len(steps))
                    for t in range(TILES):
                        after(pe, added, t - 1)
                        for c in range(C):
                            ins = pe.matmul(k.ps[4 + t % 2][:, :D], hT[:, c, t * P:(t + 1) * P], down[:, at, c, :],
                                            start=(c == 0), stop=(c == C - 1))
                        ins.then_inc(product, 1)

                @block.scalar
                def _(act):
                    for s, (c, n) in enumerate(steps):
                        act.wait_ge(gates, s + 1)
                        if gated:
                            after(act, hidden, s - 1)
                            act.activation(act_out[:, s % 2, :], k.ps[s % 2][:, :], ACT.Silu).then_inc(acted, 1)
                        else:
                            act.activation(hT[:, c, n * BANK:(n + 1) * BANK], k.ps[s % 2][:, :], ACT.Gelu,
                                           bias=cols[:, at, 2 + c:3 + c]).then_inc(acted, 1)

                @block.vector
                def _(dve):
                    if gated:
                        for s, (c, n) in enumerate(steps):
                            dve.wait_ge(acted, s + 1)
                            dve.wait_ge(upped, s + 1)
                            dve.tensor_tensor(hT[:, c, n * BANK:(n + 1) * BANK], k.ps[2 + s % 2][:, :],
                                              act_out[:, s % 2, :], ALU.mult).then_inc(hidden, 1)
                    else:
                        dve.tensor_scalar(scaled[:, :], source[:, :], cols[:, at, 0:1], cols[:, at, 1:2], ALU.mult,
                                          ALU.add).then_inc(x_scaled, 1)
                    for t in range(TILES):
                        dve.wait_ge(product, t + 1)
                        g = gate[:, t, bass.ds(e, 1)] if not isinstance(e, int) else gate[:, t, e:e + 1]
                        dve.scalar_tensor_tensor(total[:, t, :], k.ps[4 + t % 2][:, :D], g, total[:, t, :], ALU.mult,
                                                 ALU.add).then_inc(added, 1)

        with k.stage("loaded") as (block, loaded):
            @block.sync
            def _(sync):
                load(sync, loaded, loads(0, 0))
        with k.loop(E // 2 - 1) as i:
            one(2 * i, 0, loads(2 * i + 1, 1))
            one(2 * i + 1, 1, loads(2 * i + 2, 0))
        one(E - 2, 0, loads(E - 1, 1))
        one(E - 1, 1, [])


def layer2_ffn(k):
    E, F = 8, 512
    dr = k.dram
    with ExitStack() as ctx:
        xn = k.sbuf(ctx, "xn", [P, TILES, D])
        routed = k.sbuf(ctx, "routed", [P, TOK])
        total = k.sbuf(ctx, "total", [P, TILES, D])
        ln = k.sbuf(ctx, "router_ln", [P, 2])
        rw = k.sbuf(ctx, "router_w", [P, E])
        rb = k.sbuf(ctx, "router_b", [P, E])
        b2 = k.sbuf(ctx, "b2", [E, D])
        ow, ob = (k.sbuf(ctx, n, [P, D]) for n in ("out_ln_w", "out_ln_b"))
        rising = k.sbuf(ctx, "rising", [P, E])
        logits, tmp, one, two, gate = (k.sbuf(ctx, n, [P, TILES, E]) for n in (
            "logits", "tmp", "first", "second", "gate"))
        best = k.sbuf(ctx, "best", [P, 4, TILES])
        gateT = k.sbuf(ctx, "gateT", [E, TOK])
        layer_norm(k, k.x, xn, None, loads=[
            (ln[:, 0:1], dr["L2_ffn_router_ln_w"].rearrange("(p a) -> p a", a=1)),
            (ln[:, 1:2], dr["L2_ffn_router_ln_b"].rearrange("(p a) -> p a", a=1)), (rw[:, :], dr["L2_ffn_router_w"]),
            (rb[:, :], dr["L2_ffn_router_b"].partition_broadcast(P)), (b2[:, :], dr["L2_ffn_b2"]),
            (ow[:, :], dr["L2_ffn_out_ln_w"].partition_broadcast(P)),
            (ob[:, :], dr["L2_ffn_out_ln_b"].partition_broadcast(P)), (rising[:, :], dr["rising"])])
        layer_norm(k, xn, xn, k.xT)
        DIFF, FINAL = 17, 23
        with k.stage("routed", "scored", "own", "exped", "turned", "copied", "product") as (
                block, x_routed, scored, own, exped, turned, copied, product):
            @block.vector
            def _(dve):
                dve.tensor_scalar(routed[:, :], k.xT[:, :], ln[:, 0:1], ln[:, 1:2], ALU.mult,
                                  ALU.add).then_inc(x_routed, 1)
                chain = Chain(dve, own)
                dve.wait_ge(scored, 1)
                full = [P, TILES, E]
                chain.link(dve.tensor_tensor(logits[:, :, :], k.ps[0][:, 0:TILES * E].rearrange(
                    "p (t e) -> p t e", e=E), rb[:, :].unsqueeze(1).to_broadcast(full), ALU.add))
                first_best(dve, chain, logits[:, :, :], best[:, 0, :], one[:, :, :], tmp[:, :, :], rising[:, :])
                chain.link(dve.scalar_tensor_tensor(logits[:, :, :], one[:, :, :], -BIG, logits[:, :, :], ALU.mult,
                                                    ALU.add))
                first_best(dve, chain, logits[:, :, :], best[:, 1, :], two[:, :, :], tmp[:, :, :], rising[:, :])
                chain.link(dve.tensor_tensor(best[:, 2, :], best[:, 1, :], best[:, 0, :], ALU.subtract))
                dve.wait_ge(exped, 1)
                chain.link(dve.tensor_scalar(best[:, 0, :], best[:, 3, :], 1.0, None, ALU.add))
                chain.link(dve.reciprocal(best[:, 0, :], best[:, 0, :]))
                chain.link(dve.tensor_tensor(best[:, 1, :], best[:, 3, :], best[:, 0, :], ALU.mult))
                chain.link(dve.tensor_tensor(one[:, :, :], one[:, :, :], best[:, 0, :].unsqueeze(2).to_broadcast(full),
                                             ALU.mult))
                chain.link(dve.tensor_tensor(two[:, :, :], two[:, :, :], best[:, 1, :].unsqueeze(2).to_broadcast(full),
                                             ALU.mult))
                chain.link(dve.tensor_tensor(gate[:, :, :], one[:, :, :], two[:, :, :], ALU.add))
                assert chain.n == FINAL
                for n in range(2):
                    dve.wait_ge(turned, n + 1)
                    dve.tensor_copy(gateT[:, n * BANK:(n + 1) * BANK], k.ps[1 + n][0:E, :]).then_inc(copied, 1)
                for n in range(2):
                    dve.wait_ge(product, n + 1)
                    dve.tensor_copy(total[:, 4 * n:4 * n + 4, :], k.ps[3 + n][:, :].rearrange("p (t d) -> p t d", d=D))

            @block.scalar
            def _(act):
                act.wait_ge(own, DIFF)
                act.activation(best[:, 3, :], best[:, 2, :], ACT.Exp).then_inc(exped, 1)

            @block.tensor
            def _(pe):
                pe.wait_ge(x_routed, 1)
                for t in range(TILES):
                    ins = pe.matmul(k.ps[0][:, t * E:(t + 1) * E], routed[:, t * P:(t + 1) * P], rw[:, :],
                                    start=True, stop=True)
                ins.then_inc(scored, 1)
                pe.wait_ge(own, FINAL)
                for t in range(TILES):
                    ins = pe.transpose(k.ps[1 + t // 4][0:E, t % 4 * P:(t % 4 + 1) * P], gate[:, t, :], k.ident[:, :])
                    if t % 4 == 3:
                        ins.then_inc(turned, 1)
                pe.wait_ge(copied, 2)
                for t in range(TILES):
                    ins = pe.matmul(k.ps[3 + t // 4][:, t % 4 * P:(t % 4 + 1) * P], gateT[:, t * P:(t + 1) * P],
                                    b2[:, :], start=True, stop=True)
                    if t % 4 == 3:
                        ins.then_inc(product, 1)

        experts(k, E, F, k.xT, {"w1": dr["L2_ffn_w1"], "cols": dr["L2_ffn_cols"], "w2": dr["L2_ffn_w2"]}, gate, total,
                False)
        layer_norm(k, total, total, None, gamma=ow[:, :], beta=ob[:, :])
        add_to_x(k, total)


def scan_inputs(k, s):
    with k.stage("product", "tapped", "added", "biased", "silu", "rows", "projected", "row_copied", "dt",
                 "own", "absed", "logs", "split", "neg", "fresh") as (
            block, product, tapped, added, biased, silu, rows, projected, row_copied, dt, own, absed, logs, split,
            neg, fresh):
        def halves(m, n):
            return m[:, n * BANK:(n + 1) * BANK]

        @block.tensor
        def _(pe):
            for c in range(4):
                for n in range(2):
                    pe.matmul(k.ps[2 * c + n][:, :], s["in_proj"][:, c * P:(c + 1) * P], halves(k.xT, n), start=True,
                              stop=True).then_inc(product, 1)
            pe.wait_ge(silu, 2)
            for n in range(2):
                for c in range(2):
                    ins = pe.matmul(k.ps[n][0:1, :], s["x_proj"][:, c, 0:1], halves(s["xc"][:, c, :], n),
                                    start=(c == 0), stop=(c == 1))
                ins.then_inc(rows, 1)
            pe.wait_ge(silu, 6)
            for m in range(2):
                for n in range(2):
                    for c in range(2):
                        ins = pe.matmul(k.ps[4 + 2 * m + n][:, :], s["x_proj"][:, c, 1 + m * P:1 + (m + 1) * P],
                                        halves(s["xc"][:, c, :], n), start=(c == 0), stop=(c == 1))
                    ins.then_inc(projected, 1)
            pe.wait_ge(row_copied, 2)
            for c in range(2):
                for n in range(2):
                    pe.matmul(k.ps[2 * c + n][:, :], s["dt_w"][:, c * P:(c + 1) * P], halves(s["row"], n), start=True,
                              stop=True).then_inc(dt, 1)

        @block.scalar
        def _(act):
            for c in range(2):
                for n in range(2):
                    act.wait_ge(product, 2 * c + n + 1)
                    act.activation(halves(s["xc"][:, c, :], n), k.ps[2 * c + n][:, :], ACT.Copy,
                                   scale=s["conv"][:, c, 3:4]).then_inc(tapped, 1)
            for c in range(2):
                act.wait_ge(added, 6 * (c + 1))
                act.activation(s["xc"][:, c, :], s["xc"][:, c, :], ACT.Silu, bias=s["conv"][:, c, 4:5]).then_inc(silu, 1)
            for c in range(2):
                for n in range(2):
                    act.wait_ge(product, 4 + 2 * c + n + 1)
                    act.activation(halves(s["z"][:, c, :], n), k.ps[4 + 2 * c + n][:, :], ACT.Silu).then_inc(silu, 1)
            for n in range(2):
                act.wait_ge(rows, n + 1)
                act.activation(halves(s["row"], n), k.ps[n][0:1, :], ACT.Copy).then_inc(row_copied, 1)
            for c in range(2):
                for n in range(2):
                    act.wait_ge(dt, 2 * c + n + 1)
                    act.activation(halves(s["e"][:, c, :], n), k.ps[2 * c + n][:, :], ACT.Abs,
                                   bias=s["dt_b"][:, c:c + 1]).then_inc(absed, 1)
            act.wait_ge(absed, 4)
            act.activation(s["e"], s["e"], ACT.Exp, scale=-1.0).then_inc(absed, 1)
            act.wait_ge(absed, 5)
            act.activation(s["log"], s["e"], ACT.Ln, bias=1.0).then_inc(logs, 1)
            act.activation(s["a"], s["a_log"], ACT.Exp).then_inc(neg, 1)
            act.wait_ge(neg, 1)
            act.activation(s["a"], s["a"], ACT.Copy, scale=-1.0).then_inc(neg, 1)

        @block.vector
        def _(dve):
            done = 0
            for c in range(2):
                for n in range(2):
                    dve.wait_ge(tapped, 2 * c + n + 1)
                    y = halves(s["xc"][:, c, :], n).rearrange("p (b t) -> p b t", t=T)
                    x = k.ps[2 * c + n][:, :].rearrange("p (b t) -> p b t", t=T)
                    for back in (1, 2, 3):
                        dve.scalar_tensor_tensor(y[:, :, back:T], x[:, :, 0:T - back], s["conv"][:, c, 3 - back:4 - back],
                                                 y[:, :, back:T], ALU.mult, ALU.add).then_inc(added, 1)
                        done += 1
                        dve.wait_ge(added, done)
            chain = Chain(dve, split)
            for m in range(2):
                for n in range(2):
                    dve.wait_ge(projected, 2 * m + n + 1)
                    chain.link(dve.tensor_copy(halves(s["rest"], n), k.ps[4 + 2 * m + n][:, :]))
                for part in range(3):
                    chain.link(dve.tensor_copy(s["parts"][:, m, part, :], s["rest"]))
                    if part < 2:
                        chain.link(dve.tensor_tensor(s["rest"], s["rest"], s["parts"][:, m, part, :], ALU.subtract))
            chain = Chain(dve, own)
            for c in range(2):
                for n in range(2):
                    dve.wait_ge(absed, 2 * c + n + 1)
                    chain.link(dve.tensor_scalar(halves(s["dt"][:, c, :], n), k.ps[2 * c + n][:, :],
                                                 s["dt_b"][:, c:c + 1], 0.0, ALU.add, ALU.max))
            dve.wait_ge(absed, 5)
            e, series, small, log, sdt = (s[n].rearrange("p c t -> p (c t)") for n in ("e", "series", "small", "log", "dt"))
            log1p_small(dve, fresh, 0, e, series, small)
            dve.wait_ge(logs, 1)
            chain.link(dve.copy_predicated(log, small.bitcast(U32), series))
            chain.link(dve.tensor_tensor(sdt, sdt, log, ALU.add))
            chain.link(dve.tensor_tensor(s["dtx"], s["dt"], s["xc"], ALU.mult))
            chain.link(dve.memset(s["decay"].rearrange("p c (b t) -> p c b t", t=T)[:, :, :, 0], 0.0))


def scan_states(k, s, state, per):
    UNITS = 2 * per
    with k.stage("spread_b", "spread_c", "b_copied", "a_copied", "decayed", "driven", "scanned", "weighted",
                 "summed") as (
            block, spread_b, spread_c, b_copied, a_copied, decayed, driven, scanned, weighted, summed):
        @block.tensor
        def _(pe):
            def spread(i, m, sem):
                row = k.identb[:, bass.ds(state + i, 1)].to_broadcast([P, P])
                for n in range(2):
                    for part in range(3):
                        ins = pe.matmul(k.ps[2 * m + n][:, :], row, s["parts"][:, m, part, n * BANK:(n + 1) * BANK],
                                        start=(part == 0), stop=(part == 2))
                ins.then_inc(sem, 1)

            def accumulate(u):
                pe.wait_ge(weighted, u + 1)
                for n in range(2):
                    ins = pe.matmul(k.ps[4 + u % 2 * 2 + n][:, :], k.ident[:, :], s["hc"][:, u % 2, n * BANK:(n + 1) * BANK],
                                    start=False, stop=False, skip_group_check=True)
                ins.then_inc(summed, 1)

            spread(0, 0, spread_b)
            for i in range(per + 1):
                if i < per:
                    after(pe, weighted, 2 * i)
                    spread(i, 1, spread_c)
                    if i + 1 < per:
                        after(pe, b_copied, i + 1)
                        spread(i + 1, 0, spread_b)
                if i >= 1:
                    accumulate(2 * i - 2)
                    accumulate(2 * i - 1)

        @block.scalar
        def _(act):
            for i in range(per):
                act.wait_ge(spread_b, i + 1)
                after(act, driven, 2 * (i - 1))
                for n in range(2):
                    ins = act.activation(s["b_rows"][:, i % 2, n * BANK:(n + 1) * BANK], k.ps[n][:, :], ACT.Copy)
                ins.then_inc(b_copied, 1)
                for c in range(2):
                    u = 2 * i + c
                    after(act, scanned, u - 1)
                    act.activation(s["decay"][:, u % 2, :].rearrange("p (b t) -> p b t", t=T)[:, :, 1:T],
                                   s["dt"][:, c, :].rearrange("p (b t) -> p b t", t=T)[:, :, 1:T], ACT.Exp,
                                   scale=s["a_now"][:, i:i + 1]).then_inc(decayed, 1)

        @block.gpsimd
        def _(pool):
            for u in range(UNITS):
                i, c = u // 2, u % 2
                pool.wait_ge(b_copied, i + 1)
                after(pool, scanned, u - 1)
                pool.tensor_tensor(s["drive"][:, u % 2, :], s["dtx"][:, c, :], s["b_rows"][:, i % 2, :],
                                   ALU.mult).then_inc(driven, 1)

        @block.vector
        def _(dve):
            for u in range(UNITS):
                i = u // 2
                dve.wait_ge(decayed, u + 1)
                dve.wait_ge(driven, u + 1)
                dve.tensor_tensor_scan(s["h"][:, u % 2, :], s["decay"][:, u % 2, :], s["drive"][:, u % 2, :], 0.0,
                                       ALU.mult, ALU.add).then_inc(scanned, 1)
                dve.wait_ge(scanned, u + 1)
                dve.wait_ge(spread_c, i + 1)
                after(dve, summed, u - 1)
                for n in range(2):
                    ins = dve.tensor_tensor(s["hc"][:, u % 2, n * BANK:(n + 1) * BANK],
                                            s["h"][:, u % 2, n * BANK:(n + 1) * BANK], k.ps[2 + n][:, :], ALU.mult)
                ins.then_inc(weighted, 1)


def copy_rates(k, s, state, per):
    with k.stage("copied") as (block, copied):
        @block.vector
        def _(dve):
            dve.tensor_copy(s["a_now"], s["a"][:, bass.ds(state, per)]).then_inc(copied, 1)


def scan_outputs(k, s):
    with k.stage("squared", "sums", "gated", "own", "rooted", "product", "added") as (
            block, squared, sums, gated, own, rooted, product, added):
        y = [k.ps[4 + i] for i in range(4)]

        @block.scalar
        def _(act):
            for i in range(4):
                act.activation(s["sq"][:, i // 2, i % 2 * BANK:(i % 2 + 1) * BANK], y[i][:, :],
                               ACT.Square).then_inc(squared, 1)
            act.wait_ge(own, 1)
            act.activation(s["r"], s["r"], ACT.Sqrt).then_inc(rooted, 1)

        @block.tensor
        def _(pe):
            pe.wait_ge(squared, 4)
            for t in range(TILES):
                for c in range(2):
                    ins = pe.matmul(k.ps[0][:, t:t + 1], s["sq"][:, c, t * P:(t + 1) * P], s["ones"], start=(c == 0),
                                    stop=(c == 1))
            ins.then_inc(sums, 1)
            pe.wait_ge(gated, 4)
            for t in range(TILES):
                after(pe, added, t - 1)
                for c in range(2):
                    ins = pe.matmul(k.ps[1 + t % 2][:, :D], s["z"][:, c, t * P:(t + 1) * P], s["out_proj"][:, c, :],
                                    start=(c == 0), stop=(c == 1))
                ins.then_inc(product, 1)

        @block.vector
        def _(dve):
            for i in range(4):
                dve.wait_ge(squared, i + 1)
                z = s["z"][:, i // 2, i % 2 * BANK:(i % 2 + 1) * BANK]
                dve.scalar_tensor_tensor(z, y[i][:, :], s["conv"][:, i // 2, 5:6], z, ALU.mult, ALU.mult).then_inc(gated, 1)
            dve.wait_ge(sums, 1)
            dve.tensor_scalar(s["r"], k.ps[0][:, 0:TILES], 1.0 / 256, float(np.finfo(np.float32).eps), ALU.mult,
                              ALU.add).then_inc(own, 1)
            dve.wait_ge(rooted, 1)
            dve.reciprocal(s["r"], s["r"]).then_inc(own, 1)
            dve.wait_ge(own, 2)
            for t in range(TILES):
                dve.wait_ge(product, t + 1)
                dve.scalar_tensor_tensor(k.x[:, t, :], k.ps[1 + t % 2][:, :D], s["r"][:, t:t + 1], k.x[:, t, :],
                                         ALU.mult, ALU.add).then_inc(added, 1)


def layer3_scan(k):
    PER = 8
    dr = k.dram
    with ExitStack() as ctx:
        s = {}

        def room(name, shape, dt=F32):
            t = k.sbuf(ctx, name, shape, dt)
            s[name] = t[tuple(slice(None) for _ in shape)]
            return s[name]

        room("in_proj", [P, 4 * P])
        room("x_proj", [P, 2, 2 * P + 1])
        room("dt_w", [1, 2 * P])
        room("dt_b", [P, 2])
        room("conv", [P, 2, 6])
        room("a_log", [P, P])
        room("a", [P, P])
        room("a_now", [P, PER])
        room("out_proj", [P, 2, D])
        room("row", [1, TOK])
        room("rest", [P, TOK])
        room("parts", [P, 2, 3, TOK], BF16)
        for name in ("xc", "z", "e", "log", "series", "small", "dt", "dtx"):
            room(name, [P, 2, TOK])
        for name in ("b_rows", "decay", "drive", "h", "hc"):
            room(name, [P, 2, TOK])
        s["sq"] = s["h"]
        room("ones", [P, 1])
        room("r", [P, TILES])
        xn = room("xn", [P, TILES, D])
        layer_norm(k, k.x, xn, k.xT, loads=[
            (s["in_proj"], dr["L3_attn_in_proj_w"]),
            (s["x_proj"], dr["L3_attn_x_proj_w"].rearrange("(c p) n -> p c n", p=P)),
            (s["dt_w"], dr["L3_attn_dt_proj_w"]), (s["dt_b"], dr["L3_attn_dt_proj_b"]),
            (s["conv"], dr["L3_attn_columns"].rearrange("(c p) n -> p c n", p=P)),
            (s["a_log"], dr["L3_attn_A_log"].partition_broadcast(P)),
            (s["out_proj"], dr["L3_attn_out_proj_w"].rearrange("(c p) n -> p c n", p=P))])
        scan_inputs(k, s)
        with k.stage("zeroed") as (block, zeroed):
            @block.vector
            def _(dve):
                dve.memset(s["h"][:, 0, 0:BANK], 0.0).then_inc(zeroed, 1)
                dve.memset(s["ones"], 1.0).then_inc(zeroed, 1)

            @block.tensor
            def _(pe):
                pe.wait_ge(zeroed, 1)
                for i in range(4):
                    pe.matmul(k.ps[4 + i][:, :], k.ident[:, :], s["h"][:, 0, 0:BANK], start=True, stop=False,
                              skip_group_check=True)
        with k.loop(P // PER) as i:
            copy_rates(k, s, PER * i, PER)
            scan_states(k, s, PER * i, PER)
        with k.stage("closed") as (block, closed):
            @block.vector
            def _(dve):
                dve.memset(s["h"][:, 0, 0:BANK], 0.0).then_inc(closed, 1)

            @block.tensor
            def _(pe):
                pe.wait_ge(closed, 1)
                for i in range(4):
                    pe.matmul(k.ps[4 + i][:, :], k.ident[:, :], s["h"][:, 0, 0:BANK], start=False, stop=True,
                              skip_group_check=True)
        scan_outputs(k, s)


def combine(k, dst, a, b, floor=False):
    with k.stage("done") as (block, done):
        @block.vector
        def _(dve):
            if floor:
                dve.scalar_tensor_tensor(dst[:, :, :], a[:, :, :], 0.0, b[:, :, :], ALU.max, ALU.add).then_inc(done, 1)
            else:
                dve.tensor_tensor(dst[:, :, :], a[:, :, :], b[:, :, :], ALU.add).then_inc(done, 1)


def layer3_cross(k):
    dr = k.dram
    EPS = 1e-3
    with ExitStack() as ctx:
        w = {n: k.sbuf(ctx, n, [P, D]) for n in ("Wq", "Wk", "Wv", "Wcq", "Wck", "Wcv", "W1")}
        rows = {n: k.sbuf(ctx, n, [P, D]) for n in ("gamma", "beta", "b1")}
        xn, q, kk, v, o = (k.sbuf(ctx, n, [P, TILES, D]) for n in ("xn", "q", "k", "v", "o"))
        gamma, beta = rows["gamma"][:, :], rows["beta"][:, :]
        layer_norm(k, k.x, xn, k.xT, loads=[(w[n][:, :], dr["L3_xattn_" + n]) for n in w]
                   + [(rows[n][:, :], dr["L3_xattn_" + n].partition_broadcast(P)) for n in rows])
        project(k, [(k.xT, w["Wq"], q, None, False), (k.xT, w["Wk"], kk, None, False),
                    (k.xT, w["Wv"], v, None, False)])
        attention(k, q, kk, v, o, 1, D, D ** -0.5, mask=k.causal, causal=True)
        combine(k, xn, o, xn)
        layer_norm(k, xn, xn, k.xT, eps=EPS, gamma=gamma, beta=beta)
        project(k, [(k.xT, w["Wcq"], q, None, False), (k.ctxT, w["Wck"], kk, None, False),
                    (k.ctxT, w["Wcv"], v, None, False)])
        attention(k, q, kk, v, o, 1, D, D ** -0.5)
        combine(k, xn, o, xn)
        layer_norm(k, xn, xn, k.xT, eps=EPS, gamma=gamma, beta=beta)
        project(k, [(k.xT, w["W1"], q, rows["b1"], False)])
        combine(k, q, q, xn, floor=True)
        layer_norm(k, q, q, None, eps=EPS, gamma=gamma, beta=beta)
        combine(k, k.x, q, k.x, floor=True)


def rank_weights(k, e, wsel, w_col, rank, counts, scr):
    with k.stage("copied", "spread", "counted", "own") as (block, copied, spread, counted, own):
        @block.gpsimd
        def _(pool):
            pool.tensor_copy(w_col[:, :], wsel[:, :, bass.ds(e, 1)].rearrange("p t a -> p (t a)")).then_inc(copied, 1)

        @block.tensor
        def _(pe):
            pe.wait_ge(copied, 1)
            for t in range(TILES):
                ins = pe.transpose(k.ps[t // 4][:, t % 4 * P:(t % 4 + 1) * P], w_col[:, t:t + 1].to_broadcast([P, P]),
                                   k.ident[:, :])
            ins.then_inc(spread, 1)

        @block.scalar
        def _(act):
            act.wait_ge(spread, 1)
            for n in range(2):
                act.activation(scr[:, 0, n * BANK:(n + 1) * BANK], k.ps[n][:, :], ACT.Copy).then_inc(counted, 1)

        @block.vector
        def _(dve):
            dve.wait_ge(counted, 2)
            n = 0
            for t in range(TILES):
                at = t * P
                if t > 0:
                    dve.tensor_scalar(scr[:, 1, 0:at], scr[:, 0, 0:at], w_col[:, t:t + 1], 0.0, ALU.is_ge, ALU.add,
                                      accum_out=counts[:, 0, t:t + 1]).then_inc(own, 1)
                    n += 1
                dve.tensor_scalar(scr[:, 1, at:TOK], scr[:, 0, at:TOK], w_col[:, t:t + 1], 0.0, ALU.is_gt, ALU.add,
                                  accum_out=counts[:, 1, t:t + 1]).then_inc(own, 1)
                dve.scalar_tensor_tensor(scr[:, 2, 0:P], scr[:, 0, at:at + P], w_col[:, t:t + 1], scr[:, 3, 0:P],
                                         ALU.is_equal, ALU.mult, accum_out=counts[:, 2, t:t + 1]).then_inc(own, 1)
                n += 2
                dve.wait_ge(own, n)
            dve.tensor_tensor(counts[:, 1, :], counts[:, 0, :], counts[:, 1, :], ALU.add).then_inc(own, 1)
            dve.wait_ge(own, n + 1)
            dve.tensor_tensor(rank[:, :, bass.ds(e, 1)].rearrange("p t a -> p (t a)"), counts[:, 1, :],
                              counts[:, 2, :], ALU.add).then_inc(own, 1)


def layer3_ffn(k):
    E, F = 8, 512
    CAPACITY = int(1.25 * TOK / E)
    dr = k.dram
    with ExitStack() as ctx:
        xn = k.sbuf(ctx, "xn", [P, TILES, D])
        total = k.sbuf(ctx, "total", [P, TILES, D])
        rw = k.sbuf(ctx, "router_w", [P, E])
        rising = k.sbuf(ctx, "rising", [P, E])
        probs, tmp, one, two, gate, wsel, rank = (k.sbuf(ctx, n, [P, TILES, E]) for n in (
            "probs", "tmp", "first", "second", "gate", "weights", "rank"))
        best = k.sbuf(ctx, "best", [P, 5, TILES])
        w_col = k.sbuf(ctx, "w_col", [P, TILES])
        counts = k.sbuf(ctx, "counts", [P, 3, TILES])
        scr = k.sbuf(ctx, "compared", [P, 4, TOK])
        layer_norm(k, k.x, xn, k.xT, loads=[(rw[:, :], dr["L3_ffn_router_w"]), (rising[:, :], dr["rising"]),
                                            (scr[:, 3, 0:P], dr["earlier"])])
        with k.stage("scored", "own", "exped") as (block, scored, own, exped):
            full = [P, TILES, E]

            def wide(m):
                return m.unsqueeze(2).to_broadcast(full)

            @block.tensor
            def _(pe):
                for t in range(TILES):
                    ins = pe.matmul(k.ps[0][:, t * E:(t + 1) * E], k.xT[:, t * P:(t + 1) * P], rw[:, :],
                                    start=True, stop=True)
                ins.then_inc(scored, 1)

            @block.scalar
            def _(act):
                act.wait_ge(own, 2)
                act.activation(probs[:, :, :], probs[:, :, :], ACT.Exp).then_inc(exped, 1)

            @block.vector
            def _(dve):
                chain = Chain(dve, own)
                dve.wait_ge(scored, 1)
                logits = k.ps[0][:, 0:TILES * E].rearrange("p (t e) -> p t e", e=E)
                chain.link(dve.tensor_reduce(best[:, 0, :], logits, AX_X, ALU.max))
                chain.link(dve.tensor_tensor(probs[:, :, :], logits, wide(best[:, 0, :]), ALU.subtract))
                dve.wait_ge(exped, 1)
                chain.link(dve.tensor_reduce(best[:, 0, :], probs[:, :, :], AX_X, ALU.add))
                chain.link(dve.reciprocal(best[:, 0, :], best[:, 0, :]))
                chain.link(dve.tensor_tensor(probs[:, :, :], probs[:, :, :], wide(best[:, 0, :]), ALU.mult))
                first_best(dve, chain, probs[:, :, :], best[:, 1, :], one[:, :, :], tmp[:, :, :], rising[:, :])
                chain.link(dve.scalar_tensor_tensor(probs[:, :, :], one[:, :, :], -4.0, probs[:, :, :], ALU.mult,
                                                    ALU.add))
                first_best(dve, chain, probs[:, :, :], best[:, 2, :], two[:, :, :], tmp[:, :, :], rising[:, :])
                chain.link(dve.tensor_tensor(best[:, 3, :], best[:, 1, :], best[:, 2, :], ALU.add))
                chain.link(dve.tensor_scalar(best[:, 3, :], best[:, 3, :], 1e-6, None, ALU.add))
                chain.link(dve.reciprocal(best[:, 3, :], best[:, 3, :]))
                for m, hit in ((1, one), (2, two)):
                    chain.link(dve.tensor_tensor(best[:, m, :], best[:, m, :], best[:, 3, :], ALU.mult))
                    chain.link(dve.tensor_tensor(tmp[:, :, :], hit[:, :, :], wide(best[:, m, :]), ALU.mult))
                    if m == 1:
                        chain.link(dve.tensor_copy(gate[:, :, :], tmp[:, :, :]))
                    else:
                        chain.link(dve.tensor_tensor(gate[:, :, :], gate[:, :, :], tmp[:, :, :], ALU.add))
                chain.link(dve.tensor_tensor(tmp[:, :, :], one[:, :, :], two[:, :, :], ALU.add))
                chain.link(dve.tensor_scalar(wsel[:, :, :], tmp[:, :, :], 1.0, None, ALU.subtract))
                chain.link(dve.tensor_tensor(wsel[:, :, :], wsel[:, :, :], gate[:, :, :], ALU.add))
                chain.link(dve.memset(counts[:, :, :], 0.0))
                chain.link(dve.memset(total[:, :, :], 0.0))
        with k.loop(E // 2) as i:
            rank_weights(k, 2 * i, wsel, w_col, rank, counts, scr)
            rank_weights(k, 2 * i + 1, wsel, w_col, rank, counts, scr)
        with k.stage("own") as (block, own):
            @block.vector
            def _(dve):
                dve.tensor_scalar(rank[:, :, :], rank[:, :, :], float(CAPACITY), None, ALU.is_lt).then_inc(own, 1)
                dve.wait_ge(own, 1)
                dve.tensor_tensor(gate[:, :, :], gate[:, :, :], rank[:, :, :], ALU.mult).then_inc(own, 1)
        experts(k, E, F, k.xT, {n: dr["L3_ffn_" + n] for n in ("wg", "wu", "wd")}, gate, total, True)
        add_to_x(k, total)


LAYERS = (layer0_attention, layer0_cross, layer0_local, layer1_attention, layer1_cross, layer1_ffn, layer2_delta,
          layer2_cross, layer2_ffn, layer3_scan, layer3_cross, layer3_ffn)


def rotary_halves(n, d, scaled=False):
    half = np.arange(0, d, 2, dtype=np.float32)
    if not scaled:
        theta = np.arange(n, dtype=np.float32)[:, None] / np.power(np.float32(10000.0), half / d)
        cos, sin = np.cos(theta), np.sin(theta)
        return np.stack([np.concatenate([cos, cos], 1), np.concatenate([-sin, sin], 1)])
    inv = (1.0 / np.float32(10000.0) ** (half / np.float32(d))).astype(np.float32)
    t = np.arange(n, dtype=np.float32)
    theta = t[:, None] * inv[None]
    base = (half + 0.4 * d) / (1.4 * d)
    s = base[None] ** ((t - n // 2) / 16)[:, None]
    cos, sin = np.cos(theta), np.sin(theta)
    q = [np.concatenate([cos * s, cos * s], 1), np.concatenate([-sin * s, sin * s], 1)]
    kk = [np.concatenate([cos / s, cos / s], 1), np.concatenate([-sin / s, sin / s], 1)]
    return np.stack(q + kk)


def rotary_pairs(n, d):
    inv = 1.0 / 10000.0 ** (np.arange(0, d, 2, dtype=np.float32) / d)
    ang = np.outer(np.arange(n - 1, dtype=np.float32), inv)
    cos = np.concatenate([np.ones((1, d // 2)), np.cos(ang)])
    sin = np.concatenate([np.zeros((1, d // 2)), np.sin(ang)])
    return np.stack([np.stack([cos, cos], -1).reshape(n, d), np.stack([-sin, sin], -1).reshape(n, d)])


def on_positions(table):
    m, n, d = table.shape
    return np.ascontiguousarray(table.reshape(m, HALVES, P, d).transpose(0, 2, 1, 3).astype(np.float32))


def block_pairs():
    i, j = np.arange(P)[:, None, None], np.arange(P)[None, None, :]
    size = 2 ** np.arange(7)[None, :, None]
    return (i // (2 * size) == j // (2 * size)) & (i // size % 2 == 1) & (j // size % 2 == 0)


def tables():
    pairs = block_pairs()
    return {
        "rising": np.tile(np.arange(8, 0, -1, dtype=np.float32), (P, 1)),
        "earlier": np.tril(np.ones((P, P), np.float32), -1),
        "right_left": pairs.astype(np.float32),
        "left_right": np.ascontiguousarray(pairs.transpose(2, 1, 0)).astype(np.float32),
        "rope8": on_positions(rotary_halves(T, 8)),
        "rope64": on_positions(rotary_halves(T, 64, scaled=True)),
        "ropeP": on_positions(rotary_pairs(T, 64)),
    }


def build(nc, dram, out):
    with ExitStack() as ctx:
        k = Core(nc, ctx, dram)
        constants(k)
        for layer in LAYERS:
            layer(k)
        with k.stage("stored") as (block, stored):
            @block.sync
            def _(sync):
                sync.dma_start(out.rearrange("(t p) d -> p t d", p=P), k.x[:, :, :]).then_inc(stored, 16)
                sync.wait_ge(stored, 16)


TURNED = ("L1_attn_wq", "L1_attn_wk", "L1_attn_wv", "L1_attn_wo", "L1_ffn_W_con", "L2_attn_Wq",
          "L2_attn_Wk", "L2_attn_Wv", "L2_attn_Wfa", "L2_attn_Wfb", "L2_attn_Wb", "L2_attn_Wga", "L2_attn_Wgb",
          "L2_attn_Wo", "L2_xattn_Wq", "L2_xattn_Wk", "L2_xattn_Wv", "L3_attn_in_proj_w", "L3_attn_x_proj_w",
          "L3_attn_dt_proj_w", "L3_attn_out_proj_w", "L3_ffn_router_w")


def kernel(**inputs):
    import numpy as _np
    import concourse.bacc as _bacc
    from concourse import mybir as _mybir
    from concourse.bass_utils import run_bass_kernel_spmd as _run

    nc = _bacc.Bacc("TRN2", target_bir_lowering=False, num_devices=1)
    arrays = {name: _np.asarray(a) for name, a in inputs.items()}
    arrays["x"] = arrays["x"].reshape(TOK, D)
    arrays["ctxT"] = arrays.pop("ctx_1024").reshape(TOK, D).T
    arrays["mask_BxS2_bf1"] = arrays["mask_BxS2_bf1"].reshape(1, TOK).view(_np.uint8)
    for name in TURNED:
        arrays[name] = arrays[name].T
    for name in ("L1_ffn_up_weights", "L1_ffn_down_weights"):
        arrays[name] = arrays[name].reshape(-1)
    arrays["L1_ffn_up_bias"] = arrays["L1_ffn_up_bias"].reshape(-1, P).T
    for name in ("wq", "wk", "wv"):
        arrays[f"L2_attn_{name}_conv"] = arrays[f"L2_attn_{name}_conv"].reshape(-1, 4)
    arrays["L2_attn_dt_bias"] = arrays["L2_attn_dt_bias"].reshape(-1, 1)
    def by_feature(a):
        return a.reshape(a.shape[0], -1, P).transpose(0, 2, 1)

    arrays["L2_ffn_cols"] = _np.concatenate(
        [by_feature(arrays.pop("L2_ffn_" + n)) for n in ("exp_ln_w", "exp_ln_b", "b1")], axis=2)
    arrays["L3_attn_columns"] = _np.concatenate(
        [arrays.pop("L3_attn_" + n).reshape(2 * P, -1) for n in ("conv_w", "conv_b", "norm_w")], axis=1)
    arrays["L3_attn_dt_proj_b"] = arrays["L3_attn_dt_proj_b"].reshape(2, P).T
    arrays["L3_attn_A_log"] = arrays["L3_attn_A_log"].reshape(-1)
    arrays.update(tables())
    arrays = {name: _np.ascontiguousarray(a) for name, a in arrays.items()}
    dram = {name: nc.dram_tensor(f"in_{name}_dram", a.shape, _mybir.dt.from_np(a.dtype), kind="ExternalInput").ap()
            for name, a in arrays.items()}
    out = nc.dram_tensor("out_0_dram", (TOK, D), F32, kind="ExternalOutput").ap()
    build(nc, dram, out)
    r = _run(nc, [{f"in_{name}_dram": a for name, a in arrays.items()}], core_ids=[0])
    return r.results[0]["out_0_dram"].reshape(B, T, D)
```

```python
from contextlib import ExitStack, contextmanager

import numpy as np

import concourse.bass as bass
from concourse import mybir

P = 128
B, T, D = 4, 256, 128
TILES = B * T // P
HALVES = T // P
TOK = B * T
F32 = mybir.dt.float32
BF16 = mybir.dt.bfloat16
U8 = mybir.dt.uint8
U32 = mybir.dt.uint32
ALU = mybir.AluOpType
ACT = mybir.ActivationFunctionType
AX_X = mybir.AxisListType.X
BIG = 1e24
BANK = 512


def after(eng, sem, n):
    if n > 0:
        eng.wait_ge(sem, n)


class Chain:

    def __init__(self, eng, sem):
        self.eng, self.sem, self.n = eng, sem, 0

    def link(self, ins):
        self.n += 1
        ins.then_inc(self.sem, 1)
        self.eng.wait_ge(self.sem, self.n)


class Core:

    POOL = 44

    def __init__(self, nc, ctx, dram):
        self.nc, self.ctx, self.dram = nc, ctx, dram
        self.pools = [[nc.alloc_semaphore(f"pool{p}_{i}") for i in range(self.POOL)] for p in range(2)]
        self.turn = 0
        self.uid = 0
        self.x = self.sbuf(ctx, "x", [P, TILES, D])
        self.xT = self.sbuf(ctx, "xT", [P, TOK])
        self.ctxT = self.sbuf(ctx, "ctxT", [P, TOK])
        self.ident = self.sbuf(ctx, "ident", [P, P])
        self.identb = self.sbuf(ctx, "identb", [P, P], BF16)
        self.causal = self.sbuf(ctx, "causal", [P, HALVES, T], BF16)
        self.band = self.sbuf(ctx, "band", [P, HALVES, T], BF16)
        self.scratch = nc.dram_tensor("scratch", (4, TOK, 1024), F32, kind="Internal").ap()
        self.ps = [ctx.enter_context(nc.psum_tensor(f"bank{i}", [P, BANK], F32)) for i in range(8)]

    def sbuf(self, ctx, name, shape, dt=F32):
        self.uid += 1
        return ctx.enter_context(self.nc.sbuf_tensor(f"{name}_{self.uid}", shape, dt))

    @contextmanager
    def stage(self, *names):
        mine, other = self.pools[self.turn], self.pools[1 - self.turn]
        self.turn = 1 - self.turn
        assert len(names) <= self.POOL
        with self.nc.Block() as block:
            @block.gpsimd
            def _(pool):
                pool.sem_clear(range(other[0].num, other[-1].num + 1))
            yield (block, *mine[:len(names)])

    @contextmanager
    def loop(self, n):
        turn = self.turn
        with self.nc.Fori(0, n) as i:
            yield i
        assert self.turn == turn


def load(sync, sem, loads):
    for dst, src in loads:
        sync.dma_start(dst, src).then_inc(sem, 16)
    after(sync, sem, 16 * len(loads))


def constants(k):
    with k.stage("loaded", "zeroed", "made") as (block, loaded, zeroed, made):
        @block.sync
        def _(sync):
            load(sync, loaded, [
                (k.x[:, :, :], k.dram["x"].rearrange("(t p) d -> p t d", p=P)),
                (k.ctxT[:, :], k.dram["ctxT"]),
            ])

        @block.gpsimd
        def _(pool):
            for m in (k.ident, k.identb):
                pool.memset(m[:, :], 0.0).then_inc(zeroed, 1)
            for m in (k.causal, k.band):
                pool.memset(m[:, :, :], 0.0).then_inc(zeroed, 1)
            pool.wait_ge(zeroed, 4)
            for m in (k.ident, k.identb):
                pool.affine_select(out=m[:, :], in_=m[:, :], compare_op=ALU.not_equal, fill=1.0, base=0,
                                   pattern=[[-1, P]], channel_multiplier=1).then_inc(made, 1)
            for m in (k.causal, k.band):
                pool.affine_select(out=m[:, :, :], in_=m[:, :, :], compare_op=ALU.is_ge, fill=-BIG, base=0,
                                   pattern=[[P, HALVES], [-1, T]], channel_multiplier=1).then_inc(made, 1)
            pool.wait_ge(made, 4)
            pool.affine_select(out=k.band[:, :, :], in_=k.band[:, :, :], compare_op=ALU.is_ge, fill=-BIG,
                               base=32, pattern=[[-P, HALVES], [1, T]], channel_multiplier=-1).then_inc(made, 1)
            pool.wait_ge(made, 5)


def layer_norm(k, src, dst, dstT, eps=1e-5, loads=(), gamma=None, beta=None):
    with ExitStack() as ctx:
        stats = k.sbuf(ctx, "stats", [P, TILES, 6])
        mv = k.sbuf(ctx, "mean_var", [P, TILES, 2])
        std = k.sbuf(ctx, "std", [P, TILES])
        rstd = k.sbuf(ctx, "rstd", [P, TILES])
        with k.stage("loaded", "own", "var", "rooted", "normed", "turned", "copied") as (
                block, loaded, own, var, rooted, normed, turned, copied):
            @block.sync
            def _(sync):
                load(sync, loaded, loads)

            @block.vector
            def _(dve):
                for t in range(TILES):
                    dve.bn_stats(stats[:, t, :], src[:, t, :]).then_inc(own, 1)
                for t in range(TILES):
                    dve.wait_ge(own, t + 1)
                    dve.bn_aggr(mv[:, t, :], stats[:, t, :]).then_inc(own, 1)
                dve.wait_ge(own, 2 * TILES)
                dve.tensor_scalar(std[:, :], mv[:, :, 1], eps, None, ALU.add).then_inc(var, 1)
                dve.wait_ge(rooted, 1)
                dve.reciprocal(rstd[:, :], std[:, :]).then_inc(own, 1)
                dve.wait_ge(own, 2 * TILES + 1)
                if gamma is not None:
                    after(dve, loaded, 16 * len(loads))
                done = 2 * TILES + 1
                for t in range(TILES):
                    ins = dve.tensor_scalar(dst[:, t, :], src[:, t, :], mv[:, t, 0:1], rstd[:, t:t + 1],
                                            ALU.subtract, ALU.mult)
                    if gamma is None:
                        ins.then_inc(normed, 1)
                        continue
                    ins.then_inc(own, 1)
                    dve.wait_ge(own, done + 1)
                    dve.tensor_tensor(dst[:, t, :], dst[:, t, :], gamma, ALU.mult).then_inc(own, 1)
                    dve.wait_ge(own, done + 2)
                    dve.tensor_tensor(dst[:, t, :], dst[:, t, :], beta, ALU.add).then_inc(normed, 1)
                    done += 2

            @block.tensor
            def _(pe):
                for t in range(TILES if dstT is not None else 0):
                    pe.wait_ge(normed, t + 1)
                    pe.transpose(k.ps[t // 4][:, t % 4 * P:(t % 4 + 1) * P], dst[:, t, :],
                                 k.ident[:, :]).then_inc(turned, 1)

            @block.scalar
            def _(act):
                act.wait_ge(var, 1)
                act.activation(std[:, :], std[:, :], ACT.Sqrt).then_inc(rooted, 1)
                for half in range(2 if dstT is not None else 0):
                    act.wait_ge(turned, 4 * half + 4)
                    act.activation(dstT[:, half * 512:(half + 1) * 512], k.ps[half][:, :],
                                   ACT.Copy).then_inc(copied, 1)


def project(k, jobs, loads=()):
    RING = 4
    work = []
    for srcT, w, dst, bias, relu in jobs:
        cols = w.shape[-1]
        for t in range(TILES):
            for c in range(0, cols, BANK):
                work.append((srcT, w, dst, bias, relu, t, c, min(BANK, cols - c)))
    by_act = [w[3] is None and n % 2 == 1 for n, w in enumerate(work)]
    acts = [sum(by_act[:n]) for n in range(len(work) + 1)]
    with k.stage("loaded", "product", "dve_copied", "act_copied") as (block, loaded, product, dve_copied,
                                                                       act_copied):
        @block.sync
        def _(sync):
            load(sync, loaded, loads)

        @block.tensor
        def _(pe):
            for n, (srcT, w, _, _, _, t, c, m) in enumerate(work):
                if n >= RING:
                    after(pe, act_copied if by_act[n - RING] else dve_copied,
                          acts[n - RING + 1] if by_act[n - RING] else n - RING + 1 - acts[n - RING + 1])
                pe.matmul(k.ps[n % RING][:, :m], srcT[:, t * P:(t + 1) * P], w[:, c:c + m],
                          start=True, stop=True).then_inc(product, 1)

        @block.scalar
        def _(act):
            for n, (_, _, dst, _, relu, t, c, m) in enumerate(work):
                if by_act[n]:
                    act.wait_ge(product, n + 1)
                    act.activation(dst[:, t, c:c + m], k.ps[n % RING][:, :m],
                                   ACT.Relu if relu else ACT.Copy).then_inc(act_copied, 1)

        @block.vector
        def _(dve):
            after(dve, loaded, 16 * len(loads))
            for n, (_, _, dst, bias, relu, t, c, m) in enumerate(work):
                if by_act[n]:
                    continue
                dve.wait_ge(product, n + 1)
                if bias is not None:
                    ins = dve.tensor_tensor(dst[:, t, c:c + m], k.ps[n % RING][:, :m], bias[:, c:c + m], ALU.add)
                elif relu:
                    ins = dve.tensor_scalar(dst[:, t, c:c + m], k.ps[n % RING][:, :m], 0.0, None, ALU.max)
                else:
                    ins = dve.tensor_copy(dst[:, t, c:c + m], k.ps[n % RING][:, :m])
                ins.then_inc(dve_copied, 1)


def out_project(k, o, w, y, bias=None, loads=(), regroup=None):
    chunks = o.shape[2] // P
    groups = -(-chunks // 4)
    with ExitStack() as ctx:
        oT = k.sbuf(ctx, "oT", [P, 2, chunks * P])
        with k.stage("loaded", "turned", "copied", "product", "added", "biased",
                     *(f"written_{b}" for b in range(B)), *(f"read_{b}" for b in range(B))) as (
                block, loaded, turned, copied, product, added, biased, *moved):
            written, read = moved[:B], moved[B:]

            @block.sync
            def _(sync):
                load(sync, loaded, loads)
                if regroup is not None:
                    for b in range(B):
                        for dst, src in regroup[0](b):
                            sync.dma_start(dst, src).then_inc(written[b], 16)
                    for b in range(B):
                        sync.wait_ge(written[b], 16 * HALVES)
                        dst, src = regroup[1](b)
                        sync.dma_start(dst, src).then_inc(read[b], 16)

            @block.tensor
            def _(pe):
                for t in range(TILES + 1):
                    if t < TILES:
                        if regroup is not None:
                            pe.wait_ge(read[t // HALVES], 16)
                        for g in range(groups):
                            after(pe, copied, groups * (t - 2) + g + 1)
                            for c in range(4 * g, min(4 * g + 4, chunks)):
                                ins = pe.transpose(k.ps[t % 2 * 2 + g][:, c % 4 * P:(c % 4 + 1) * P],
                                                   o[:, t, c * P:(c + 1) * P], k.ident[:, :])
                            ins.then_inc(turned, 1)
                    if t >= 1:
                        u = t - 1
                        pe.wait_ge(copied, groups * (u + 1))
                        after(pe, added, u - 1)
                        for c in range(chunks):
                            ins = pe.matmul(k.ps[4 + u % 2][:, :D], oT[:, u % 2, c * P:(c + 1) * P], w[:, c, :],
                                            start=(c == 0), stop=(c == chunks - 1))
                        ins.then_inc(product, 1)

            @block.scalar
            def _(act):
                for t in range(TILES):
                    after(act, product, t - 1)
                    for g in range(groups):
                        act.wait_ge(turned, groups * t + g + 1)
                        m = min(4, chunks - 4 * g) * P
                        act.activation(oT[:, t % 2, g * 512:g * 512 + m], k.ps[t % 2 * 2 + g][:, :m],
                                       ACT.Copy).then_inc(copied, 1)

            @block.vector
            def _(dve):
                for t in range(TILES):
                    if bias is not None:
                        dve.tensor_tensor(y[:, t, :], y[:, t, :], bias, ALU.add).then_inc(biased, 1)
                        dve.wait_ge(biased, t + 1)
                    dve.wait_ge(product, t + 1)
                    dve.tensor_tensor(y[:, t, :], y[:, t, :], k.ps[4 + t % 2][:, :D],
                                      ALU.add).then_inc(added, 1)


def attention(k, q, kk, v, o, heads, d, scale, mask=None, causal=False, key_row=None, q_factor=None, k_factor=None,
              first_key=0, prob=None):
    wide = 32 if d < 32 else d
    pack = min(heads, P // wide)
    packs = heads // pack
    group = min(heads, 4 if d == 64 else 16)
    keys = [slice(0, P), slice(first_key, T)] if causal else [slice(0, T), slice(0, T)]
    with ExitStack() as ctx:
        qs = k.sbuf(ctx, "q_packed", [P, 2, HALVES, P])
        ks = k.sbuf(ctx, "k_packed", [P, 2, HALVES, P])
        qkT = k.sbuf(ctx, "qkT", [P, 2, 4 * P])
        prob = k.sbuf(ctx, "prob", [P, 3, HALVES, T]) if prob is None else prob
        probT = k.sbuf(ctx, "probT", [P, 2, HALVES, T])
        peak = k.sbuf(ctx, "peak", [P, 2 * heads, HALVES])
        sums = k.sbuf(ctx, "sums", [P, 2 * heads, HALVES])
        rsum = k.sbuf(ctx, "rsum", [P, 2 * heads, HALVES])

        if wide != d:
            with k.stage("zeroed") as (block, zeroed):
                @block.gpsimd
                def _(pool):
                    pool.memset(qs[:, :, :, :], 0.0).then_inc(zeroed, 1)
                    pool.memset(ks[:, :, :, :], 0.0).then_inc(zeroed, 1)
                    pool.wait_ge(zeroed, 2)

        def two_batches(b2):
            def half_of(i, t):
                return bass.ds(HALVES * (2 * b2 + i // heads) + t, 1)

            with k.stage("packed", "turned", "unpacked", "scored", "peaked", "scaled", "weighed", "p_turned",
                         "p_copied", "mixed", "inverted", "normed") as (
                    block, packed, turned, unpacked, scored, peaked, scaled, weighed, p_turned, p_copied, mixed,
                    inverted, normed):
                @block.gpsimd
                def _(pool):
                    for n in range(2 * packs):
                        after(pool, turned, n - 1)
                        m = n % packs
                        tiles = bass.ds(HALVES * (2 * b2 + n // packs), HALVES)
                        hs = slice(m * pack, (m + 1) * pack)
                        cols = slice(m * pack * d, (m + 1) * pack * d)
                        for dst, src, factor in ((qs, q, None), (ks, kk, k_factor)):
                            out = dst[:, n % 2, :, :].rearrange("p t (s w) -> p t s w", w=wide)[:, :, 0:pack, 0:d]
                            src = src[:, tiles, cols].rearrange("p t (h d) -> p t h d", d=d)
                            if factor is None:
                                pool.tensor_copy(out, src).then_inc(packed, 1)
                            else:
                                pool.tensor_tensor(out, src, factor[:, tiles, hs].unsqueeze(3).to_broadcast(
                                    [P, HALVES, pack, d]), ALU.mult).then_inc(packed, 1)

                @block.tensor
                def _(pe):
                    def turn(n):
                        pe.wait_ge(packed, 2 * (n + 1))
                        after(pe, unpacked, n)
                        for i, src in enumerate((qs, ks)):
                            for t in range(HALVES):
                                ins = pe.transpose(k.ps[0][:, (2 * i + t) * P:(2 * i + t + 1) * P],
                                                   src[:, n % 2, t, :], k.ident[:, :])
                        ins.then_inc(turned, 1)

                    def score(i):
                        n = i // pack
                        pe.wait_ge(unpacked, n + 1)
                        after(pe, weighed, 2 * (i - 2))
                        lo = i % pack * wide
                        bank = k.ps[1 + i % 3]
                        for t in range(HALVES):
                            out = bank[:, t * T:(t + 1) * T][:, keys[t]]
                            ins = pe.matmul(out, qkT[lo:lo + d, n % 2, t * P:(t + 1) * P],
                                            qkT[lo:lo + d, n % 2, 2 * P:4 * P][:, keys[t]],
                                            start=True, stop=(mask is None and key_row is None))
                            if mask is not None:
                                ins = pe.matmul(out, k.identb[:, :], mask[:, t, keys[t]], start=False, stop=True)
                            if key_row is not None:
                                ins = pe.matmul(out, key_row[0][:, :], key_row[1][:, bass.ds((2 * b2 + i // heads) * T, T)],
                                                start=False, stop=True)
                        ins.then_inc(scored, 1)

                    def turn_prob(i):
                        pe.wait_ge(weighed, 2 * (i + 1))
                        after(pe, p_copied, i - 1)
                        for t in range(HALVES):
                            for u in range(keys[t].stop // P):
                                ins = pe.transpose(k.ps[4 + i % 2][:, u * T + t * P:u * T + (t + 1) * P],
                                                   prob[:, i % 3, t, u * P:(u + 1) * P], k.ident[:, :])
                        ins.then_inc(p_turned, 1)

                    def mix(i):
                        pe.wait_ge(p_copied, i + 1)
                        g = i // group
                        if i % group == 0:
                            after(pe, normed, HALVES * (g - 1))
                        for t in range(HALVES):
                            at = (t * group + i % group) * d
                            for u in range(keys[t].stop // P):
                                ins = pe.matmul(k.ps[6 + g % 2][:, at:at + d],
                                                probT[:, i % 2, u, t * P:(t + 1) * P],
                                                v[:, half_of(i, u), i % heads * d:(i % heads + 1) * d]
                                                .rearrange("p a d -> p (a d)"),
                                                start=(u == 0), stop=(u == keys[t].stop // P - 1))
                        ins.then_inc(mixed, 1)

                    turn(0)
                    for i in range(2 * heads + 3):
                        if i < 2 * heads:
                            if i % pack == 0 and i // pack + 1 < 2 * packs:
                                turn(i // pack + 1)
                            score(i)
                        if 2 <= i < 2 * heads + 2:
                            turn_prob(i - 2)
                        if i >= 3:
                            mix(i - 3)

                @block.scalar
                def _(act):
                    def unpack(n):
                        act.wait_ge(turned, n + 1)
                        after(act, scored, (n - 1) * pack)
                        act.activation(qkT[:, n % 2, :], k.ps[0][:, :], ACT.Copy).then_inc(unpacked, 1)

                    unpack(0)
                    for i in range(2 * heads):
                        if i % pack == 0 and i // pack + 1 < 2 * packs:
                            unpack(i // pack + 1)
                        act.wait_ge(scaled, i + 1)
                        after(act, p_turned, i - 2)
                        for t in range(HALVES):
                            by = scale if q_factor is None else q_factor[:, half_of(i, t), i % heads]
                            act.activation(prob[:, i % 3, t, keys[t]], k.ps[1 + i % 3][:, t * T:(t + 1) * T][:, keys[t]],
                                           ACT.Exp, bias=peak[:, i, t:t + 1], scale=by,
                                           accum_out=sums[:, i, t:t + 1]).then_inc(weighed, 1)

                @block.vector
                def _(dve):
                    def copy_prob(i):
                        dve.wait_ge(p_turned, i + 1)
                        after(dve, mixed, i - 1)
                        bank = k.ps[4 + i % 2]
                        if causal:
                            dve.tensor_copy(probT[:, i % 2, 0, :], bank[:, 0:T])
                            dve.tensor_copy(probT[:, i % 2, 1, P:T], bank[:, T + P:2 * T]).then_inc(p_copied, 1)
                        else:
                            dve.tensor_copy(probT[:, i % 2, :, :], bank[:, :].rearrange("p (u t) -> p u t", u=2)
                                            ).then_inc(p_copied, 1)

                    def normalise(g):
                        dve.wait_ge(mixed, (g + 1) * group)
                        dve.wait_ge(weighed, 2 * (g + 1) * group)
                        hs = slice(g * group, (g + 1) * group)
                        dve.reciprocal(rsum[:, hs, :], sums[:, hs, :]).then_inc(inverted, 1)
                        dve.wait_ge(inverted, g + 1)
                        for t in range(HALVES):
                            at = g * group % heads * d
                            out = o[:, half_of(g * group, t), at:at + group * d]
                            dve.tensor_tensor(
                                out.rearrange("p a (h d) -> p (a h) d", d=d),
                                k.ps[6 + g % 2][:, t * group * d:(t + 1) * group * d].rearrange(
                                    "p (h d) -> p h d", d=d),
                                rsum[:, hs, t:t + 1].to_broadcast([P, group, d]), ALU.mult).then_inc(normed, 1)

                    def find_peak(i):
                        dve.wait_ge(scored, i + 1)
                        bank = k.ps[1 + i % 3]
                        if causal:
                            for t in range(HALVES):
                                dve.tensor_reduce(peak[:, i, t:t + 1], bank[:, t * T:(t + 1) * T][:, keys[t]], AX_X,
                                                  ALU.max, negate=True).then_inc(peaked, 1)
                        else:
                            dve.tensor_reduce(peak[:, i, :], bank[:, :].rearrange("p (t k) -> p t k", k=T),
                                              AX_X, ALU.max, negate=True).then_inc(peaked, 2)
                        dve.wait_ge(peaked, 2 * (i + 1))
                        if q_factor is None:
                            dve.tensor_scalar(peak[:, i, :], peak[:, i, :], scale, None, ALU.mult).then_inc(scaled, 1)
                        else:
                            dve.tensor_tensor(peak[:, i, :], peak[:, i, :], q_factor[:, bass.ds(HALVES * (2 * b2 + i // heads), HALVES), i % heads],
                                              ALU.mult).then_inc(scaled, 1)

                    for i in range(2 * heads + 3):
                        if i < 2 * heads:
                            find_peak(i)
                        if 2 <= i < 2 * heads + 2:
                            copy_prob(i - 2)
                        if i > 3 and (i - 3) % group == 0:
                            normalise((i - 3) // group - 1)
                    normalise(2 * heads // group - 1)

        with k.loop(B // 2) as b2:
            two_batches(b2)
            with k.stage() as (block,):
                pass


def rope_split(jobs):
    work = [(b, j) for b in range(B) for j in range(len(jobs))]
    mine = [n % 8 not in (1, 4, 6) for n in range(len(work))]
    return [w for w, m in zip(work, mine) if m], [w for w, m in zip(work, mine) if not m]


def rotate_batches(eng, sem, jobs, mine, tmps, swaps, arrived=None, per_batch=0):
    done = 0
    for b, j in mine:
        qk, cos, sin = jobs[j]
        heads, d = qk.shape[2], qk.shape[3]
        at = slice(HALVES * b, HALVES * (b + 1))
        a, c = (m[:, 0:HALVES * heads * d].rearrange("p (t h d) -> p t h d", t=HALVES, h=heads) for m in tmps)
        if arrived is not None:
            eng.wait_ge(arrived[b], per_batch)
        eng.tensor_tensor(a, qk[:, at], cos.unsqueeze(2).to_broadcast([P, HALVES, heads, d]),
                          ALU.mult).then_inc(sem, 1)
        for to, fro in swaps:
            eng.tensor_tensor(c[:, :, :, to], qk[:, at, :, fro],
                              sin[:, :, to].unsqueeze(2).to_broadcast([P, HALVES, heads, d // 2]),
                              ALU.mult).then_inc(sem, 1)
        eng.wait_ge(sem, done + 3)
        eng.tensor_tensor(qk[:, at], a, c, ALU.add).then_inc(sem, 1)
        done += 4
        eng.wait_ge(sem, done)


def rope(k, jobs, tmp, swaps):
    by_dve, by_pool = rope_split(jobs)
    with k.stage("dve_own", "pool_own") as (block, dve_own, pool_own):
        @block.vector
        def _(dve):
            rotate_batches(dve, dve_own, jobs, by_dve, tmp[0:2], swaps)

        @block.gpsimd
        def _(pool):
            rotate_batches(pool, pool_own, jobs, by_pool, tmp[2:4], swaps)


def layer0_attention(k):
    H, d = 16, 8
    dr = k.dram
    with ExitStack() as ctx:
        w = k.sbuf(ctx, "w_qkv", [P, 3 * D])
        wo = k.sbuf(ctx, "w_out", [P, 1, D])
        cos = k.sbuf(ctx, "cos", [P, HALVES, d])
        sin = k.sbuf(ctx, "sin", [P, HALVES, d])
        qkv = k.sbuf(ctx, "qkv", [P, TILES, 3 * D])
        o = k.sbuf(ctx, "o", [P, TILES, D])
        tmp = [k.sbuf(ctx, "rope_tmp", [P, HALVES * 2 * D]) for _ in range(4)]
        xn = k.sbuf(ctx, "xn", [P, TILES, D])
        layer_norm(k, k.x, xn, k.xT, loads=[
            (w[:, :], dr["L0_attn_w_qkv"]), (wo[:, 0, :], dr["L0_attn_w_out"]),
            (cos[:, :, :], dr["rope8"][0]), (sin[:, :, :], dr["rope8"][1])])
        project(k, [(k.xT, w, qkv, None, False)])
        qk = qkv[:, :, 0:2 * D].rearrange("p t (h d) -> p t h d", d=d)
        lo, hi = slice(0, d // 2), slice(d // 2, d)
        rope(k, [(qk, cos[:, :, :], sin[:, :, :])], tmp, [(lo, hi), (hi, lo)])
        attention(k, qkv, qkv[:, :, D:2 * D], qkv[:, :, 2 * D:3 * D], o, H, d, d ** -0.5, mask=k.causal,
                  causal=True)
        out_project(k, o, wo, k.x)


def layer0_cross(k):
    dr = k.dram
    with ExitStack() as ctx:
        w = {n: k.sbuf(ctx, n, [P, D]) for n in ("Wq", "Wk", "Wv")}
        bias = {n: k.sbuf(ctx, n, [P, D]) for n in ("bq", "bk", "bv", "bo")}
        wo = k.sbuf(ctx, "wo", [P, 1, D])
        xn, q, kk, v, o = (k.sbuf(ctx, n, [P, TILES, D]) for n in ("xn", "q", "k", "v", "o"))
        layer_norm(k, k.x, xn, k.xT, loads=[(w[n][:, :], dr["L0_xattn_" + n]) for n in w]
                   + [(bias[n][:, :], dr["L0_xattn_" + n].partition_broadcast(P)) for n in bias]
                   + [(wo[:, 0, :], dr["L0_xattn_Wo"])])
        project(k, [(k.xT, w["Wq"], q, bias["bq"], False), (k.ctxT, w["Wk"], kk, bias["bk"], False),
                    (k.ctxT, w["Wv"], v, bias["bv"], False)])
        attention(k, q, kk, v, o, 1, D, D ** -0.5)
        out_project(k, o, wo, k.x, bias["bo"][:, :])


def turn_shifted(k, y, yT, loads):
    with k.stage("loaded", "turned", "copied") as (block, loaded, turned, copied):
        @block.sync
        def _(sync):
            load(sync, loaded, loads)

        @block.tensor
        def _(pe):
            for t in range(TILES):
                pe.transpose(k.ps[t // 4][:, t % 4 * P:(t % 4 + 1) * P], y[:, t, :],
                             k.ident[:, :]).then_inc(turned, 1)

        @block.scalar
        def _(act):
            for n in range(2):
                act.wait_ge(turned, 4 * n + 4)
                act.activation(yT[0:64, n * BANK:(n + 1) * BANK], k.ps[n][0:64, :], ACT.Copy).then_inc(copied, 1)
                act.activation(yT[64:P, n * BANK:(n + 1) * BANK].rearrange("p (b t) -> p b t", t=T)[:, :, 1:T],
                               k.ps[n][64:P, :].rearrange("p (b t) -> p b t", t=T)[:, :, 0:T - 1],
                               ACT.Copy).then_inc(copied, 1)
                act.activation(yT[64:P, n * BANK:(n + 1) * BANK].rearrange("p (b t) -> p b t", t=T)[:, :, 0],
                               k.ident[64:P, 0:2], ACT.Copy).then_inc(copied, 1)


def shift_tokens(k, y, ys, loads):
    with k.stage("loaded", "copied") as (block, loaded, copied):
        @block.sync
        def _(sync):
            load(sync, loaded, [
                (ys[1:P, :, 64:D], y[0:P - 1, :, 64:D]),
                (ys[0:1, 1:TILES:2, 64:D], y[P - 1:P, 0:TILES:2, 64:D])] + loads)

        @block.gpsimd
        def _(pool):
            pool.memset(ys[0:1, 0:TILES:2, 64:D], 0.0).then_inc(copied, 1)

        @block.vector
        def _(dve):
            dve.tensor_copy(ys[:, :, 0:64], y[:, :, 0:64]).then_inc(copied, 1)


def project_rotated(k, w, qkv, d, sq, tmp, norms, stab, tabs, swaps, scale, loads):
    RING = 8
    chunks = w.shape[-1] // BANK
    heads = w.shape[-1] // 3 // d
    with k.stage("product", "copied", "squared", "summed", "rooted", "own", "scaled", "dve_own", "pool_own",
                 "dve_rotated", "pool_rotated", "loaded") as (
            block, product, copied, squared, summed, rooted, own, scaled, dve_own, pool_own, dve_rotated,
            pool_rotated, loaded):
        @block.sync
        def _(sync):
            load(sync, loaded, loads)

        qk = qkv[:, :, 0:2 * heads * d].rearrange("p t (h d) -> p t h d", d=d)
        CUT = 19
        tmp = tmp.rearrange("p (h d) -> p h d", d=d)
        tmp = [tmp[:, 0:CUT], tmp[:, CUT:2 * CUT], tmp[:, 2 * CUT:CUT + 2 * heads],
               tmp[:, CUT + 2 * heads:4 * heads]]

        @block.tensor
        def _(pe):
            for n in range(TILES * chunks):
                t, c = n // chunks, n % chunks
                after(pe, copied, n - RING + 1)
                pe.matmul(k.ps[n % RING][:, :], k.xT[:, t * P:(t + 1) * P], w[:, c * BANK:(c + 1) * BANK],
                          start=True, stop=True).then_inc(product, 1)

        @block.scalar
        def _(act):
            for t in range(TILES):
                for c in range(chunks):
                    act.wait_ge(product, t * chunks + c + 1)
                    act.activation(qkv[:, t, c * BANK:(c + 1) * BANK], k.ps[(t * chunks + c) % RING][:, :],
                                   ACT.Copy).then_inc(copied, 1)
                after(act, summed, t - 1)
                act.wait_ge(copied, (t + 1) * chunks)
                act.activation(sq[:, t % 2, :, :], qk[:, t, :, :], ACT.Square).then_inc(squared, 1)
            act.wait_ge(summed, TILES)
            act.activation(norms[:, :, :], norms[:, :, :], ACT.Sqrt).then_inc(rooted, 1)

        def rotate(eng, sem, rotated, done, t, lo, hi, a, c):
            parts = [(m, max(lo, m * heads), min(hi, (m + 1) * heads)) for m in range(2)]
            parts = [p for p in parts if p[1] < p[2]]
            for m, x, y in parts:
                n = y - x
                eng.tensor_tensor(a[:, x - lo:y - lo, :], qk[:, t, x:y, :],
                                  stab[:, 2 * m, t % 2:t % 2 + 1, :].to_broadcast([P, n, d]), ALU.mult).then_inc(sem, 1)
                for to, fro in swaps:
                    eng.tensor_tensor(c[:, x - lo:y - lo, to], qk[:, t, x:y, fro],
                                      stab[:, 2 * m + 1, t % 2:t % 2 + 1, to].to_broadcast([P, n, d // 2]),
                                      ALU.mult).then_inc(sem, 1)
                done += 3
            eng.wait_ge(sem, done)
            eng.tensor_tensor(qk[:, t, lo:hi, :], a[:, 0:hi - lo, :], c[:, 0:hi - lo, :], ALU.add).then_inc(rotated, 1)
            return done

        @block.gpsimd
        def _(pool):
            for dst, src, by in tabs:
                pool.tensor_tensor(dst, src, by.unsqueeze(1).to_broadcast(list(src.shape)),
                                   ALU.mult).then_inc(scaled, 1)
            pool.wait_ge(scaled, len(tabs))
            done = 0
            for t in range(TILES):
                pool.wait_ge(squared, t + 1)
                after(pool, pool_rotated, t)
                done = rotate(pool, pool_own, pool_rotated, done, t, CUT, 2 * heads, *tmp[2:4])

        @block.vector
        def _(dve):
            dve.wait_ge(scaled, len(tabs))
            done = 0
            for t in range(TILES):
                dve.wait_ge(squared, t + 1)
                dve.tensor_reduce(norms[:, t, :], sq[:, t % 2, :, :], AX_X, ALU.add).then_inc(summed, 1)
                after(dve, dve_rotated, t)
                done = rotate(dve, dve_own, dve_rotated, done, t, 0, CUT, *tmp[0:2])
            dve.wait_ge(rooted, 1)
            dve.tensor_scalar(norms[:, :, :], norms[:, :, :], 1e-12, None, ALU.max).then_inc(own, 1)
            dve.wait_ge(own, 1)
            dve.reciprocal(norms[:, :, :], norms[:, :, :]).then_inc(own, 1)
            dve.wait_ge(own, 2)
            dve.tensor_scalar(norms[:, :, 0:heads], norms[:, :, 0:heads], scale, None, ALU.mult).then_inc(own, 1)


def glu_ffn(k, y, w1, b1, w2, b2, inner):
    chunks = [(c, min(P, inner - c)) for c in range(0, inner, P)]
    steps = [(c, n) for c in range(len(chunks)) for n in range(2)]
    with ExitStack() as ctx:
        hT = k.sbuf(ctx, "hT", [P, len(chunks), TOK])
        gate = k.sbuf(ctx, "gate", [P, 2, BANK])
        with k.stage("gated", "gelued", "upped", "hidden", "product", "biased", "added") as (
                block, gated, gelued, upped, hidden, product, biased, added):
            @block.tensor
            def _(pe):
                for s, (c, n) in enumerate(steps):
                    at, m = chunks[c]
                    cols = slice(n * BANK, (n + 1) * BANK)
                    after(pe, gelued, s - 1)
                    pe.matmul(k.ps[s % 2][:m, :], w1[:, inner + at:inner + at + m], k.xT[:, cols],
                              start=True, stop=True).then_inc(gated, 1)
                    after(pe, hidden, s - 1)
                    pe.matmul(k.ps[2 + s % 2][:m, :], w1[:, at:at + m], k.xT[:, cols],
                              start=True, stop=True).then_inc(upped, 1)
                pe.wait_ge(hidden, len(steps))
                for t in range(TILES):
                    after(pe, added, t - 1)
                    for c, (at, m) in enumerate(chunks):
                        ins = pe.matmul(k.ps[4 + t % 2][:, :D], hT[:m, c, t * P:(t + 1) * P], w2[:m, c, :],
                                        start=(c == 0), stop=(c == len(chunks) - 1))
                    ins.then_inc(product, 1)

            @block.scalar
            def _(act):
                for s, (c, n) in enumerate(steps):
                    m = chunks[c][1]
                    act.wait_ge(gated, s + 1)
                    after(act, hidden, s - 1)
                    act.activation(gate[:m, s % 2, :], k.ps[s % 2][:m, :], ACT.Gelu,
                                   bias=b1[:m, 1, c:c + 1]).then_inc(gelued, 1)

            @block.vector
            def _(dve):
                for s, (c, n) in enumerate(steps):
                    m = chunks[c][1]
                    dve.wait_ge(gelued, s + 1)
                    dve.wait_ge(upped, s + 1)
                    dve.scalar_tensor_tensor(hT[:m, c, n * BANK:(n + 1) * BANK], k.ps[2 + s % 2][:m, :],
                                             b1[:m, 0, c:c + 1], gate[:m, s % 2, :], ALU.add,
                                             ALU.mult).then_inc(hidden, 1)
                for t in range(TILES):
                    dve.tensor_tensor(y[:, t, :], y[:, t, :], b2[:, :], ALU.add).then_inc(biased, 1)
                    dve.wait_ge(biased, t + 1)
                    dve.wait_ge(product, t + 1)
                    dve.tensor_tensor(y[:, t, :], y[:, t, :], k.ps[4 + t % 2][:, :D], ALU.add).then_inc(added, 1)


def add_to_x(k, y):
    with k.stage("added") as (block, added):
        @block.vector
        def _(dve):
            dve.tensor_tensor(k.x[:, :, :], k.x[:, :, :], y[:, :, :], ALU.add).then_inc(added, 1)


def layer0_local(k):
    DEPTH, H, d, INNER, WINDOW = 6, 16, 64, 341, 32
    dr = k.dram
    with ExitStack() as ctx:
        wqkv = k.sbuf(ctx, "wqkv", [P, 3 * H * d])
        wo = k.sbuf(ctx, "wo", [P, H * d // P, D])
        w1 = k.sbuf(ctx, "w1", [P, 2 * INNER])
        w2 = k.sbuf(ctx, "w2", [P, 3, D])
        b1 = k.sbuf(ctx, "b1", [P, 2, 3])
        b2 = k.sbuf(ctx, "b2", [P, D])
        g, beta = (k.sbuf(ctx, n, [P, D]) for n in ("ln_g", "ln_b"))
        tab = k.sbuf(ctx, "rotary", [P, 4, HALVES, d])
        stab = k.sbuf(ctx, "rotary_scaled", [P, 4, HALVES, d])
        scales = k.sbuf(ctx, "qk_scales", [P, 2, d])
        rnorm = k.sbuf(ctx, "rnorm", [P, TILES, 2 * H])
        y = k.sbuf(ctx, "y", [P, TILES, D])
        prob = k.sbuf(ctx, "prob", [P, 3, HALVES, T])
        layer_norm(k, k.x, y, None, loads=[(tab[:, :, :, :], dr["rope64"].rearrange("m p t d -> p m t d")),
                                           (wqkv[:, :], dr["L0_ffn_Wqkv"][0])])
        with k.stage("zeroed") as (block, zeroed):
            @block.gpsimd
            def _(pool):
                pool.memset(prob[:, :, 1, 0:P - WINDOW], 0.0).then_inc(zeroed, 1)
        lo, hi = slice(0, d // 2), slice(d // 2, d)
        with k.loop(DEPTH) as i:
            def of(name, depth=i):
                a = dr["L0_ffn_" + name][bass.ds(depth, 1)]
                return a.rearrange("i a b -> (i a) b") if len(a.shape) == 3 else a.rearrange("i a -> (i a)")

            with ExitStack() as inner:
                qkv = k.sbuf(inner, "qkv", [P, TILES, 3 * H * d])
                o = k.sbuf(inner, "o", [P, TILES, H * d])
                w2_i, b1_i = of("W2"), of("b1")
                full = INNER // P
                turn_shifted(k, y, k.xT, [(scales[:, n, :], of(name).partition_broadcast(P))
                                          for n, name in enumerate(("q_scale", "k_scale"))])
                tabs = []
                for n in range(2):
                    tabs += [(stab[:, 2 * n, :, :], tab[:, 2 * n, :, :], scales[:, n, :]),
                             (stab[:, 2 * n + 1, :, lo], tab[:, 2 * n + 1, :, lo], scales[:, n, hi]),
                             (stab[:, 2 * n + 1, :, hi], tab[:, 2 * n + 1, :, hi], scales[:, n, lo])]
                flat = o[:, :, :].rearrange("p t n -> p (t n)")
                sq = flat[:, 0:2 * 2 * H * d].rearrange("p (a h d) -> p a h d", a=2, d=d)
                project_rotated(
                    k, wqkv, qkv, d, sq, flat[:, 4 * H * d:], rnorm, stab, tabs, [(lo, hi), (hi, lo)], 8.0,
                    [(wo[:, :, :], of("Wo").rearrange("(c p) n -> p c n", p=P)), (w1[:, :], of("W1")),
                     (w2[:, 0:full, :], w2_i[0:full * P, :].rearrange("(c p) n -> p c n", p=P)),
                     (w2[0:INNER - full * P, full, :], w2_i[full * P:INNER, :]),
                     (b2[:, :], of("b2").partition_broadcast(P)), (g[:, :], of("ln_g").partition_broadcast(P)),
                     (beta[:, :], of("ln_b").partition_broadcast(P))]
                    + [(b1[0:m, n, c:c + 1],
                        b1_i[n * INNER + c * P:n * INNER + c * P + m].rearrange("(p a) -> p a", a=1))
                       for n in range(2) for c, m in ((0, P), (1, P), (2, INNER - 2 * P))])
                HD = H * d
                attention(k, qkv, qkv[:, :, HD:2 * HD], qkv[:, :, 2 * HD:3 * HD], o, H, d, 8.0, mask=k.band,
                          causal=True, q_factor=rnorm[:, :, 0:H], k_factor=rnorm[:, :, H:2 * H],
                          first_key=P - WINDOW, prob=prob)
                out_project(k, o, wo, y, loads=[(wqkv[:, :], of("Wqkv", i + 1))])
            with ExitStack() as inner:
                ys = k.sbuf(inner, "y_shifted", [P, TILES, D])
                shift_tokens(k, y, ys, [])
                layer_norm(k, ys, ys, k.xT, gamma=g[:, :], beta=beta[:, :])
                glu_ffn(k, y, w1, b1, w2, b2, INNER)
        add_to_x(k, y)


def project_regrouped(k, w, qkv, written_to, read_from, jobs, tmp, swaps):
    RING = 8
    chunks = w.shape[-1] // BANK
    by_dve, by_pool = rope_split(jobs)
    with k.stage("product", "copied", "dve_own", "pool_own", *(f"written_{b}" for b in range(B)),
                 *(f"read_{b}" for b in range(B))) as (block, product, copied, dve_own, pool_own, *moved):
        written, read = moved[:B], moved[B:]
        reads = 16 * len(read_from(0))

        @block.tensor
        def _(pe):
            for n in range(TILES * chunks):
                t, c = n // chunks, n % chunks
                after(pe, copied, n - RING + 1)
                pe.matmul(k.ps[n % RING][:, :], k.xT[:, t * P:(t + 1) * P], w[:, c * BANK:(c + 1) * BANK],
                          start=True, stop=True).then_inc(product, 1)

        @block.scalar
        def _(act):
            for n in range(TILES * chunks):
                t, c = n // chunks, n % chunks
                act.wait_ge(product, n + 1)
                act.activation(qkv[:, t, c * BANK:(c + 1) * BANK], k.ps[n % RING][:, :], ACT.Copy).then_inc(copied, 1)

        @block.sync
        def _(sync):
            for b in range(B + 1):
                if b < B:
                    for t in range(HALVES * b, HALVES * (b + 1)):
                        sync.wait_ge(copied, (t + 1) * chunks)
                        dst, src = written_to(t)
                        sync.dma_start(dst, src).then_inc(written[b], 16)
                if b >= 1:
                    sync.wait_ge(written[b - 1], 16 * HALVES)
                    for dst, src in read_from(b - 1):
                        sync.dma_start(dst, src).then_inc(read[b - 1], 16)
            for b in range(B):
                sync.wait_ge(read[b], reads)

        @block.vector
        def _(dve):
            rotate_batches(dve, dve_own, jobs, by_dve, tmp[0:2], swaps, read, reads)

        @block.gpsimd
        def _(pool):
            rotate_batches(pool, pool_own, jobs, by_pool, tmp[2:4], swaps, read, reads)


def layer1_attention(k):
    H, d = 16, 64
    HD = H * d
    dr = k.dram
    with ExitStack() as ctx:
        w = k.sbuf(ctx, "wqkv", [P, 3 * HD])
        wo = k.sbuf(ctx, "wo", [P, HD // P, D])
        rot = k.sbuf(ctx, "rotary", [P, 2, HALVES, d])
        qkv = k.sbuf(ctx, "qkv", [P, TILES, 3 * HD])
        o = k.sbuf(ctx, "o", [P, TILES, HD])
        xn = o[:, 0, :].rearrange("p (t d) -> p t d", d=D)
        layer_norm(k, k.x, xn, k.xT, loads=[(w[:, n * HD:(n + 1) * HD], dr["L1_attn_" + name])
                                            for n, name in enumerate(("wq", "wk", "wv"))]
                   + [(wo[:, :, :], dr["L1_attn_wo"].rearrange("(c p) n -> p c n", p=P)),
                      (rot[:, :, :, :], dr["ropeP"].rearrange("m p t d -> p m t d"))])

        def as_heads(m):
            return m.rearrange("(b n) c -> b (n c)", b=B).rearrange("b (h t p d) -> b t p h d", h=H, t=HALVES, p=P)

        def parts(sb, m, b):
            return [(sb[:, HALVES * b + t, :].rearrange("p (h d) -> p h d", d=d), as_heads(m)[b, t])
                    for t in range(HALVES)]

        flat = o[:, :, :].rearrange("p t n -> p (t n)")
        even, odd = slice(0, d, 2), slice(1, d, 2)
        project_regrouped(
            k, w, qkv,
            lambda t: (k.scratch[0:3, t * P:(t + 1) * P, :].rearrange("n p c -> p n c"),
                       qkv[:, t, :].rearrange("p (n c) -> p n c", n=3)),
            lambda b: [part for n in range(3) for part in parts(qkv[:, :, n * HD:(n + 1) * HD], k.scratch[n], b)],
            [(qkv[:, :, n * HD:(n + 1) * HD].rearrange("p t (h d) -> p t h d", d=d), rot[:, 0, :, :],
              rot[:, 1, :, :]) for n in range(2)],
            [flat[:, n * 2048:(n + 1) * 2048] for n in range(4)], [(even, odd), (odd, even)])
        attention(k, qkv, qkv[:, :, HD:2 * HD], qkv[:, :, 2 * HD:3 * HD], o, H, d, d ** -0.5)
        back = k.scratch[3].rearrange("(t p) c -> p t c", p=P)
        out_project(k, o, wo, k.x, regroup=(
            lambda b: [(dst, src) for src, dst in parts(o, k.scratch[3], b)],
            lambda b: (o[:, HALVES * b:HALVES * (b + 1), :], back[:, HALVES * b:HALVES * (b + 1), :])))


def layer1_cross(k):
    H, d = 16, 64
    HD = H * d
    dr = k.dram
    with ExitStack() as ctx:
        w = {n: k.sbuf(ctx, n, [P, HD]) for n in ("Wq", "Wk", "Wv")}
        wo = k.sbuf(ctx, "wo", [P, HD // P, D])
        bo = k.sbuf(ctx, "bo", [P, D])
        valid = k.sbuf(ctx, "valid", [1, TOK], U8)
        row = k.sbuf(ctx, "mask_row", [1, TOK], BF16)
        ones = k.sbuf(ctx, "ones", [1, P], BF16)
        qkv = k.sbuf(ctx, "qkv", [P, TILES, 3 * HD])
        o = k.sbuf(ctx, "o", [P, TILES, HD])
        xn = o[:, 0, :].rearrange("p (t d) -> p t d", d=D)
        layer_norm(k, k.x, xn, k.xT, loads=[(w[n][:, :], dr["L1_xattn_" + n]) for n in w] + [
            (wo[:, :, :], dr["L1_xattn_Wo"].rearrange("(c p) n -> p c n", p=P)),
            (bo[:, :], dr["L1_xattn_bo"].partition_broadcast(P)), (valid[:, :], dr["mask_BxS2_bf1"])])
        q, kk, v = (qkv[:, :, n * HD:(n + 1) * HD] for n in range(3))
        project(k, [(k.xT, w["Wq"], q, None, False), (k.ctxT, w["Wk"], kk, None, False),
                    (k.ctxT, w["Wv"], v, None, False)])
        with k.stage("made") as (block, made):
            @block.vector
            def _(dve):
                dve.memset(ones[:, :], 1.0).then_inc(made, 1)
                dve.tensor_scalar(row[:, :], valid[:, :], 1.0, 3.38e38, ALU.subtract, ALU.mult).then_inc(made, 1)
                dve.wait_ge(made, 2)
        attention(k, q, kk, v, o, H, d, d ** -0.5, key_row=(ones, row))
        out_project(k, o, wo, k.x, bo[:, :])


def butterfly_step(eng, sem, done, y, w, tmp, stage, turned):
    s = 2 ** stage
    groups, hidden = y.shape[1], y.shape[2]
    nb = hidden // (2 * s)
    yr = y.rearrange("p g (n a s) -> p g n a s", a=2, s=s)
    a, b = yr[:, :, :, 0, :], yr[:, :, :, 1, :]
    t = [m.rearrange("p g (n s) -> p g n s", s=s) for m in tmp]

    def by(i, j):
        m = w[:, :, j, i] if turned else w[:, :, i, j]
        return m.rearrange("p (n s) -> p n s", s=s).unsqueeze(1).to_broadcast([P, groups, nb, s])

    eng.tensor_tensor(t[0], a, by(0, 0), ALU.mult).then_inc(sem, 1)
    eng.tensor_tensor(t[1], b, by(0, 1), ALU.mult).then_inc(sem, 1)
    eng.tensor_tensor(t[2], a, by(1, 0), ALU.mult).then_inc(sem, 1)
    eng.tensor_tensor(t[3], b, by(1, 1), ALU.mult).then_inc(sem, 1)
    eng.wait_ge(sem, done + 4)
    eng.tensor_tensor(a, t[0], t[1], ALU.add).then_inc(sem, 1)
    eng.tensor_tensor(b, t[2], t[3], ALU.add).then_inc(sem, 1)
    eng.wait_ge(sem, done + 6)
    return done + 6


def layer1_ffn(k):
    HID, STAGES = 512, 9
    C = HID // P
    dr = k.dram
    with ExitStack() as ctx:
        up = k.sbuf(ctx, "up", [P, 2, HID])
        down = k.sbuf(ctx, "down", [P, 1, HID])
        wu = k.sbuf(ctx, "up_weights", [P, STAGES, HID // 2, 2, 2])
        wd = k.sbuf(ctx, "down_weights", [P, STAGES, HID // 2, 2, 2])
        tmp = [k.sbuf(ctx, "tmp_up", [P, 2, HID // 2]) for _ in range(4)]
        tmp2 = [k.sbuf(ctx, "tmp_down", [P, 1, HID // 2]) for _ in range(4)]
        up_bias = k.sbuf(ctx, "up_bias", [P, C])
        bias = k.sbuf(ctx, "bias", [P, C])
        bc, bd = (k.sbuf(ctx, n, [P, D]) for n in ("b_con", "down_bias"))
        contract = k.sbuf(ctx, "contract", [P, C, D])
        hT = k.sbuf(ctx, "hT", [P, C, TOK])
        xn = k.sbuf(ctx, "xn", [P, TILES, D])
        layer_norm(k, k.x, xn, k.xT, loads=[
            (up[:, 0, :], dr["L1_ffn_W_exp"]), (up[:, 1, :], dr["L1_ffn_b_exp"].partition_broadcast(P)),
            (down[:, 0, :], dr["L1_ffn_W_con"]),
            (wu[:, :, :, :, :].rearrange("p s n i j -> p (s n i j)"), dr["L1_ffn_up_weights"].partition_broadcast(P)),
            (wd[:, :, :, :, :].rearrange("p s n i j -> p (s n i j)"), dr["L1_ffn_down_weights"].partition_broadcast(P)),
            (up_bias[:, :], dr["L1_ffn_up_bias"]),
            (bc[:, :], dr["L1_ffn_b_con"].partition_broadcast(P)),
            (bd[:, :], dr["L1_ffn_down_bias"].partition_broadcast(P))])
        with k.stage("up_own", "down_own", "turned", "down_turned", "biased", "contracted") as (
                block, up_own, down_own, turned, down_turned, biased, contracted):
            @block.vector
            def _(dve):
                done = 0
                for s in range(STAGES):
                    done = butterfly_step(dve, up_own, done, up[:, :, :], wu[:, s], [m[:, :, :] for m in tmp], s, False)
                dve.wait_ge(turned, 1)
                dve.tensor_tensor(bias[:, :], k.ps[0][:, 0:HID:P], up_bias[:, :], ALU.add).then_inc(biased, 1)
                dve.wait_ge(down_turned, 1)
                dve.tensor_copy(contract[:, :, :], k.ps[1][:, :].rearrange("p (c d) -> p c d", d=D)
                                ).then_inc(contracted, 1)

            @block.gpsimd
            def _(pool):
                done = 0
                for s in reversed(range(STAGES)):
                    done = butterfly_step(pool, down_own, done, down[:, :, :], wd[:, s], [m[:, :, :] for m in tmp2], s,
                                          True)

            @block.tensor
            def _(pe):
                pe.wait_ge(up_own, 6 * STAGES)
                for c in range(C):
                    ins = pe.transpose(k.ps[0][:, c * P:(c + 1) * P], up[:, 1, c * P:(c + 1) * P], k.ident[:, :])
                ins.then_inc(turned, 1)
                pe.wait_ge(down_own, 6 * STAGES)
                for c in range(C):
                    ins = pe.transpose(k.ps[1][:, c * P:(c + 1) * P], down[:, 0, c * P:(c + 1) * P], k.ident[:, :])
                ins.then_inc(down_turned, 1)

        with k.stage("upped", "gelued", "product", "own", "added") as (block, upped, gelued, product, own, added):
            @block.tensor
            def _(pe):
                for s in range(2 * C):
                    c, n = s // 2, s % 2
                    after(pe, gelued, s - 3)
                    pe.matmul(k.ps[s % 4][:, :], up[:, 0, c * P:(c + 1) * P], k.xT[:, n * BANK:(n + 1) * BANK],
                              start=True, stop=True).then_inc(upped, 1)
                pe.wait_ge(gelued, 2 * C)
                for t in range(TILES):
                    after(pe, added, t - 1)
                    for c in range(C):
                        ins = pe.matmul(k.ps[4 + t % 2][:, :D], hT[:, c, t * P:(t + 1) * P], contract[:, c, :],
                                        start=(c == 0), stop=(c == C - 1))
                    ins.then_inc(product, 1)

            @block.scalar
            def _(act):
                for s in range(2 * C):
                    c, n = s // 2, s % 2
                    act.wait_ge(upped, s + 1)
                    act.activation(hT[:, c, n * BANK:(n + 1) * BANK], k.ps[s % 4][:, :], ACT.Gelu,
                                   bias=bias[:, c:c + 1]).then_inc(gelued, 1)

            @block.vector
            def _(dve):
                dve.tensor_tensor(bc[:, :], bc[:, :], bd[:, :], ALU.add).then_inc(own, 1)
                dve.wait_ge(own, 1)
                for t in range(TILES):
                    dve.tensor_tensor(k.x[:, t, :], k.x[:, t, :], bc[:, :], ALU.add).then_inc(own, 1)
                    dve.wait_ge(own, t + 2)
                    dve.wait_ge(product, t + 1)
                    dve.tensor_tensor(k.x[:, t, :], k.x[:, t, :], k.ps[4 + t % 2][:, :D], ALU.add).then_inc(added, 1)


def delta_setup(k, w, low, beta, neg_a, wb, loads_a_log):
    with k.stage("product", "betas", "copied") as (block, product, betas, copied):
        @block.tensor
        def _(pe):
            for m in range(2):
                for n in range(2):
                    pe.matmul(k.ps[2 * m + n][:, :], w[:, m, :], k.xT[:, n * BANK:(n + 1) * BANK],
                              start=True, stop=True).then_inc(product, 1)
            for t in range(TILES):
                ins = pe.matmul(k.ps[4][:, t * 8:(t + 1) * 8], k.xT[:, t * P:(t + 1) * P], wb[:, :],
                                start=True, stop=True)
            ins.then_inc(betas, 1)

        @block.vector
        def _(dve):
            for m in range(2):
                for n in range(2):
                    dve.wait_ge(product, 2 * m + n + 1)
                    dve.tensor_copy(low[:, m, n * BANK:(n + 1) * BANK], k.ps[2 * m + n][:, :]).then_inc(copied, 1)

        @block.scalar
        def _(act):
            act.activation(neg_a[:, 0, :], loads_a_log, ACT.Exp).then_inc(copied, 1)
            act.wait_ge(betas, 1)
            act.activation(beta[:, :, :], k.ps[4][:, 0:TILES * 8].rearrange("p (t h) -> p t h", h=8),
                           ACT.Sigmoid).then_inc(copied, 1)
            act.wait_ge(copied, 6)
            act.activation(neg_a[:, 1, :], neg_a[:, 0, :], ACT.Copy, scale=-1.0).then_inc(copied, 1)


def delta_qkv(k, w, conv, qkv):
    with k.stage("product", "tapped", "added", "silu") as (block, product, tapped, added, silu):
        @block.tensor
        def _(pe):
            for m in range(3):
                for n in range(2):
                    pe.matmul(k.ps[2 * m + n][:, :], w[:, m, :], k.xT[:, n * BANK:(n + 1) * BANK],
                              start=True, stop=True).then_inc(product, 1)

        @block.scalar
        def _(act):
            for m in range(3):
                for n in range(2):
                    act.wait_ge(product, 2 * m + n + 1)
                    act.activation(qkv[:, m, n * BANK:(n + 1) * BANK], k.ps[2 * m + n][:, :], ACT.Copy,
                                   scale=conv[:, m, 3:4]).then_inc(tapped, 1)
            for m in range(3):
                act.wait_ge(added, 6 * (m + 1))
                act.activation(qkv[:, m, :], qkv[:, m, :], ACT.Silu).then_inc(silu, 1)

        @block.vector
        def _(dve):
            done = 0
            for m in range(3):
                for n in range(2):
                    dve.wait_ge(tapped, 2 * m + n + 1)
                    y = qkv[:, m, n * BANK:(n + 1) * BANK].rearrange("p (b t) -> p b t", t=T)
                    x = k.ps[2 * m + n][:, :].rearrange("p (b t) -> p b t", t=T)
                    for back in (1, 2, 3):
                        dve.scalar_tensor_tensor(y[:, :, back:T], x[:, :, 0:T - back], conv[:, m, 3 - back:4 - back],
                                                 y[:, :, back:T], ALU.mult, ALU.add).then_inc(added, 1)
                        done += 1
                        dve.wait_ge(added, done)


def log1p_small(dve, sem, done, e, series, small):
    dve.tensor_scalar(small, e, 1.0 / 64, None, ALU.is_lt).then_inc(sem, 1)
    dve.tensor_scalar(series, e, -0.25, None, ALU.mult).then_inc(sem, 1)
    for n, c in enumerate((1.0 / 3, -0.5, 1.0)):
        dve.wait_ge(sem, done + 2 + n)
        dve.scalar_tensor_tensor(series, series, c, e, ALU.add, ALU.mult).then_inc(sem, 1)
    dve.wait_ge(sem, done + 5)


def delta_gates(k, h, s):
    nq, nk = (s["factors"][:, 0:TILES], s["factors"][:, TILES:2 * TILES])
    with k.stage("squared", "z", "gate", "v_turned", "sums", "absed", "logs", "floored", "own", "rooted",
                 "own_pool", "sig", "q_squared", "same") as (
            block, squared, z, gate, v_turned, sums, absed, logs, floored, own, rooted, own_pool, sig, q_squared,
            same):
        q, kk, v = (s["qkv"][:, m, :] for m in range(3))
        spare = s["kq"].rearrange("p a t m d -> p (a t m d)")
        log, series, small = (spare[:, n * TOK:(n + 1) * TOK] for n in range(3))

        @block.gpsimd
        def _(pool):
            pool.tensor_tensor(s["sq"][:, 0, :], q, q, ALU.mult).then_inc(q_squared, 1)
            pool.memset(s["suffix"][:, :], 0.0).then_inc(own_pool, 1)
            for a in range(2):
                pool.tensor_copy(s["inv"][:, :, a, :], k.ident[:, :].unsqueeze(1).to_broadcast([P, TILES, P])
                                 ).then_inc(own_pool, 1)
            pool.wait_ge(same, 1)
            pool.tensor_tensor(s["att"], k.ident[:, :].unsqueeze(1).to_broadcast([P, TILES, P]),
                               s["qk_same"][:, :].unsqueeze(2).to_broadcast([P, TILES, P]), ALU.mult).then_inc(own_pool, 1)

        @block.tensor
        def _(pe):
            for n in range(2):
                pe.matmul(k.ps[n][:, :], s["w"][:, 3, :], s["low"][:, 0, n * BANK:(n + 1) * BANK],
                          start=True, stop=True).then_inc(z, 1)
            for t in range(TILES):
                cols = slice(t % 4 * P, (t % 4 + 1) * P)
                pe.matmul(k.ps[2 + t // 4][:, cols], s["low"][:, 1, t * P:(t + 1) * P], s["w"][:, 4, :],
                          start=True, stop=True).then_inc(gate, 1)
            for t in range(TILES):
                cols = slice(t % 4 * P, (t % 4 + 1) * P)
                pe.transpose(k.ps[4 + t // 4][:, cols], v[:, t * P:(t + 1) * P], k.ident[:, :]).then_inc(v_turned, 1)
            for m in (1, 2, 0):
                if m == 0:
                    pe.wait_ge(q_squared, 1)
                else:
                    pe.wait_ge(squared, m)
                for t in range(TILES):
                    ins = pe.matmul(k.ps[6][:, m * TILES + t:m * TILES + t + 1], s["sq"][:, m, t * P:(t + 1) * P],
                                    s["ones"][:, :], start=True, stop=True)
            ins.then_inc(sums, 1)

        @block.scalar
        def _(act):
            for n in range(2):
                cols = slice(n * BANK, (n + 1) * BANK)
                act.wait_ge(z, n + 1)
                act.activation(s["decay"][:, cols], k.ps[n][:, :], ACT.Abs, bias=s["dt"][:, 0:1]).then_inc(absed, 1)
            act.wait_ge(absed, 2)
            act.activation(s["decay"][:, :], s["decay"][:, :], ACT.Exp, scale=-1.0).then_inc(absed, 1)
            act.wait_ge(absed, 3)
            act.activation(log, s["decay"][:, :], ACT.Ln, bias=1.0).then_inc(logs, 1)
            act.wait_ge(own, 1)
            act.activation(s["factors"][:, :], s["factors"][:, :], ACT.Sqrt).then_inc(rooted, 1)
            for n in range(2):
                act.wait_ge(gate, 4 * n + 4)
                act.activation(s["gate"][:, 4 * n:4 * n + 4, :], k.ps[2 + n][:, :].rearrange(
                    "p (t d) -> p t d", d=P), ACT.Sigmoid).then_inc(sig, 1)

        @block.vector
        def _(dve):
            dve.tensor_tensor(s["sq"][:, 1, :], kk, kk, ALU.mult).then_inc(squared, 1)
            dve.tensor_tensor(s["sq"][:, 2, :], q, kk, ALU.mult).then_inc(squared, 1)
            for n in range(2):
                cols = slice(n * BANK, (n + 1) * BANK)
                dve.wait_ge(absed, n + 1)
                dve.tensor_scalar(s["prefix"][:, cols], k.ps[n][:, :], s["dt"][:, 0:1], 0.0, ALU.add,
                                  ALU.max).then_inc(floored, 1)
            dve.wait_ge(absed, 3)
            log1p_small(dve, floored, 2, s["decay"][:, :], series, small)
            dve.wait_ge(sums, 1)
            dve.tensor_scalar(s["factors"][:, :], k.ps[6][:, 0:2 * TILES], 1.0 / P, 1e-6, ALU.mult,
                              ALU.add).then_inc(own, 1)
            dve.tensor_copy(s["qk_same"][:, :], k.ps[6][:, 2 * TILES:3 * TILES]).then_inc(same, 1)
            dve.wait_ge(logs, 1)
            dve.copy_predicated(log, small.bitcast(U32), series).then_inc(floored, 1)
            dve.wait_ge(floored, 2 + 5 + 1)
            dve.tensor_tensor(s["prefix"][:, :], s["prefix"][:, :], log, ALU.add).then_inc(own, 1)
            dve.wait_ge(own, 2)
            dve.tensor_scalar(s["prefix"][:, :], s["prefix"][:, :], s["neg_a"][:, 1, bass.ds(h, 1)], None,
                              ALU.mult).then_inc(own, 1)
            dve.wait_ge(rooted, 1)
            dve.reciprocal(s["factors"][:, :], s["factors"][:, :]).then_inc(own, 1)
            dve.wait_ge(own, 4)
            beta = s["beta"][:, :, bass.ds(h, 1)].rearrange("p t a -> p (t a)")
            scale = float(P) ** -0.5
            dve.scalar_tensor_tensor(s["v_factor"][:, :], nk, scale, beta, ALU.mult, ALU.mult).then_inc(own, 1)
            dve.wait_ge(own, 5)
            dve.scalar_tensor_tensor(s["k_factor"][:, :], nk, scale, s["v_factor"][:, :], ALU.mult,
                                     ALU.mult).then_inc(own, 1)
            dve.tensor_scalar(s["q_factor"][:, :], nq, scale * scale, None, ALU.mult).then_inc(own, 1)
            dve.wait_ge(own, 7)
            dve.tensor_scalar(s["minus_k_factor"][:, :], s["k_factor"][:, :], -1.0, None, ALU.mult).then_inc(own, 1)
            for t in range(TILES):
                dve.wait_ge(v_turned, t + 1)
                dve.tensor_scalar(s["vb"][:, t, :], k.ps[4 + t // 4][:, t % 4 * P:(t % 4 + 1) * P],
                                  s["v_factor"][:, t:t + 1], None, ALU.mult).then_inc(own, 1)


def delta_levels(k, s, loads):
    LEVELS = 7
    PAIRS = TILES // 2
    STEPS = LEVELS * PAIRS
    q, kk = s["qkv"][:, 0, :], s["qkv"][:, 1, :]

    def split(m, l):
        return m.rearrange("p (n a s) -> p n a s", a=2, s=2 ** l)

    with k.stage("summed", "own_pool", "decayed", "k_scaled", "q_scaled", "paired", "masked", "folded", "unfolded",
                 "corrected", "updated", "loaded") as (
            block, summed, own_pool, decayed, k_scaled, q_scaled, paired, masked, folded, unfolded, corrected,
            updated, loaded):
        @block.sync
        def _(sync):
            load(sync, loaded, loads)

        @block.gpsimd
        def _(pool):
            for l in range(LEVELS + 1):
                if l > 0:
                    pre, suf = split(s["prefix"], l - 1), split(s["suffix"], l - 1)
                    shape = [P, pre.shape[1], 2 ** (l - 1)]
                    end = 2 ** (l - 1) - 1
                    pool.wait_ge(decayed, 2 * l)
                    pool.tensor_tensor(suf[:, :, 0, :], suf[:, :, 0, :], pre[:, :, 1, end:end + 1].to_broadcast(shape),
                                       ALU.add).then_inc(own_pool, 1)
                    pool.wait_ge(own_pool, 2 * l - 1)
                    pool.tensor_tensor(pre[:, :, 1, :], pre[:, :, 1, :], pre[:, :, 0, end:end + 1].to_broadcast(shape),
                                       ALU.add).then_inc(own_pool, 1)
                    pool.wait_ge(own_pool, 2 * l)
                    pool.sem_inc(summed, 1)
                if l < LEVELS:
                    pool.wait_ge(decayed, 2 * (l + 1))
                    after(pool, paired, PAIRS * (l - 1))
                    pool.tensor_tensor(s["kq"][:, l % 2, :, 0, :], kk.rearrange("p (t d) -> p t d", d=P),
                                       s["scales"][:, l % 2, :].rearrange("p (t d) -> p t d", d=P),
                                       ALU.mult).then_inc(k_scaled, 1)

        @block.scalar
        def _(act):
            def exps(l):
                if l > 0:
                    act.wait_ge(summed, l)
                after(act, k_scaled, l - 1)
                after(act, q_scaled, l - 1)
                out = split(s["scales"][:, l % 2, :], l)
                act.activation(out[:, :, 0, :], split(s["suffix"], l)[:, :, 0, :], ACT.Exp).then_inc(decayed, 1)
                act.activation(out[:, :, 1, :], split(s["prefix"], l)[:, :, 1, :], ACT.Exp).then_inc(decayed, 1)

            exps(0)
            for n in range(STEPS):
                if n % PAIRS == 0 and n // PAIRS + 1 < LEVELS:
                    exps(n // PAIRS + 1)
                act.wait_ge(folded, n + 1)
                after(act, corrected, n - 1)
                act.activation(s["fold"][:, n % 2, :], k.ps[2 + n % 2][:, 0:2 * P], ACT.Copy).then_inc(unfolded, 1)

        @block.tensor
        def _(pe):
            def pair(n):
                l, p = n // PAIRS, n % PAIRS
                if p == 0:
                    pe.wait_ge(k_scaled, l + 1)
                    pe.wait_ge(q_scaled, l + 1)
                after(pe, masked, n - 1)
                for a in range(2):
                    ins = pe.matmul(k.ps[n % 2][:, a * 2 * P:(a + 1) * 2 * P], s["kq"][:, l % 2, 2 * p + a, 0, :],
                                    s["kq"][:, l % 2, 2 * p + a, :, :], start=True, stop=True)
                ins.then_inc(paired, 1)

            def fold(n):
                p = n % PAIRS
                pe.wait_ge(masked, n + 1)
                after(pe, updated, n - PAIRS + 1)
                after(pe, unfolded, n - 1)
                for a in range(2):
                    ins = pe.matmul(k.ps[2 + n % 2][:, a * P:(a + 1) * P], s["lower"][:, 2 * p + a, :],
                                    s["inv"][:, 2 * p + a, 1, :], start=True, stop=True)
                ins.then_inc(folded, 1)

            def correct(n):
                p = n % PAIRS
                pe.wait_ge(unfolded, n + 1)
                after(pe, updated, n - 1)
                for a in range(2):
                    y = s["fold"][:, n % 2, a * P:(a + 1) * P]
                    at = a * 2 * P
                    pe.matmul(k.ps[4 + n % 2][:, at:at + P], y, s["inv"][:, 2 * p + a, 0, :], start=True, stop=True)
                    ins = pe.matmul(k.ps[4 + n % 2][:, at + P:at + 2 * P], s["inv"][:, 2 * p + a, 0, :], y,
                                    start=True, stop=True)
                ins.then_inc(corrected, 1)

            for n in range(STEPS + 2):
                if n < STEPS:
                    pair(n)
                if 1 <= n < STEPS + 1:
                    fold(n - 1)
                if n >= 2:
                    correct(n - 2)

        @block.vector
        def _(dve):
            def scale_q(l):
                dve.wait_ge(decayed, 2 * (l + 1))
                after(dve, paired, PAIRS * (l - 1))
                dve.tensor_tensor(s["kq"][:, l % 2, :, 1, :], q.rearrange("p (t d) -> p t d", d=P),
                                  s["scales"][:, l % 2, :].rearrange("p (t d) -> p t d", d=P),
                                  ALU.mult).then_inc(q_scaled, 1)

            scale_q(0)
            for n in range(STEPS + 2):
                if n < STEPS:
                    l, p = n // PAIRS, n % PAIRS
                    dve.wait_ge(paired, n + 1)
                    after(dve, folded, n - PAIRS + 1)
                    for a in range(2):
                        t = 2 * p + a
                        dve.scalar_tensor_tensor(s["lower"][:, t, :], k.ps[n % 2][:, a * 2 * P:a * 2 * P + P],
                                                 s["k_factor"][:, t:t + 1], s["right_left"][:, l, :], ALU.mult,
                                                 ALU.mult)
                    dve.copy_predicated(s["att"][:, 2 * p:2 * p + 2, :],
                                        s["left_right"].bitcast(U32)[:, l, :].unsqueeze(1).to_broadcast([P, 2, P]),
                                        k.ps[n % 2][:, :].rearrange("p (a m i) -> p a m i", a=2, m=2)[:, :, 1, :]
                                        ).then_inc(masked, 1)
                if n >= 2:
                    m = n - 2
                    p = m % PAIRS
                    dve.wait_ge(corrected, m + 1)
                    inv = s["inv"][:, 2 * p:2 * p + 2, :, :].rearrange("p a m i -> p (a m i)")
                    dve.tensor_tensor(inv, inv, k.ps[4 + m % 2][:, :], ALU.subtract).then_inc(updated, 1)
                if n % PAIRS == 1 and n // PAIRS + 1 < LEVELS and n < STEPS:
                    scale_q(n // PAIRS + 1)


def delta_outputs(k, h, s):
    q, kk = (s["qkv"][:, m, :].rearrange("p (b c t) -> p b c t", c=HALVES, t=P) for m in range(2))
    pre, suf = (s[n].rearrange("p (b c t) -> p b c t", c=HALVES, t=P) for n in ("prefix", "suffix"))
    with k.stage("decayed", "scaled", "k_turned", "k_copied", "u0", "u0_copied", "o0", "state", "state_copied",
                 "read", "w1", "u1", "u1_copied", "o1", "own", "squared", "rooted", "gated") as (
            block, decayed, scaled, k_turned, k_copied, u0, u0_copied, o0, state, state_copied, read, w1, u1,
            u1_copied, o1, own, squared, rooted, gated):
        def bank(i, b):
            return k.ps[i][:, b * P:(b + 1) * P]

        @block.scalar
        def _(act):
            act.activation(s["ends"][:, 0, :, :], suf[:, :, 0, :], ACT.Exp).then_inc(decayed, 1)
            act.activation(s["ends"][:, 1, :, :], pre[:, :, 1, :], ACT.Exp).then_inc(decayed, 1)
            act.wait_ge(u0, 1)
            act.activation(s["u"][:, 0, :, :], k.ps[1][:, :].rearrange("p (b d) -> p b d", d=P),
                           ACT.Copy).then_inc(u0_copied, 1)
            act.wait_ge(state, 1)
            act.activation(s["state"][:, :, :], k.ps[3][:, :].rearrange("p (b d) -> p b d", d=P),
                           ACT.Copy).then_inc(state_copied, 1)
            act.wait_ge(u1, 1)
            act.activation(s["u"][:, 1, :, :], k.ps[5][:, :].rearrange("p (b d) -> p b d", d=P),
                           ACT.Copy).then_inc(u1_copied, 1)
            for b in range(B):
                for c in range(HALVES):
                    act.wait_ge(own, HALVES * b + c + 1)
                    act.activation(s["sq"][:, 0, 0:P], s["o_head"][:, HALVES * b + c, :], ACT.Square,
                                   accum_out=s["o_sums"][:, HALVES * b + c:HALVES * b + c + 1]).then_inc(squared, 1)
                    act.wait_ge(squared, HALVES * b + c + 1)
            act.wait_ge(own, TILES + 1)
            act.activation(s["o_sums"][:, :], s["o_sums"][:, :], ACT.Sqrt).then_inc(rooted, 1)

        @block.gpsimd
        def _(pool):
            pool.wait_ge(decayed, 2)
            pool.tensor_tensor(s["k_end"][:, :, :], kk[:, :, 0, :], s["ends"][:, 0, :, :], ALU.mult).then_inc(scaled, 1)
            pool.tensor_tensor(s["k_start"][:, :, :], kk[:, :, 1, :], s["ends"][:, 1, :, :], ALU.mult).then_inc(scaled, 1)
            pool.tensor_tensor(s["q_start"][:, :, :], q[:, :, 1, :], s["ends"][:, 1, :, :], ALU.mult).then_inc(scaled, 1)
            for t in range(TILES):
                pool.tensor_tensor(s["gate"][:, t, :], s["gate"][:, t, :], s["norm_w"][:, :], ALU.mult).then_inc(gated, 1)

        @block.tensor
        def _(pe):
            for b in range(B):
                ins = pe.matmul(bank(1, b), s["inv"][:, HALVES * b, 1, :], s["vb"][:, HALVES * b, :], start=True, stop=True)
            ins.then_inc(u0, 1)
            pe.wait_ge(scaled, 1)
            for b in range(B):
                ins = pe.transpose(bank(0, b), s["k_end"][:, b, :], k.ident[:, :])
            ins.then_inc(k_turned, 1)
            pe.wait_ge(u0_copied, 1)
            for b in range(B):
                ins = pe.matmul(bank(2, b), s["att"][:, HALVES * b, :], s["u"][:, 0, b, :], start=True, stop=True)
            ins.then_inc(o0, 1)
            pe.wait_ge(k_copied, 1)
            for b in range(B):
                ins = pe.matmul(bank(3, b), s["k_end_tokens"][:, b, :], s["u"][:, 0, b, :], start=True, stop=True)
            ins.then_inc(state, 1)
            pe.wait_ge(state_copied, 1)
            pe.wait_ge(scaled, 3)
            for b in range(B):
                ins = pe.matmul(bank(4, b), s["k_start"][:, b, :], s["state"][:, b, :], start=True, stop=True)
            ins.then_inc(read, 1)
            pe.wait_ge(w1, B)
            for b in range(B):
                ins = pe.matmul(bank(5, b), s["inv"][:, HALVES * b + 1, 1, :], s["vb"][:, HALVES * b + 1, :],
                                start=True, stop=True)
            ins.then_inc(u1, 1)
            pe.wait_ge(u1_copied, 1)
            for b in range(B):
                pe.matmul(bank(6, b), s["q_start"][:, b, :], s["state"][:, b, :], start=True, stop=False)
                ins = pe.matmul(bank(6, b), s["att"][:, HALVES * b + 1, :], s["u"][:, 1, b, :], start=False, stop=True)
            ins.then_inc(o1, 1)

        @block.vector
        def _(dve):
            dve.wait_ge(k_turned, 1)
            dve.tensor_copy(s["k_end_tokens"][:, :, :], k.ps[0][:, :].rearrange("p (b d) -> p b d", d=P)
                            ).then_inc(k_copied, 1)
            dve.wait_ge(read, 1)
            for b in range(B):
                t = HALVES * b + 1
                dve.scalar_tensor_tensor(s["vb"][:, t, :], bank(4, b), s["minus_k_factor"][:, t:t + 1], s["vb"][:, t, :],
                                         ALU.mult, ALU.add).then_inc(w1, 1)
            dve.wait_ge(o1, 1)
            for b in range(B):
                for c in range(HALVES):
                    t = HALVES * b + c
                    dve.tensor_scalar(s["o_head"][:, t, :], bank(2 if c == 0 else 6, b), s["q_factor"][:, t:t + 1], None,
                                      ALU.mult).then_inc(own, 1)
            dve.wait_ge(squared, TILES)
            dve.tensor_scalar(s["o_sums"][:, :], s["o_sums"][:, :], 1.0 / P, 1e-5, ALU.mult, ALU.add).then_inc(own, 1)
            dve.wait_ge(rooted, 1)
            dve.reciprocal(s["o_sums"][:, :], s["o_sums"][:, :]).then_inc(own, 1)
            dve.wait_ge(own, TILES + 2)
            dve.wait_ge(gated, TILES)
            for t in range(TILES):
                dve.scalar_tensor_tensor(s["o"][:, t, bass.ds(h * P, P)], s["o_head"][:, t, :], s["o_sums"][:, t:t + 1],
                                         s["gate"][:, t, :], ALU.mult, ALU.mult)


def layer2_delta(k):
    H = 8
    dr = k.dram
    with ExitStack() as ctx:
        s = {}

        def room(name, shape, dt=F32):
            t = k.sbuf(ctx, name, shape, dt)
            s[name] = t[tuple(slice(None) for _ in shape)]
            return s[name]

        bottleneck = room("bottleneck", [P, 2, P])
        wb = room("wb", [P, H])
        room("beta", [P, TILES, H])
        room("neg_a", [P, 2, H])
        room("a_log", [P, H])
        room("low", [P, 2, TOK])
        room("w", [P, 5, P])
        room("conv", [P, 3, 4])
        room("dt", [P, 1])
        room("norm_w", [P, P])
        room("ones", [P, 1])
        room("right_left", [P, 7, P])
        room("left_right", [P, 7, P])
        room("qkv", [P, 3, TOK])
        room("sq", [P, 3, TOK])
        for name in ("decay", "prefix", "suffix"):
            room(name, [P, TOK])
        for name in ("vb", "att", "gate", "lower", "o_head"):
            room(name, [P, TILES, P])
        room("inv", [P, TILES, 2, P])
        room("factors", [P, 2 * TILES])
        for name in ("v_factor", "k_factor", "q_factor", "minus_k_factor", "qk_same", "o_sums"):
            room(name, [P, TILES])
        room("kq", [P, 2, TILES, 2, P])
        room("scales", [P, 2, TOK])
        room("fold", [P, 2, 2 * P])
        room("ends", [P, 2, B, P])
        for name in ("k_end", "k_start", "q_start", "k_end_tokens", "state"):
            room(name, [P, B, P])
        room("u", [P, 2, B, P])
        room("o", [P, TILES, H * P])
        wo = room("wo", [P, H, D])

        def of_head(h):
            return [(s["w"][:, n, :], dr["L2_attn_" + name][:, bass.ds(h * P, P)])
                    for n, name in enumerate(("Wq", "Wk", "Wv", "Wfb", "Wgb"))] + [
                (s["conv"][:, n, :], dr[f"L2_attn_w{name}_conv"][bass.ds(h * P, P), :]) for n, name in enumerate("qkv")
            ] + [(s["dt"], dr["L2_attn_dt_bias"][bass.ds(h * P, P), :])]

        layer_norm(k, k.x, s["o_head"], k.xT, loads=of_head(0) + [
            (bottleneck[:, 0, :], dr["L2_attn_Wfa"]), (bottleneck[:, 1, :], dr["L2_attn_Wga"]), (wb, dr["L2_attn_Wb"]),
            (s["a_log"], dr["L2_attn_A_log"].partition_broadcast(P)),
            (s["norm_w"], dr["L2_attn_o_norm_w"].partition_broadcast(P)), (s["right_left"], dr["right_left"]),
            (s["left_right"], dr["left_right"]), (wo, dr["L2_attn_Wo"].rearrange("(c p) n -> p c n", p=P))])
        delta_setup(k, bottleneck, s["low"], s["beta"], s["neg_a"], wb, s["a_log"])
        with k.stage("made") as (block, made):
            @block.gpsimd
            def _(pool):
                pool.memset(s["ones"], 1.0).then_inc(made, 1)
        with k.loop(H) as h:
            delta_qkv(k, s["w"], s["conv"], s["qkv"])
            delta_gates(k, h, s)
            delta_levels(k, s, of_head(h + 1))
            delta_outputs(k, h, s)
        out_project(k, s["o"], wo, k.x)


def layer2_cross(k):
    H, d = 16, 8
    dr = k.dram
    with ExitStack() as ctx:
        w = {n: k.sbuf(ctx, n, [P, D]) for n in ("Wq", "Wk", "Wv")}
        xn, q, kk, v, o = (k.sbuf(ctx, n, [P, TILES, D]) for n in ("xn", "q", "k", "v", "o"))
        layer_norm(k, k.x, xn, k.xT, loads=[(w[n][:, :], dr["L2_xattn_" + n]) for n in w])
        project(k, [(k.xT, w["Wq"], q, None, True), (k.ctxT, w["Wk"], kk, None, True),
                    (k.ctxT, w["Wv"], v, None, True)])
        attention(k, q, kk, v, o, H, d, d ** -0.5)
        add_to_x(k, o)


def first_best(dve, own, values, best, hit, tmp, rising):
    shape = list(values.shape)
    own.link(dve.tensor_reduce(best, values, AX_X, ALU.max))
    own.link(dve.tensor_tensor(tmp, values, best.unsqueeze(2).to_broadcast(shape), ALU.is_equal))
    own.link(dve.tensor_tensor(tmp, tmp, rising.unsqueeze(1).to_broadcast(shape), ALU.mult))
    own.link(dve.tensor_reduce(hit[:, :, 0], tmp, AX_X, ALU.max))
    own.link(dve.tensor_copy(best_index := hit[:, :, 1], hit[:, :, 0]))
    own.link(dve.tensor_tensor(tmp, tmp, best_index.unsqueeze(2).to_broadcast(shape), ALU.is_equal))
    own.link(dve.tensor_copy(hit, tmp))


def rank_tile(dve, sem, done, t, compared, w_col, counts):
    at = t * P
    if t > 0:
        dve.tensor_scalar(compared[:, 1, 0:at], compared[:, 0, 0:at], w_col[:, t:t + 1], 0.0, ALU.is_ge, ALU.add,
                          accum_out=counts[:, 0, t:t + 1]).then_inc(sem, 1)
        done += 1
    dve.tensor_scalar(compared[:, 1, at:TOK], compared[:, 0, at:TOK], w_col[:, t:t + 1], 0.0, ALU.is_gt, ALU.add,
                      accum_out=counts[:, 1, t:t + 1]).then_inc(sem, 1)
    dve.scalar_tensor_tensor(compared[:, 2, 0:P], compared[:, 0, at:at + P], w_col[:, t:t + 1], compared[:, 3, 0:P],
                             ALU.is_equal, ALU.mult, accum_out=counts[:, 2, t:t + 1]).then_inc(sem, 1)
    done += 2
    dve.wait_ge(sem, done)
    return done


def experts(k, E, F, source, weights, gate, total, gated, limit=None):
    C = F // P
    ups = 2 if gated else 1
    with ExitStack() as ctx:
        up = k.sbuf(ctx, "expert_up", [P, 2, ups, F])
        down = k.sbuf(ctx, "expert_down", [P, 2, C, D])
        cols = k.sbuf(ctx, "expert_columns", [P, 2, C + 2])
        scaled = k.sbuf(ctx, "expert_x", [P, TOK])
        hT = k.sbuf(ctx, "hT", [P, C, TOK])
        act_out = k.sbuf(ctx, "act_out", [P, 2, BANK])

        def loads(e, at):
            def of(name):
                a = weights[name][bass.ds(e, 1)]
                return a.rearrange("e a b -> (e a) b")
            if gated:
                ins = [(up[:, at, 0, :], of("wg")), (up[:, at, 1, :], of("wu"))]
                last = "wd"
            else:
                ins = [(up[:, at, 0, :], of("w1")), (cols[:, at, :], of("cols"))]
                last = "w2"
            return ins + [(down[:, at, :, :], of(last).rearrange("(c p) n -> p c n", p=P))]

        def one(e, at, following):
            steps = [(c, n) for c in range(C) for n in range(2)]
            with k.stage("loaded", "scaled", "gates", "acted", "ups", "hidden", "product", "added", "column",
                         "spread", "spread_copied", "counted", "kept") as (
                    block, loaded, x_scaled, gates, acted, upped, hidden, product, added, column, spread,
                    spread_copied, counted, kept):
                x = source if gated else scaled
                if limit is not None:
                    capacity, wsel, compared, w_col, counts = limit
                    assert len(steps) == TILES

                    @block.gpsimd
                    def _(pool):
                        pool.tensor_copy(w_col[:, :], wsel[:, :, bass.ds(e, 1)].rearrange("p t a -> p (t a)")
                                         ).then_inc(column, 1)

                @block.sync
                def _(sync):
                    load(sync, loaded, following)

                @block.tensor
                def _(pe):
                    if not gated:
                        pe.wait_ge(x_scaled, 1)
                    for s, (c, n) in enumerate(steps):
                        after(pe, acted, s - 1)
                        pe.matmul(k.ps[s % 2][:, :], up[:, at, 0, c * P:(c + 1) * P], x[:, n * BANK:(n + 1) * BANK],
                                  start=True, stop=True).then_inc(gates, 1)
                        if gated:
                            after(pe, hidden, s - 1)
                            pe.matmul(k.ps[2 + s % 2][:, :], up[:, at, 1, c * P:(c + 1) * P],
                                      x[:, n * BANK:(n + 1) * BANK], start=True, stop=True).then_inc(upped, 1)
                        if limit is not None and s == 0:
                            pe.wait_ge(column, 1)
                            for t in range(TILES):
                                ins = pe.transpose(k.ps[6 + t // 4][:, t % 4 * P:(t % 4 + 1) * P],
                                                   w_col[:, t:t + 1].to_broadcast([P, P]), k.ident[:, :])
                            ins.then_inc(spread, 1)
                    pe.wait_ge(hidden if gated else acted, len(steps))
                    for t in range(TILES):
                        after(pe, added, t - 1)
                        for c in range(C):
                            ins = pe.matmul(k.ps[4 + t % 2][:, :D], hT[:, c, t * P:(t + 1) * P], down[:, at, c, :],
                                            start=(c == 0), stop=(c == C - 1))
                        ins.then_inc(product, 1)

                @block.scalar
                def _(act):
                    for s, (c, n) in enumerate(steps):
                        act.wait_ge(gates, s + 1)
                        if gated:
                            after(act, hidden, s - 1)
                            act.activation(act_out[:, s % 2, :], k.ps[s % 2][:, :], ACT.Silu).then_inc(acted, 1)
                            if limit is not None and s == 0:
                                act.wait_ge(spread, 1)
                                for half in range(2):
                                    act.activation(compared[:, 0, half * BANK:(half + 1) * BANK], k.ps[6 + half][:, :],
                                                   ACT.Copy).then_inc(spread_copied, 1)
                        else:
                            act.activation(hT[:, c, n * BANK:(n + 1) * BANK], k.ps[s % 2][:, :], ACT.Gelu,
                                           bias=cols[:, at, 2 + c:3 + c]).then_inc(acted, 1)

                @block.vector
                def _(dve):
                    ranked = 0
                    if gated:
                        for s, (c, n) in enumerate(steps):
                            dve.wait_ge(acted, s + 1)
                            dve.wait_ge(upped, s + 1)
                            dve.tensor_tensor(hT[:, c, n * BANK:(n + 1) * BANK], k.ps[2 + s % 2][:, :],
                                              act_out[:, s % 2, :], ALU.mult).then_inc(hidden, 1)
                            if limit is not None:
                                dve.wait_ge(spread_copied, 2)
                                ranked = rank_tile(dve, counted, ranked, s, compared, w_col, counts)
                    else:
                        dve.tensor_scalar(scaled[:, :], source[:, :], cols[:, at, 0:1], cols[:, at, 1:2], ALU.mult,
                                          ALU.add).then_inc(x_scaled, 1)
                    if limit is not None:
                        chain = Chain(dve, kept)
                        rank = counts[:, 0, :]
                        chain.link(dve.tensor_tensor(rank, counts[:, 0, :], counts[:, 1, :], ALU.add))
                        chain.link(dve.tensor_tensor(rank, rank, counts[:, 2, :], ALU.add))
                        chain.link(dve.tensor_scalar(counts[:, 1, :], rank, float(capacity), None, ALU.is_lt))
                        chain.link(dve.tensor_tensor(
                            counts[:, 3, :], counts[:, 1, :], gate[:, :, bass.ds(e, 1)].rearrange("p t a -> p (t a)"),
                            ALU.mult))
                        chain.link(dve.memset(counts[:, 0, 0:1], 0.0))
                    for t in range(TILES):
                        dve.wait_ge(product, t + 1)
                        if limit is not None:
                            g = counts[:, 3, t:t + 1]
                        else:
                            g = gate[:, t, bass.ds(e, 1)] if not isinstance(e, int) else gate[:, t, e:e + 1]
                        dve.scalar_tensor_tensor(total[:, t, :], k.ps[4 + t % 2][:, :D], g, total[:, t, :], ALU.mult,
                                                 ALU.add).then_inc(added, 1)

        with k.stage("loaded") as (block, loaded):
            @block.sync
            def _(sync):
                load(sync, loaded, loads(0, 0))
        with k.loop(E // 2 - 1) as i:
            one(2 * i, 0, loads(2 * i + 1, 1))
            one(2 * i + 1, 1, loads(2 * i + 2, 0))
        one(E - 2, 0, loads(E - 1, 1))
        one(E - 1, 1, [])


def layer2_ffn(k):
    E, F = 8, 512
    dr = k.dram
    with ExitStack() as ctx:
        xn = k.sbuf(ctx, "xn", [P, TILES, D])
        routed = k.sbuf(ctx, "routed", [P, TOK])
        total = k.sbuf(ctx, "total", [P, TILES, D])
        ln = k.sbuf(ctx, "router_ln", [P, 2])
        rw = k.sbuf(ctx, "router_w", [P, E])
        rb = k.sbuf(ctx, "router_b", [P, E])
        b2 = k.sbuf(ctx, "b2", [E, D])
        ow, ob = (k.sbuf(ctx, n, [P, D]) for n in ("out_ln_w", "out_ln_b"))
        rising = k.sbuf(ctx, "rising", [P, E])
        logits, tmp, one, two, gate = (k.sbuf(ctx, n, [P, TILES, E]) for n in (
            "logits", "tmp", "first", "second", "gate"))
        best = k.sbuf(ctx, "best", [P, 4, TILES])
        gateT = k.sbuf(ctx, "gateT", [E, TOK])
        layer_norm(k, k.x, xn, None, loads=[
            (ln[:, 0:1], dr["L2_ffn_router_ln_w"].rearrange("(p a) -> p a", a=1)),
            (ln[:, 1:2], dr["L2_ffn_router_ln_b"].rearrange("(p a) -> p a", a=1)), (rw[:, :], dr["L2_ffn_router_w"]),
            (rb[:, :], dr["L2_ffn_router_b"].partition_broadcast(P)), (b2[:, :], dr["L2_ffn_b2"]),
            (ow[:, :], dr["L2_ffn_out_ln_w"].partition_broadcast(P)),
            (ob[:, :], dr["L2_ffn_out_ln_b"].partition_broadcast(P)), (rising[:, :], dr["rising"])])
        layer_norm(k, xn, xn, k.xT)
        DIFF, FINAL = 17, 23
        with k.stage("routed", "scored", "own", "exped", "turned", "copied", "product") as (
                block, x_routed, scored, own, exped, turned, copied, product):
            @block.vector
            def _(dve):
                dve.tensor_scalar(routed[:, :], k.xT[:, :], ln[:, 0:1], ln[:, 1:2], ALU.mult,
                                  ALU.add).then_inc(x_routed, 1)
                chain = Chain(dve, own)
                dve.wait_ge(scored, 1)
                full = [P, TILES, E]
                chain.link(dve.tensor_tensor(logits[:, :, :], k.ps[0][:, 0:TILES * E].rearrange(
                    "p (t e) -> p t e", e=E), rb[:, :].unsqueeze(1).to_broadcast(full), ALU.add))
                first_best(dve, chain, logits[:, :, :], best[:, 0, :], one[:, :, :], tmp[:, :, :], rising[:, :])
                chain.link(dve.scalar_tensor_tensor(logits[:, :, :], one[:, :, :], -BIG, logits[:, :, :], ALU.mult,
                                                    ALU.add))
                first_best(dve, chain, logits[:, :, :], best[:, 1, :], two[:, :, :], tmp[:, :, :], rising[:, :])
                chain.link(dve.tensor_tensor(best[:, 2, :], best[:, 1, :], best[:, 0, :], ALU.subtract))
                dve.wait_ge(exped, 1)
                chain.link(dve.tensor_scalar(best[:, 0, :], best[:, 3, :], 1.0, None, ALU.add))
                chain.link(dve.reciprocal(best[:, 0, :], best[:, 0, :]))
                chain.link(dve.tensor_tensor(best[:, 1, :], best[:, 3, :], best[:, 0, :], ALU.mult))
                chain.link(dve.tensor_tensor(one[:, :, :], one[:, :, :], best[:, 0, :].unsqueeze(2).to_broadcast(full),
                                             ALU.mult))
                chain.link(dve.tensor_tensor(two[:, :, :], two[:, :, :], best[:, 1, :].unsqueeze(2).to_broadcast(full),
                                             ALU.mult))
                chain.link(dve.tensor_tensor(gate[:, :, :], one[:, :, :], two[:, :, :], ALU.add))
                assert chain.n == FINAL
                for n in range(2):
                    dve.wait_ge(turned, n + 1)
                    dve.tensor_copy(gateT[:, n * BANK:(n + 1) * BANK], k.ps[1 + n][0:E, :]).then_inc(copied, 1)
                for n in range(2):
                    dve.wait_ge(product, n + 1)
                    dve.tensor_copy(total[:, 4 * n:4 * n + 4, :], k.ps[3 + n][:, :].rearrange("p (t d) -> p t d", d=D))

            @block.scalar
            def _(act):
                act.wait_ge(own, DIFF)
                act.activation(best[:, 3, :], best[:, 2, :], ACT.Exp).then_inc(exped, 1)

            @block.tensor
            def _(pe):
                pe.wait_ge(x_routed, 1)
                for t in range(TILES):
                    ins = pe.matmul(k.ps[0][:, t * E:(t + 1) * E], routed[:, t * P:(t + 1) * P], rw[:, :],
                                    start=True, stop=True)
                ins.then_inc(scored, 1)
                pe.wait_ge(own, FINAL)
                for t in range(TILES):
                    ins = pe.transpose(k.ps[1 + t // 4][0:E, t % 4 * P:(t % 4 + 1) * P], gate[:, t, :], k.ident[:, :])
                    if t % 4 == 3:
                        ins.then_inc(turned, 1)
                pe.wait_ge(copied, 2)
                for t in range(TILES):
                    ins = pe.matmul(k.ps[3 + t // 4][:, t % 4 * P:(t % 4 + 1) * P], gateT[:, t * P:(t + 1) * P],
                                    b2[:, :], start=True, stop=True)
                    if t % 4 == 3:
                        ins.then_inc(product, 1)

        experts(k, E, F, k.xT, {"w1": dr["L2_ffn_w1"], "cols": dr["L2_ffn_cols"], "w2": dr["L2_ffn_w2"]}, gate, total,
                False)
        layer_norm(k, total, total, None, gamma=ow[:, :], beta=ob[:, :])
        add_to_x(k, total)


def scan_inputs(k, s):
    with k.stage("product", "tapped", "added", "biased", "silu", "rows", "projected", "row_copied", "dt",
                 "own", "absed", "logs", "split", "neg", "fresh") as (
            block, product, tapped, added, biased, silu, rows, projected, row_copied, dt, own, absed, logs, split,
            neg, fresh):
        def halves(m, n):
            return m[:, n * BANK:(n + 1) * BANK]

        @block.tensor
        def _(pe):
            for c in range(4):
                for n in range(2):
                    pe.matmul(k.ps[2 * c + n][:, :], s["in_proj"][:, c * P:(c + 1) * P], halves(k.xT, n), start=True,
                              stop=True).then_inc(product, 1)
            pe.wait_ge(silu, 2)
            for n in range(2):
                for c in range(2):
                    ins = pe.matmul(k.ps[n][0:1, :], s["x_proj"][:, c, 0:1], halves(s["xc"][:, c, :], n),
                                    start=(c == 0), stop=(c == 1))
                ins.then_inc(rows, 1)
            pe.wait_ge(silu, 6)
            for m in range(2):
                for n in range(2):
                    for c in range(2):
                        ins = pe.matmul(k.ps[4 + 2 * m + n][:, :], s["x_proj"][:, c, 1 + m * P:1 + (m + 1) * P],
                                        halves(s["xc"][:, c, :], n), start=(c == 0), stop=(c == 1))
                    ins.then_inc(projected, 1)
            pe.wait_ge(row_copied, 2)
            for c in range(2):
                for n in range(2):
                    pe.matmul(k.ps[2 * c + n][:, :], s["dt_w"][:, c * P:(c + 1) * P], halves(s["row"], n), start=True,
                              stop=True).then_inc(dt, 1)

        @block.scalar
        def _(act):
            for c in range(2):
                for n in range(2):
                    act.wait_ge(product, 2 * c + n + 1)
                    act.activation(halves(s["xc"][:, c, :], n), k.ps[2 * c + n][:, :], ACT.Copy,
                                   scale=s["conv"][:, c, 3:4]).then_inc(tapped, 1)
            for c in range(2):
                act.wait_ge(added, 6 * (c + 1))
                act.activation(s["xc"][:, c, :], s["xc"][:, c, :], ACT.Silu, bias=s["conv"][:, c, 4:5]).then_inc(silu, 1)
            for c in range(2):
                for n in range(2):
                    act.wait_ge(product, 4 + 2 * c + n + 1)
                    act.activation(halves(s["z"][:, c, :], n), k.ps[4 + 2 * c + n][:, :], ACT.Silu).then_inc(silu, 1)
            for n in range(2):
                act.wait_ge(rows, n + 1)
                act.activation(halves(s["row"], n), k.ps[n][0:1, :], ACT.Copy).then_inc(row_copied, 1)
            for c in range(2):
                for n in range(2):
                    act.wait_ge(dt, 2 * c + n + 1)
                    act.activation(halves(s["e"][:, c, :], n), k.ps[2 * c + n][:, :], ACT.Abs,
                                   bias=s["dt_b"][:, c:c + 1]).then_inc(absed, 1)
            act.wait_ge(absed, 4)
            act.activation(s["e"], s["e"], ACT.Exp, scale=-1.0).then_inc(absed, 1)
            act.wait_ge(absed, 5)
            act.activation(s["log"], s["e"], ACT.Ln, bias=1.0).then_inc(logs, 1)
            act.activation(s["a"], s["a_log"], ACT.Exp).then_inc(neg, 1)
            act.wait_ge(neg, 1)
            act.activation(s["a"], s["a"], ACT.Copy, scale=-1.0).then_inc(neg, 1)

        @block.vector
        def _(dve):
            done = 0
            for c in range(2):
                for n in range(2):
                    dve.wait_ge(tapped, 2 * c + n + 1)
                    y = halves(s["xc"][:, c, :], n).rearrange("p (b t) -> p b t", t=T)
                    x = k.ps[2 * c + n][:, :].rearrange("p (b t) -> p b t", t=T)
                    for back in (1, 2, 3):
                        dve.scalar_tensor_tensor(y[:, :, back:T], x[:, :, 0:T - back], s["conv"][:, c, 3 - back:4 - back],
                                                 y[:, :, back:T], ALU.mult, ALU.add).then_inc(added, 1)
                        done += 1
                        dve.wait_ge(added, done)
            chain = Chain(dve, split)
            for m in range(2):
                for n in range(2):
                    dve.wait_ge(projected, 2 * m + n + 1)
                    chain.link(dve.tensor_copy(halves(s["rest"], n), k.ps[4 + 2 * m + n][:, :]))
                for part in range(3):
                    chain.link(dve.tensor_copy(s["parts"][:, m, part, :], s["rest"]))
                    if part < 2:
                        chain.link(dve.tensor_tensor(s["rest"], s["rest"], s["parts"][:, m, part, :], ALU.subtract))
            chain = Chain(dve, own)
            for c in range(2):
                for n in range(2):
                    dve.wait_ge(absed, 2 * c + n + 1)
                    chain.link(dve.tensor_scalar(halves(s["dt"][:, c, :], n), k.ps[2 * c + n][:, :],
                                                 s["dt_b"][:, c:c + 1], 0.0, ALU.add, ALU.max))
            dve.wait_ge(absed, 5)
            e, series, small, log, sdt = (s[n].rearrange("p c t -> p (c t)") for n in ("e", "series", "small", "log", "dt"))
            log1p_small(dve, fresh, 0, e, series, small)
            dve.wait_ge(logs, 1)
            chain.link(dve.copy_predicated(log, small.bitcast(U32), series))
            chain.link(dve.tensor_tensor(sdt, sdt, log, ALU.add))
            chain.link(dve.tensor_tensor(s["dtx"], s["dt"], s["xc"], ALU.mult))
            chain.link(dve.memset(s["decay"].rearrange("p c (b t) -> p c b t", t=T)[:, :, :, 0], 0.0))


def stack_parts(k, s):
    with k.stage("moved", "made") as (block, moved, made):
        @block.sync
        def _(sync):
            load(sync, moved, [(s["stacked"][32 * part:32 * (part + 1), :, g, :],
                                s["parts"][32 * g:32 * (g + 1), :, part, :])
                               for g in range(4) for part in range(3)])

        @block.vector
        def _(dve):
            sel = s["selector"]
            dve.tensor_tensor(sel, k.identb[0:96, 0:32], k.identb[0:96, 32:64], ALU.add).then_inc(made, 1)
            dve.wait_ge(made, 1)
            dve.tensor_tensor(sel, sel, k.identb[0:96, 64:96], ALU.add).then_inc(made, 1)


def copy_rates(k, s, group):
    with k.stage("copied") as (block, copied):
        @block.vector
        def _(dve):
            dve.tensor_copy(s["a_now"], s["a"][:, bass.ds(group * 32, 32)]).then_inc(copied, 1)


def scan_states(k, s, group, per):
    UNITS = 2 * per
    HC = 4
    with k.stage("spread_b", "spread_c", "b_copied", "decayed", "driven", "scanned", "weighted",
                 "summed") as (
            block, spread_b, spread_c, b_copied, decayed, driven, scanned, weighted, summed):
        @block.tensor
        def _(pe):
            def spread(i, m, sem):
                column = s["selector"][:, i:i + 1].to_broadcast([96, P])
                for n in range(2):
                    ins = pe.matmul(k.ps[2 * m + n][:, :], column,
                                    s["stacked"][:, m, bass.ds(group, 1), n * BANK:(n + 1) * BANK].rearrange(
                                        "p a t -> p (a t)"), start=True, stop=True)
                ins.then_inc(sem, 1)

            def accumulate(u):
                pe.wait_ge(weighted, u + 1)
                for n in range(2):
                    ins = pe.matmul(k.ps[4 + u % 2 * 2 + n][:, :], k.ident[:, :], s["hc"][:, u % HC, n * BANK:(n + 1) * BANK],
                                    start=False, stop=False, skip_group_check=True)
                ins.then_inc(summed, 1)

            spread(0, 0, spread_b)
            for i in range(per + 1):
                if i + 1 < per:
                    pe.wait_ge(b_copied, i + 1)
                    spread(i + 1, 0, spread_b)
                if i >= 1:
                    accumulate(2 * i - 2)
                if i < per:
                    after(pe, weighted, 2 * i)
                    spread(i, 1, spread_c)
                if i >= 1:
                    accumulate(2 * i - 1)

        @block.scalar
        def _(act):
            for i in range(per):
                act.wait_ge(spread_b, i + 1)
                after(act, driven, 2 * (i - 1))
                for n in range(2):
                    ins = act.activation(s["b_rows"][:, i % 2, n * BANK:(n + 1) * BANK], k.ps[n][:, :], ACT.Copy)
                ins.then_inc(b_copied, 1)
                for c in range(2):
                    u = 2 * i + c
                    after(act, scanned, u - 1)
                    act.activation(s["decay"][:, u % 2, :].rearrange("p (b t) -> p b t", t=T)[:, :, 1:T],
                                   s["dt"][:, c, :].rearrange("p (b t) -> p b t", t=T)[:, :, 1:T], ACT.Exp,
                                   scale=s["a_now"][:, i:i + 1]).then_inc(decayed, 1)

        @block.gpsimd
        def _(pool):
            for u in range(UNITS):
                i, c = u // 2, u % 2
                pool.wait_ge(b_copied, i + 1)
                after(pool, scanned, u - 1)
                pool.tensor_tensor(s["drive"][:, u % 2, :], s["dtx"][:, c, :], s["b_rows"][:, i % 2, :],
                                   ALU.mult).then_inc(driven, 1)

        @block.vector
        def _(dve):
            for u in range(UNITS + 1):
                if u < UNITS:
                    dve.wait_ge(decayed, u + 1)
                    dve.wait_ge(driven, u + 1)
                    after(dve, weighted, u - 2)
                    dve.tensor_tensor_scan(s["h"][:, u % 3, :], s["decay"][:, u % 2, :], s["drive"][:, u % 2, :], 0.0,
                                           ALU.mult, ALU.add).then_inc(scanned, 1)
                if u >= 1:
                    w = u - 1
                    dve.wait_ge(scanned, w + 1)
                    dve.wait_ge(spread_c, w // 2 + 1)
                    after(dve, summed, w - HC + 1)
                    for n in range(2):
                        ins = dve.tensor_tensor(s["hc"][:, w % HC, n * BANK:(n + 1) * BANK],
                                                s["h"][:, w % 3, n * BANK:(n + 1) * BANK], k.ps[2 + n][:, :], ALU.mult)
                    ins.then_inc(weighted, 1)


def scan_outputs(k, s):
    with k.stage("squared", "sums", "gated", "own", "rooted", "product", "added") as (
            block, squared, sums, gated, own, rooted, product, added):
        y = [k.ps[4 + i] for i in range(4)]

        @block.scalar
        def _(act):
            for i in range(4):
                act.activation(s["sq"][:, i // 2, i % 2 * BANK:(i % 2 + 1) * BANK], y[i][:, :],
                               ACT.Square).then_inc(squared, 1)
            act.wait_ge(own, 1)
            act.activation(s["r"], s["r"], ACT.Sqrt).then_inc(rooted, 1)

        @block.tensor
        def _(pe):
            pe.wait_ge(squared, 4)
            for t in range(TILES):
                for c in range(2):
                    ins = pe.matmul(k.ps[0][:, t:t + 1], s["sq"][:, c, t * P:(t + 1) * P], s["ones"], start=(c == 0),
                                    stop=(c == 1))
            ins.then_inc(sums, 1)
            pe.wait_ge(gated, 4)
            for t in range(TILES):
                after(pe, added, t - 1)
                for c in range(2):
                    ins = pe.matmul(k.ps[1 + t % 2][:, :D], s["z"][:, c, t * P:(t + 1) * P], s["out_proj"][:, c, :],
                                    start=(c == 0), stop=(c == 1))
                ins.then_inc(product, 1)

        @block.vector
        def _(dve):
            for i in range(4):
                dve.wait_ge(squared, i + 1)
                z = s["z"][:, i // 2, i % 2 * BANK:(i % 2 + 1) * BANK]
                dve.scalar_tensor_tensor(z, y[i][:, :], s["conv"][:, i // 2, 5:6], z, ALU.mult, ALU.mult).then_inc(gated, 1)
            dve.wait_ge(sums, 1)
            dve.tensor_scalar(s["r"], k.ps[0][:, 0:TILES], 1.0 / 256, float(np.finfo(np.float32).eps), ALU.mult,
                              ALU.add).then_inc(own, 1)
            dve.wait_ge(rooted, 1)
            dve.reciprocal(s["r"], s["r"]).then_inc(own, 1)
            dve.wait_ge(own, 2)
            for t in range(TILES):
                dve.wait_ge(product, t + 1)
                dve.scalar_tensor_tensor(k.x[:, t, :], k.ps[1 + t % 2][:, :D], s["r"][:, t:t + 1], k.x[:, t, :],
                                         ALU.mult, ALU.add).then_inc(added, 1)


def layer3_scan(k):
    PER = 32
    dr = k.dram
    with ExitStack() as ctx:
        s = {}

        def room(name, shape, dt=F32):
            t = k.sbuf(ctx, name, shape, dt)
            s[name] = t[tuple(slice(None) for _ in shape)]
            return s[name]

        room("in_proj", [P, 4 * P])
        room("x_proj", [P, 2, 2 * P + 1])
        room("dt_w", [1, 2 * P])
        room("dt_b", [P, 2])
        room("conv", [P, 2, 6])
        room("a_log", [P, P])
        room("a", [P, P])
        room("a_now", [P, PER])
        room("out_proj", [P, 2, D])
        room("row", [1, TOK])
        room("rest", [P, TOK])
        room("parts", [P, 2, 3, TOK], BF16)
        for name in ("xc", "z", "e", "log", "series", "small", "dt", "dtx"):
            room(name, [P, 2, TOK])
        room("stacked", [96, 2, 4, TOK], BF16)
        room("selector", [96, 32], BF16)
        for name in ("b_rows", "decay", "drive"):
            room(name, [P, 2, TOK])
        room("h", [P, 3, TOK])
        room("hc", [P, 4, TOK])
        s["sq"] = s["h"]
        room("ones", [P, 1])
        room("r", [P, TILES])
        xn = room("xn", [P, TILES, D])
        layer_norm(k, k.x, xn, k.xT, loads=[
            (s["in_proj"], dr["L3_attn_in_proj_w"]),
            (s["x_proj"], dr["L3_attn_x_proj_w"].rearrange("(c p) n -> p c n", p=P)),
            (s["dt_w"], dr["L3_attn_dt_proj_w"]), (s["dt_b"], dr["L3_attn_dt_proj_b"]),
            (s["conv"], dr["L3_attn_columns"].rearrange("(c p) n -> p c n", p=P)),
            (s["a_log"], dr["L3_attn_A_log"].partition_broadcast(P)),
            (s["out_proj"], dr["L3_attn_out_proj_w"].rearrange("(c p) n -> p c n", p=P))])
        scan_inputs(k, s)
        stack_parts(k, s)
        with k.stage("zeroed") as (block, zeroed):
            @block.vector
            def _(dve):
                dve.memset(s["h"][:, 0, 0:BANK], 0.0).then_inc(zeroed, 1)
                dve.memset(s["ones"], 1.0).then_inc(zeroed, 1)

            @block.tensor
            def _(pe):
                pe.wait_ge(zeroed, 1)
                for i in range(4):
                    pe.matmul(k.ps[4 + i][:, :], k.ident[:, :], s["h"][:, 0, 0:BANK], start=True, stop=False,
                              skip_group_check=True)
        with k.loop(P // PER) as group:
            copy_rates(k, s, group)
            scan_states(k, s, group, PER)
        with k.stage("closed") as (block, closed):
            @block.vector
            def _(dve):
                dve.memset(s["h"][:, 0, 0:BANK], 0.0).then_inc(closed, 1)

            @block.tensor
            def _(pe):
                pe.wait_ge(closed, 1)
                for i in range(4):
                    pe.matmul(k.ps[4 + i][:, :], k.ident[:, :], s["h"][:, 0, 0:BANK], start=False, stop=True,
                              skip_group_check=True)
        scan_outputs(k, s)


def combine(k, dst, a, b, floor=False):
    with k.stage("done") as (block, done):
        @block.vector
        def _(dve):
            if floor:
                dve.scalar_tensor_tensor(dst[:, :, :], a[:, :, :], 0.0, b[:, :, :], ALU.max, ALU.add).then_inc(done, 1)
            else:
                dve.tensor_tensor(dst[:, :, :], a[:, :, :], b[:, :, :], ALU.add).then_inc(done, 1)


def layer3_cross(k):
    dr = k.dram
    EPS = 1e-3
    with ExitStack() as ctx:
        w = {n: k.sbuf(ctx, n, [P, D]) for n in ("Wq", "Wk", "Wv", "Wcq", "Wck", "Wcv", "W1")}
        rows = {n: k.sbuf(ctx, n, [P, D]) for n in ("gamma", "beta", "b1")}
        xn, q, kk, v, o = (k.sbuf(ctx, n, [P, TILES, D]) for n in ("xn", "q", "k", "v", "o"))
        gamma, beta = rows["gamma"][:, :], rows["beta"][:, :]
        layer_norm(k, k.x, xn, k.xT, loads=[(w[n][:, :], dr["L3_xattn_" + n]) for n in w]
                   + [(rows[n][:, :], dr["L3_xattn_" + n].partition_broadcast(P)) for n in rows])
        project(k, [(k.xT, w["Wq"], q, None, False), (k.xT, w["Wk"], kk, None, False),
                    (k.xT, w["Wv"], v, None, False)])
        attention(k, q, kk, v, o, 1, D, D ** -0.5, mask=k.causal, causal=True)
        combine(k, xn, o, xn)
        layer_norm(k, xn, xn, k.xT, eps=EPS, gamma=gamma, beta=beta)
        project(k, [(k.xT, w["Wcq"], q, None, False), (k.ctxT, w["Wck"], kk, None, False),
                    (k.ctxT, w["Wcv"], v, None, False)])
        attention(k, q, kk, v, o, 1, D, D ** -0.5)
        combine(k, xn, o, xn)
        layer_norm(k, xn, xn, k.xT, eps=EPS, gamma=gamma, beta=beta)
        project(k, [(k.xT, w["W1"], q, rows["b1"], False)])
        combine(k, q, q, xn, floor=True)
        layer_norm(k, q, q, None, eps=EPS, gamma=gamma, beta=beta)
        combine(k, k.x, q, k.x, floor=True)


def layer3_ffn(k):
    E, F = 8, 512
    CAPACITY = int(1.25 * TOK / E)
    dr = k.dram
    with ExitStack() as ctx:
        xn = k.sbuf(ctx, "xn", [P, TILES, D])
        total = k.sbuf(ctx, "total", [P, TILES, D])
        rw = k.sbuf(ctx, "router_w", [P, E])
        rising = k.sbuf(ctx, "rising", [P, E])
        probs, tmp, one, two, gate, wsel = (k.sbuf(ctx, n, [P, TILES, E]) for n in (
            "probs", "tmp", "first", "second", "gate", "weights"))
        best = k.sbuf(ctx, "best", [P, 5, TILES])
        w_col = k.sbuf(ctx, "w_col", [P, TILES])
        counts = k.sbuf(ctx, "counts", [P, 4, TILES])
        scr = k.sbuf(ctx, "compared", [P, 4, TOK])
        layer_norm(k, k.x, xn, k.xT, loads=[(rw[:, :], dr["L3_ffn_router_w"]), (rising[:, :], dr["rising"]),
                                            (scr[:, 3, 0:P], dr["earlier"])])
        with k.stage("scored", "own", "exped") as (block, scored, own, exped):
            full = [P, TILES, E]

            def wide(m):
                return m.unsqueeze(2).to_broadcast(full)

            @block.tensor
            def _(pe):
                for t in range(TILES):
                    ins = pe.matmul(k.ps[0][:, t * E:(t + 1) * E], k.xT[:, t * P:(t + 1) * P], rw[:, :],
                                    start=True, stop=True)
                ins.then_inc(scored, 1)

            @block.scalar
            def _(act):
                act.wait_ge(own, 2)
                act.activation(probs[:, :, :], probs[:, :, :], ACT.Exp).then_inc(exped, 1)

            @block.vector
            def _(dve):
                chain = Chain(dve, own)
                dve.wait_ge(scored, 1)
                logits = k.ps[0][:, 0:TILES * E].rearrange("p (t e) -> p t e", e=E)
                chain.link(dve.tensor_reduce(best[:, 0, :], logits, AX_X, ALU.max))
                chain.link(dve.tensor_tensor(probs[:, :, :], logits, wide(best[:, 0, :]), ALU.subtract))
                dve.wait_ge(exped, 1)
                chain.link(dve.tensor_reduce(best[:, 0, :], probs[:, :, :], AX_X, ALU.add))
                chain.link(dve.reciprocal(best[:, 0, :], best[:, 0, :]))
                chain.link(dve.tensor_tensor(probs[:, :, :], probs[:, :, :], wide(best[:, 0, :]), ALU.mult))
                first_best(dve, chain, probs[:, :, :], best[:, 1, :], one[:, :, :], tmp[:, :, :], rising[:, :])
                chain.link(dve.scalar_tensor_tensor(probs[:, :, :], one[:, :, :], -4.0, probs[:, :, :], ALU.mult,
                                                    ALU.add))
                first_best(dve, chain, probs[:, :, :], best[:, 2, :], two[:, :, :], tmp[:, :, :], rising[:, :])
                chain.link(dve.tensor_tensor(best[:, 3, :], best[:, 1, :], best[:, 2, :], ALU.add))
                chain.link(dve.tensor_scalar(best[:, 3, :], best[:, 3, :], 1e-6, None, ALU.add))
                chain.link(dve.reciprocal(best[:, 3, :], best[:, 3, :]))
                for m, hit in ((1, one), (2, two)):
                    chain.link(dve.tensor_tensor(best[:, m, :], best[:, m, :], best[:, 3, :], ALU.mult))
                    chain.link(dve.tensor_tensor(tmp[:, :, :], hit[:, :, :], wide(best[:, m, :]), ALU.mult))
                    if m == 1:
                        chain.link(dve.tensor_copy(gate[:, :, :], tmp[:, :, :]))
                    else:
                        chain.link(dve.tensor_tensor(gate[:, :, :], gate[:, :, :], tmp[:, :, :], ALU.add))
                chain.link(dve.tensor_tensor(tmp[:, :, :], one[:, :, :], two[:, :, :], ALU.add))
                chain.link(dve.tensor_scalar(wsel[:, :, :], tmp[:, :, :], 1.0, None, ALU.subtract))
                chain.link(dve.tensor_tensor(wsel[:, :, :], wsel[:, :, :], gate[:, :, :], ALU.add))
                chain.link(dve.memset(counts[:, :, :], 0.0))
                chain.link(dve.memset(total[:, :, :], 0.0))
        experts(k, E, F, k.xT, {n: dr["L3_ffn_" + n] for n in ("wg", "wu", "wd")}, gate, total, True,
                (CAPACITY, wsel, scr, w_col, counts))
        add_to_x(k, total)


LAYERS = (layer0_attention, layer0_cross, layer0_local, layer1_attention, layer1_cross, layer1_ffn, layer2_delta,
          layer2_cross, layer2_ffn, layer3_scan, layer3_cross, layer3_ffn)


def rotary_halves(n, d, scaled=False):
    half = np.arange(0, d, 2, dtype=np.float32)
    if not scaled:
        theta = np.arange(n, dtype=np.float32)[:, None] / np.power(np.float32(10000.0), half / d)
        cos, sin = np.cos(theta), np.sin(theta)
        return np.stack([np.concatenate([cos, cos], 1), np.concatenate([-sin, sin], 1)])
    inv = (1.0 / np.float32(10000.0) ** (half / np.float32(d))).astype(np.float32)
    t = np.arange(n, dtype=np.float32)
    theta = t[:, None] * inv[None]
    base = (half + 0.4 * d) / (1.4 * d)
    s = base[None] ** ((t - n // 2) / 16)[:, None]
    cos, sin = np.cos(theta), np.sin(theta)
    q = [np.concatenate([cos * s, cos * s], 1), np.concatenate([-sin * s, sin * s], 1)]
    kk = [np.concatenate([cos / s, cos / s], 1), np.concatenate([-sin / s, sin / s], 1)]
    return np.stack(q + kk)


def rotary_pairs(n, d):
    inv = 1.0 / 10000.0 ** (np.arange(0, d, 2, dtype=np.float32) / d)
    ang = np.outer(np.arange(n - 1, dtype=np.float32), inv)
    cos = np.concatenate([np.ones((1, d // 2)), np.cos(ang)])
    sin = np.concatenate([np.zeros((1, d // 2)), np.sin(ang)])
    return np.stack([np.stack([cos, cos], -1).reshape(n, d), np.stack([-sin, sin], -1).reshape(n, d)])


def on_positions(table):
    m, n, d = table.shape
    return np.ascontiguousarray(table.reshape(m, HALVES, P, d).transpose(0, 2, 1, 3).astype(np.float32))


def block_pairs():
    i, j = np.arange(P)[:, None, None], np.arange(P)[None, None, :]
    size = 2 ** np.arange(7)[None, :, None]
    return (i // (2 * size) == j // (2 * size)) & (i // size % 2 == 1) & (j // size % 2 == 0)


def tables():
    pairs = block_pairs()
    return {
        "rising": np.tile(np.arange(8, 0, -1, dtype=np.float32), (P, 1)),
        "earlier": np.tril(np.ones((P, P), np.float32), -1),
        "right_left": pairs.astype(np.float32),
        "left_right": np.ascontiguousarray(pairs.transpose(2, 1, 0)).astype(np.float32),
        "rope8": on_positions(rotary_halves(T, 8)),
        "rope64": on_positions(rotary_halves(T, 64, scaled=True)),
        "ropeP": on_positions(rotary_pairs(T, 64)),
    }


def build(nc, dram, out):
    with ExitStack() as ctx:
        k = Core(nc, ctx, dram)
        constants(k)
        for layer in LAYERS:
            layer(k)
        with k.stage("stored") as (block, stored):
            @block.sync
            def _(sync):
                sync.dma_start(out.rearrange("(t p) d -> p t d", p=P), k.x[:, :, :]).then_inc(stored, 16)
                sync.wait_ge(stored, 16)


TURNED = ("L1_attn_wq", "L1_attn_wk", "L1_attn_wv", "L1_attn_wo", "L1_ffn_W_con", "L2_attn_Wq",
          "L2_attn_Wk", "L2_attn_Wv", "L2_attn_Wfa", "L2_attn_Wfb", "L2_attn_Wb", "L2_attn_Wga", "L2_attn_Wgb",
          "L2_attn_Wo", "L2_xattn_Wq", "L2_xattn_Wk", "L2_xattn_Wv", "L3_attn_in_proj_w", "L3_attn_x_proj_w",
          "L3_attn_dt_proj_w", "L3_attn_out_proj_w", "L3_ffn_router_w")


def kernel(**inputs):
    import numpy as _np
    import concourse.bacc as _bacc
    from concourse import mybir as _mybir
    from concourse.bass_utils import run_bass_kernel_spmd as _run

    nc = _bacc.Bacc("TRN2", target_bir_lowering=False, num_devices=1)
    arrays = {name: _np.asarray(a) for name, a in inputs.items()}
    arrays["x"] = arrays["x"].reshape(TOK, D)
    arrays["ctxT"] = arrays.pop("ctx_1024").reshape(TOK, D).T
    arrays["mask_BxS2_bf1"] = arrays["mask_BxS2_bf1"].reshape(1, TOK).view(_np.uint8)
    for name in TURNED:
        arrays[name] = arrays[name].T
    for name in ("L1_ffn_up_weights", "L1_ffn_down_weights"):
        arrays[name] = arrays[name].reshape(-1)
    arrays["L1_ffn_up_bias"] = arrays["L1_ffn_up_bias"].reshape(-1, P).T
    for name in ("wq", "wk", "wv"):
        arrays[f"L2_attn_{name}_conv"] = arrays[f"L2_attn_{name}_conv"].reshape(-1, 4)
    arrays["L2_attn_dt_bias"] = arrays["L2_attn_dt_bias"].reshape(-1, 1)
    def by_feature(a):
        return a.reshape(a.shape[0], -1, P).transpose(0, 2, 1)

    arrays["L2_ffn_cols"] = _np.concatenate(
        [by_feature(arrays.pop("L2_ffn_" + n)) for n in ("exp_ln_w", "exp_ln_b", "b1")], axis=2)
    arrays["L3_attn_columns"] = _np.concatenate(
        [arrays.pop("L3_attn_" + n).reshape(2 * P, -1) for n in ("conv_w", "conv_b", "norm_w")], axis=1)
    arrays["L3_attn_dt_proj_b"] = arrays["L3_attn_dt_proj_b"].reshape(2, P).T
    for name in ("Wq", "Wk", "Wv", "Wfb", "Wgb"):
        arrays["L2_attn_" + name] = _np.concatenate([arrays["L2_attn_" + name], arrays["L2_attn_" + name][:, :P]], axis=1)
    for name in ("wq_conv", "wk_conv", "wv_conv", "dt_bias"):
        arrays["L2_attn_" + name] = _np.concatenate([arrays["L2_attn_" + name], arrays["L2_attn_" + name][:P]])
    arrays["L0_ffn_Wqkv"] = _np.concatenate([arrays["L0_ffn_Wqkv"], arrays["L0_ffn_Wqkv"][:1]])
    arrays["L3_attn_A_log"] = arrays["L3_attn_A_log"].reshape(-1)
    arrays.update(tables())
    arrays = {name: _np.ascontiguousarray(a) for name, a in arrays.items()}
    dram = {name: nc.dram_tensor(f"in_{name}_dram", a.shape, _mybir.dt.from_np(a.dtype), kind="ExternalInput").ap()
            for name, a in arrays.items()}
    out = nc.dram_tensor("out_0_dram", (TOK, D), F32, kind="ExternalOutput").ap()
    build(nc, dram, out)
    r = _run(nc, [{f"in_{name}_dram": a for name, a in arrays.items()}], core_ids=[0])
    return r.results[0]["out_0_dram"].reshape(B, T, D)
```
